# Optimizing a Trainium2 kernel written in Bass

```python
import numpy as np
import jax
import jax.numpy as jnp

def _softmax(x, axis=-1):
    return jax.nn.softmax(x, axis=axis)

def _gelu(x):
    return jax.nn.gelu(x, approximate=True)

def _silu(x):
    return jax.nn.silu(x)

def _sigmoid(x):
    return jax.nn.sigmoid(x)

def _layernorm(x, axis=-1, eps=1e-05):
    m = jnp.mean(x, axis=axis, keepdims=True)
    v = jnp.var(x, axis=axis, keepdims=True)
    return (x - m) / jnp.sqrt(v + eps)

def _scatter_add(tgt, idx, src, axis=0):
    return tgt.at[idx].add(src)

def _segment_sum(src, seg, n):
    return jax.ops.segment_sum(src, seg, n)
kernel_name = 'mk_gnn_preln_d4_gnn_r32_c4aa19'

def setup_inputs(seed: int=0):
    np.random.seed(seed)
    _w = jnp.asarray

    def _rec_inputs():
        import jax
        import jax.numpy as jnp
        _gk = jax.random.key(seed)
        x = -8.776e-05 + 1 * jax.random.normal(jax.random.fold_in(_gk, 1), (3125, 128), jnp.float32)
        _s = jax.random.randint(jax.random.fold_in(_gk, 2), (25000,), 0, 3125, jnp.int32)
        _d = jax.random.randint(jax.random.fold_in(_gk, 3), (25000,), 0, 3125, jnp.int32)
        _loop = jnp.arange(3125, dtype=jnp.int32)
        src = jnp.concatenate([_s, _d, _loop])
        dst = jnp.concatenate([_d, _s, _loop])
        _o = jnp.argsort(dst, stable=True)
        src = src[_o]
        dst = dst[_o]
        edge_type_16 = jax.random.randint(jax.random.fold_in(_gk, 13), (53125,), 0, 16, jnp.int32)
        edge_type_4 = jax.random.randint(jax.random.fold_in(_gk, 14), (53125,), 0, 4, jnp.int32)
        edge_weight = jax.random.uniform(jax.random.fold_in(_gk, 15), (53125,), jnp.float32, 0.0, 0.999998)
        edge_weight1 = jax.random.uniform(jax.random.fold_in(_gk, 16), (53125, 1), jnp.float32, 0.0, 0.999998)
        return (x, src, dst, edge_type_16, edge_type_4, edge_weight, edge_weight1)
    x, src, dst, edge_type_16, edge_type_4, edge_weight, edge_weight1 = _rec_inputs()

    def _L0_gnn_setup():
        import jax, jax.numpy as jnp
        import numpy as np
        LN_EPS = 1e-05
        key = jax.random.key(seed)
        k1, k2, k3, k4 = jax.random.split(key, 4)
        N, D, E = (1250, 128, 20000)
        x = jax.random.normal(k1, (N, D), dtype=jnp.float32)
        edge_index = jax.random.randint(k2, (2, E), 0, N, dtype=jnp.int64)
        W_agg = jax.random.normal(k3, (D, 2 * D), dtype=jnp.float32) / np.sqrt(2 * D)
        b_agg = jax.random.normal(k4, (D,), dtype=jnp.float32) * 0.02
        gamma = jnp.ones((D,), dtype=jnp.float32)
        beta = jnp.zeros((D,), dtype=jnp.float32)
        return {'x': x, 'edge_index': edge_index, 'W_agg': W_agg, 'b_agg': b_agg, 'gamma': gamma, 'beta': beta}
    _L0_gnn_all = _L0_gnn_setup()
    _L0_gnn_in = {k: v for k, v in _L0_gnn_all.items() if k in ('W_agg', 'b_agg', 'gamma', 'beta')}
    del _L0_gnn_all

    def _L1_gnn_setup():
        import jax, jax.numpy as jnp
        import numpy as np
        N, E, C = (50000, 18750, 128)

        def _spline_conv(x, src, dst, u, W, root, b):
            n = x.shape[0]
            h0 = x @ W[0]
            h1 = x @ W[1]
            msg = (1.0 - u) * h0[src] + u * h1[src]
            agg = jax.ops.segment_sum(msg, dst, num_segments=n)
            deg = jax.ops.segment_sum(jnp.ones((src.shape[0],), msg.dtype), dst, num_segments=n)
            agg = agg / jnp.maximum(deg, 1.0)[:, None]
            return agg + x @ root + b
        key = jax.random.key(seed)
        ks = jax.random.split(key, 9)
        s = 1.0 / np.sqrt(C)
        return {'x': jax.random.normal(ks[0], (N, C), jnp.float32), 'edge_index': jax.random.randint(ks[1], (2, E), 0, N, jnp.int32), 'edge_attr': jax.random.uniform(ks[2], (E, 1), jnp.float32), 'W1': jax.random.normal(ks[3], (2, C, C), jnp.float32) * s, 'root1': jax.random.normal(ks[4], (C, C), jnp.float32) * s, 'b1': jax.random.normal(ks[5], (C,), jnp.float32) * 0.01, 'W2': jax.random.normal(ks[6], (2, C, C), jnp.float32) * s, 'root2': jax.random.normal(ks[7], (C, C), jnp.float32) * s, 'b2': jax.random.normal(ks[8], (C,), jnp.float32) * 0.01}
    _L1_gnn_all = _L1_gnn_setup()
    _L1_gnn_in = {k: v for k, v in _L1_gnn_all.items() if k in ('W1', 'root1', 'b1', 'W2', 'root2', 'b2')}
    del _L1_gnn_all

    def _L2_gnn_setup():
        import jax, jax.numpy as jnp
        import numpy as np
        N, E, D, R, H = (50000, 6250, 128, 4, 64)
        key = jax.random.key(seed)
        ks = jax.random.split(key, 12)
        s = 0.02
        return {'node_feature': jax.random.normal(ks[0], (N, D), dtype=jnp.float32), 'edge_src': jax.random.randint(ks[1], (E,), 0, N, dtype=jnp.int32), 'edge_dst': jax.random.randint(ks[2], (E,), 0, N, dtype=jnp.int32), 'edge_type': jax.random.randint(ks[3], (E,), 0, R, dtype=jnp.int32), 'Wr1': s * jax.random.normal(ks[4], (R, D, H), dtype=jnp.float32), 'br1': jnp.zeros((R, H), dtype=jnp.float32), 'Wr2': s * jax.random.normal(ks[5], (R, H, H), dtype=jnp.float32), 'br2': jnp.zeros((R, H), dtype=jnp.float32), 'Wr3': s * jax.random.normal(ks[6], (R, H, D), dtype=jnp.float32), 'br3': jnp.zeros((R, D), dtype=jnp.float32), 'Wn1': s * jax.random.normal(ks[7], ((R + 1) * D, H), dtype=jnp.float32), 'bn1': jnp.zeros((H,), dtype=jnp.float32), 'Wn2': s * jax.random.normal(ks[8], (H, H), dtype=jnp.float32), 'bn2': jnp.zeros((H,), dtype=jnp.float32), 'Wn3': s * jax.random.normal(ks[9], (H, D), dtype=jnp.float32), 'bn3': jnp.zeros((D,), dtype=jnp.float32)}
    _L2_gnn_all = _L2_gnn_setup()
    _L2_gnn_in = {k: v for k, v in _L2_gnn_all.items() if k in ('Wr1', 'br1', 'Wr2', 'br2', 'Wr3', 'br3', 'Wn1', 'bn1', 'Wn2', 'bn2', 'Wn3', 'bn3')}
    del _L2_gnn_all

    def _L3_gnn_setup():
        import jax, jax.numpy as jnp
        import numpy as np
        N, E, D, R, H, L = (30000, 15000, 128, 16, 4, 3)
        DH = D // H
        key = jax.random.key(seed)
        ks = jax.random.split(key, 16)
        s = 1.0 / np.sqrt(D)
        return {'feat': jax.random.normal(ks[0], (N, D), jnp.float32), 'src': jax.random.randint(ks[1], (E,), 0, N, jnp.int32), 'dst': jax.random.randint(ks[2], (E,), 0, N, jnp.int32), 'etype': jax.random.randint(ks[3], (E,), 0, R, jnp.int32), 'temporal_weight': jax.random.uniform(ks[4], (E,), jnp.float32), 'W_rel': jax.random.normal(ks[5], (L, R, D, D), jnp.float32) * s, 'b_rel': jnp.zeros((L, D), jnp.float32), 'W_loop': jax.random.normal(ks[6], (L, D, D), jnp.float32) * s, 'W_gat': jax.random.normal(ks[7], (L, D, D), jnp.float32) * s, 'attn_l': jax.random.normal(ks[8], (L, H, DH), jnp.float32) * s, 'attn_r': jax.random.normal(ks[9], (L, H, DH), jnp.float32) * s, 'b_gat': jnp.zeros((L, D), jnp.float32), 'W_fuse': jax.random.normal(ks[10], (2 * D, D), jnp.float32) * (1.0 / np.sqrt(2 * D)), 'b_fuse': jnp.zeros((D,), jnp.float32), 'W_gate': jax.random.normal(ks[11], (D + 1, D), jnp.float32) * s, 'b_gate': jnp.zeros((D,), jnp.float32)}
    _L3_gnn_all = _L3_gnn_setup()
    _L3_gnn_in = {k: v for k, v in _L3_gnn_all.items() if k in ('W_rel', 'b_rel', 'W_loop', 'W_gat', 'attn_l', 'attn_r', 'b_gat', 'W_fuse', 'b_fuse', 'W_gate', 'b_gate')}
    del _L3_gnn_all
    return {'x': x, 'src': src, 'dst': dst, 'edge_type_16': edge_type_16, 'edge_type_4': edge_type_4, 'edge_weight': edge_weight, 'edge_weight1': edge_weight1, 'L0_gnn_W_agg': _L0_gnn_in['W_agg'], 'L0_gnn_b_agg': _L0_gnn_in['b_agg'], 'L0_gnn_gamma': _L0_gnn_in['gamma'], 'L0_gnn_beta': _L0_gnn_in['beta'], 'L1_gnn_W1': _L1_gnn_in['W1'], 'L1_gnn_root1': _L1_gnn_in['root1'], 'L1_gnn_b1': _L1_gnn_in['b1'], 'L1_gnn_W2': _L1_gnn_in['W2'], 'L1_gnn_root2': _L1_gnn_in['root2'], 'L1_gnn_b2': _L1_gnn_in['b2'], 'L2_gnn_Wr1': _L2_gnn_in['Wr1'], 'L2_gnn_br1': _L2_gnn_in['br1'], 'L2_gnn_Wr2': _L2_gnn_in['Wr2'], 'L2_gnn_br2': _L2_gnn_in['br2'], 'L2_gnn_Wr3': _L2_gnn_in['Wr3'], 'L2_gnn_br3': _L2_gnn_in['br3'], 'L2_gnn_Wn1': _L2_gnn_in['Wn1'], 'L2_gnn_bn1': _L2_gnn_in['bn1'], 'L2_gnn_Wn2': _L2_gnn_in['Wn2'], 'L2_gnn_bn2': _L2_gnn_in['bn2'], 'L2_gnn_Wn3': _L2_gnn_in['Wn3'], 'L2_gnn_bn3': _L2_gnn_in['bn3'], 'L3_gnn_W_rel': _L3_gnn_in['W_rel'], 'L3_gnn_b_rel': _L3_gnn_in['b_rel'], 'L3_gnn_W_loop': _L3_gnn_in['W_loop'], 'L3_gnn_W_gat': _L3_gnn_in['W_gat'], 'L3_gnn_attn_l': _L3_gnn_in['attn_l'], 'L3_gnn_attn_r': _L3_gnn_in['attn_r'], 'L3_gnn_b_gat': _L3_gnn_in['b_gat'], 'L3_gnn_W_fuse': _L3_gnn_in['W_fuse'], 'L3_gnn_b_fuse': _L3_gnn_in['b_fuse'], 'L3_gnn_W_gate': _L3_gnn_in['W_gate'], 'L3_gnn_b_gate': _L3_gnn_in['b_gate']}

def reference(x, src, dst, edge_type_16, edge_type_4, edge_weight, edge_weight1, L0_gnn_W_agg, L0_gnn_b_agg, L0_gnn_gamma, L0_gnn_beta, L1_gnn_W1, L1_gnn_root1, L1_gnn_b1, L1_gnn_W2, L1_gnn_root2, L1_gnn_b2, L2_gnn_Wr1, L2_gnn_br1, L2_gnn_Wr2, L2_gnn_br2, L2_gnn_Wr3, L2_gnn_br3, L2_gnn_Wn1, L2_gnn_bn1, L2_gnn_Wn2, L2_gnn_bn2, L2_gnn_Wn3, L2_gnn_bn3, L3_gnn_W_rel, L3_gnn_b_rel, L3_gnn_W_loop, L3_gnn_W_gat, L3_gnn_attn_l, L3_gnn_attn_r, L3_gnn_b_gat, L3_gnn_W_fuse, L3_gnn_b_fuse, L3_gnn_W_gate, L3_gnn_b_gate):
    import jax
    import jax.numpy as jnp

    def _L0_gnn_ref(x, edge_index, W_agg, b_agg, gamma, beta):
        import jax, jax.numpy as jnp
        import numpy as np
        LN_EPS = 1e-05
        N = x.shape[0]
        src, dst = (edge_index[0], edge_index[1])
        messages = x[src]
        agg = jax.ops.segment_sum(messages, dst, num_segments=N)
        deg = jax.ops.segment_sum(jnp.ones(dst.shape, x.dtype), dst, num_segments=N)
        agg = agg / jnp.maximum(deg, 1.0)[:, None]
        h_in = jnp.concatenate([x, agg], axis=-1)
        h = h_in @ W_agg.T + b_agg
        y = h + x
        mean = jnp.mean(y, axis=-1, keepdims=True)
        var = jnp.var(y, axis=-1, keepdims=True)
        out = (y - mean) * jax.lax.rsqrt(var + LN_EPS) * gamma + beta
        return jax.nn.relu(out)

    def _L1_gnn_ref(x, edge_index, edge_attr, W1, root1, b1, W2, root2, b2):
        import jax, jax.numpy as jnp
        import numpy as np
        N, E, C = (50000, 18750, 128)

        def _spline_conv(x, src, dst, u, W, root, b):
            n = x.shape[0]
            h0 = x @ W[0]
            h1 = x @ W[1]
            msg = (1.0 - u) * h0[src] + u * h1[src]
            agg = jax.ops.segment_sum(msg, dst, num_segments=n)
            deg = jax.ops.segment_sum(jnp.ones((src.shape[0],), msg.dtype), dst, num_segments=n)
            agg = agg / jnp.maximum(deg, 1.0)[:, None]
            return agg + x @ root + b
        src, dst = (edge_index[0], edge_index[1])
        h = _spline_conv(x, src, dst, edge_attr, W1, root1, b1)
        return _spline_conv(h, src, dst, edge_attr, W2, root2, b2)

    def _L2_gnn_ref(node_feature, edge_src, edge_dst, edge_type, Wr1, br1, Wr2, br2, Wr3, br3, Wn1, bn1, Wn2, bn2, Wn3, bn3):
        import jax, jax.numpy as jnp
        import numpy as np
        N, E, D, R, H = (50000, 6250, 128, 4, 64)
        n, d = node_feature.shape
        r = Wr1.shape[0]
        x_src = node_feature[edge_src]
        h = jax.nn.relu(jnp.einsum('ed,rdh->reh', x_src, Wr1) + br1[:, None, :])
        h = jax.nn.relu(jnp.einsum('reh,rhk->rek', h, Wr2) + br2[:, None, :])
        msg = jax.nn.relu(jnp.einsum('rek,rkd->red', h, Wr3) + br3[:, None, :])
        mask = edge_type[None, :] == jnp.arange(r, dtype=edge_type.dtype)[:, None]
        msg = msg * mask[:, :, None].astype(msg.dtype)
        agg = jax.vmap(lambda m: jax.ops.segment_sum(m, edge_dst, num_segments=n))(msg)
        node_in = jnp.concatenate([jax.nn.relu(node_feature), agg.transpose(1, 0, 2).reshape(n, r * d)], axis=1)
        h = jax.nn.relu(node_in @ Wn1 + bn1)
        h = jax.nn.relu(h @ Wn2 + bn2)
        return h @ Wn3 + bn3

    def _L3_gnn_ref(feat, src, dst, etype, temporal_weight, W_rel, b_rel, W_loop, W_gat, attn_l, attn_r, b_gat, W_fuse, b_fuse, W_gate, b_gate):
        import jax, jax.numpy as jnp
        import numpy as np
        N, E, D, R, H, L = (30000, 15000, 128, 16, 4, 3)
        DH = D // H
        n = feat.shape[0]
        h = feat
        tw_mean = jnp.mean(temporal_weight)
        for l in range(L):
            ht = jnp.einsum('nd,rdo->nro', h, W_rel[l])
            msg = ht[src, etype]
            h_rel = jax.ops.segment_sum(msg, dst, num_segments=n)
            h_rel = h_rel + h @ W_loop[l] + b_rel[l]
            z = (h @ W_gat[l]).reshape(n, H, DH)
            el = jnp.sum(z * attn_l[l], axis=-1)
            er = jnp.sum(z * attn_r[l], axis=-1)
            e = jax.nn.leaky_relu(el[src] + er[dst], 0.2)
            m = jax.ops.segment_max(e, dst, num_segments=n)
            ex = jnp.exp(e - m[dst])
            denom = jax.ops.segment_sum(ex, dst, num_segments=n)
            alpha = ex / denom[dst]
            h_gat = jax.ops.segment_sum(alpha[:, :, None] * z[src], dst, num_segments=n)
            h_gat = h_gat.reshape(n, D) + b_gat[l]
            hc = jnp.concatenate([h_rel, h_gat], axis=1) @ W_fuse + b_fuse
            if l == 0:
                avg = jnp.full((n, 1), tw_mean, dtype=hc.dtype)
                gate = jax.nn.sigmoid(jnp.concatenate([hc, avg], axis=1) @ W_gate + b_gate)
                hc = hc * gate
            h = jax.nn.relu(hc)
        return h
    edge_index = jnp.stack([src, dst])
    h = jnp.maximum(_layernorm(x, axis=-1), 0.0)
    x = x + _L0_gnn_ref(h, edge_index, L0_gnn_W_agg, L0_gnn_b_agg, L0_gnn_gamma, L0_gnn_beta)
    h = jnp.maximum(_layernorm(x, axis=-1), 0.0)
    x = x + _L1_gnn_ref(h, edge_index, edge_weight1, L1_gnn_W1, L1_gnn_root1, L1_gnn_b1, L1_gnn_W2, L1_gnn_root2, L1_gnn_b2)
    h = jnp.maximum(_layernorm(x, axis=-1), 0.0)
    x = x + _L2_gnn_ref(h, src, dst, edge_type_4, L2_gnn_Wr1, L2_gnn_br1, L2_gnn_Wr2, L2_gnn_br2, L2_gnn_Wr3, L2_gnn_br3, L2_gnn_Wn1, L2_gnn_bn1, L2_gnn_Wn2, L2_gnn_bn2, L2_gnn_Wn3, L2_gnn_bn3)
    h = jnp.maximum(_layernorm(x, axis=-1), 0.0)
    x = x + _L3_gnn_ref(h, src, dst, edge_type_16, edge_weight, L3_gnn_W_rel, L3_gnn_b_rel, L3_gnn_W_loop, L3_gnn_W_gat, L3_gnn_attn_l, L3_gnn_attn_r, L3_gnn_b_gat, L3_gnn_W_fuse, L3_gnn_b_fuse, L3_gnn_W_gate, L3_gnn_b_gate)
    return x

_drawn_inputs = setup_inputs


def setup_inputs(seed=0):
    import zlib

    import numpy as np

    out = dict(_drawn_inputs(seed))
    spreads = {'L0_gnn_gamma': (1.0, 0.2),
     'L0_gnn_beta': (0.0, 0.403),
     'L2_gnn_br1': (0.0, 0.8),
     'L2_gnn_br2': (0.0, 0.8),
     'L2_gnn_br3': (0.0, 0.8),
     'L2_gnn_bn1': (0.0, 0.8),
     'L2_gnn_bn2': (0.0, 0.8),
     'L2_gnn_bn3': (0.0, 0.8),
     'L3_gnn_b_rel': (0.0, 0.391),
     'L3_gnn_b_gat': (0.0, 0.437),
     'L3_gnn_b_fuse': (0.0, 0.365),
     'L3_gnn_b_gate': (0.0, 0.409)}
    factors = {'edge_weight': 64.0,
     'L0_gnn_b_agg': 4.391,
     'L1_gnn_b1': 6.976,
     'L1_gnn_b2': 26.452,
     'L2_gnn_Wr1': 8.0,
     'L2_gnn_Wr2': 8.0,
     'L2_gnn_Wr3': 8.0,
     'L2_gnn_Wn1': 8.0,
     'L2_gnn_Wn2': 8.0,
     'L2_gnn_Wn3': 6.83,
     'L3_gnn_attn_r': 13.327,
     'edge_weight1': 2.896}
    for name, (base, spread) in spreads.items():
        noise = np.random.default_rng([zlib.crc32(name.encode()), seed]).standard_normal(out[name].shape)
        drawn = base * np.exp(spread * noise) if base else spread * noise
        out[name] = jnp.asarray(drawn.astype(out[name].dtype))
    for name, factor in factors.items():
        out[name] = (out[name] * factor).astype(out[name].dtype)
    return out
```

```python
from contextlib import ExitStack

import concourse.bass as bass
from concourse import mybir

P = 128
F32 = mybir.dt.float32
I32 = mybir.dt.int32
ALU = mybir.AluOpType
ACT = mybir.ActivationFunctionType
AX_X = mybir.AxisListType.X

N = 3125
D = 128
E = 53125
NT = 26
NP = NT * P
TPG = 4
GE = TPG * P
NG = -(-E // GE)
GR = P
TILES = GR * TPG
WIN = P
RING = 4
TURNS = NG // RING
R4, R16 = 4, 16
H, DH = 4, 32
HID = 64
LAYERS = 3
EPS = 1e-5
BIG = 1.0e30
PAD_NODE = 4000
FIRST_SEM = 110
FIRST_GATHER_SEM = 200
CH = [(4 * q, min(4, NT - 4 * q)) for q in range(-(-NT // 4))]
NCH = len(CH)


class Phase:

    def __init__(self, nc, name):
        self.nc, self.name, self.stack = nc, name, ExitStack()
        self.sems = []

    def __enter__(self):
        return self

    def sem(self, name):
        s = self.nc.alloc_semaphore(f"{self.name}_{name}", num=FIRST_SEM + len(self.sems))
        self.sems.append(s)
        return s

    def sb(self, name, shape, dt=F32):
        return self.stack.enter_context(self.nc.sbuf_tensor(f"{self.name}_{name}", shape, dt))

    def ps(self, name, shape, dt=F32):
        return self.stack.enter_context(self.nc.psum_tensor(f"{self.name}_{name}", shape, dt))

    def __exit__(self, *exc):
        if exc[0] is None:
            self.nc.all_engine_barrier(sems_to_clear=range(FIRST_SEM, FIRST_SEM + len(self.sems)))
            for s in self.sems:
                self.nc.release_semaphore(s)
        self.stack.close()


class Link:

    def __init__(self, eng, sem):
        self.eng, self.sem, self.n = eng, sem, 0

    def mark(self, ins):
        self.n += 1
        ins.then_inc(self.sem, 1)

    def join(self):
        self.eng.wait_ge(self.sem, self.n)

    def __call__(self, ins):
        self.mark(ins)
        self.join()


class Net:
    pass


def chunk(t, c):
    return t[:, c[0] * P:(c[0] + c[1]) * P]


def chunk3(t, c):
    return chunk(t, c).rearrange("p (t d) -> p t d", d=D)


def rows(dram, c):
    return dram[c[0] * P:(c[0] + c[1]) * P].rearrange("(t p) d -> p t d", p=P)


def load_phase(nc, n, a):
    with Phase(nc, "load") as ph:
        loaded, zeroed, built, made = ph.sem("loaded"), ph.sem("zeroed"), ph.sem("built"), ph.sem("made")
        turned = ph.sem("turned")
        iota_i = ph.sb("iota_i", [P, P], I32)
        wagg = ph.sb("wagg", [P, 2 * D])
        wt = ph.ps("wt", [P, 2, D])
        full, rest = NG - 1, E - (NG - 1) * GE
        xt, xr = N // P, N % P

        def col(v):
            return v.rearrange("(p o) -> p o", o=1)

        def bcast(v):
            return v.rearrange("(o d) -> o d", o=1).to_broadcast([P, D])

        plain = [
            (wagg[:, :], a["L0_gnn_W_agg"]),
            (n.w1[:, 0:2, :], a["L1_gnn_W1"].rearrange("k c o -> c k o")), (n.w1[:, 2, :], a["L1_gnn_root1"]),
            (n.w2[:, 0:2, :], a["L1_gnn_W2"].rearrange("k c o -> c k o")), (n.w2[:, 2, :], a["L1_gnn_root2"]),
            (n.wr1[:, :, :], a["L2_gnn_Wr1"].rearrange("r c o -> c r o")),
            (n.wr2[:, :, :], a["L2_gnn_Wr2"].rearrange("r c o -> c r o")),
            (n.wr3[:, :, :], a["L2_gnn_Wr3"].rearrange("r c o -> c r o")),
            (n.wn1[:, :, :], a["L2_gnn_Wn1"].rearrange("(k c) o -> c k o", c=D)),
            (n.wn2[:, :], a["L2_gnn_Wn2"]), (n.wn3[:, :], a["L2_gnn_Wn3"]),
            (n.br1[:, :], a["L2_gnn_br1"].rearrange("r h -> h r")),
            (n.br2[:, :], a["L2_gnn_br2"].rearrange("r h -> h r")),
            (n.br3[:, :], a["L2_gnn_br3"].rearrange("r h -> h r")),
            (n.bn12[:, 0:1], col(a["L2_gnn_bn1"])), (n.bn12[:, 1:2], col(a["L2_gnn_bn2"])),
            (n.wloop[:, :, :], a["L3_gnn_W_loop"].rearrange("l c o -> c l o")),
            (n.wgat[:, :, :], a["L3_gnn_W_gat"].rearrange("l c o -> c l o")),
            (n.wfuse[:, :, :], a["L3_gnn_W_fuse"].rearrange("(k c) o -> c k o", c=D)),
            (n.wgate[:, :], a["L3_gnn_W_gate"][0:D, :]),
            (n.cols[:, 0:3], a["L3_gnn_b_rel"].rearrange("l d -> d l")),
            (n.cols[:, 3:6], a["L3_gnn_b_gat"].rearrange("l d -> d l")),
            (n.cols[:, 6:7], col(a["L3_gnn_b_fuse"])), (n.cols[:, 7:8], col(a["L3_gnn_b_gate"])),
            (n.cols[:, 8:9], a["L3_gnn_W_gate"][D:D + 1, :].rearrange("o d -> d o")),
            (n.rowb[:, 0, :], bcast(a["L0_gnn_b_agg"])), (n.rowb[:, 1, :], bcast(a["L0_gnn_gamma"])),
            (n.rowb[:, 2, :], bcast(a["L0_gnn_beta"])), (n.rowb[:, 3, :], bcast(a["L1_gnn_b1"])),
            (n.rowb[:, 4, :], bcast(a["L1_gnn_b2"])), (n.rowb[:, 5, :], bcast(a["L2_gnn_bn3"])),
        ]
        for l in range(LAYERS):
            for side, w in enumerate(("L3_gnn_attn_l", "L3_gnn_attn_r")):
                plain.append((n.attn[:, l, side, :], a[w][l].rearrange("h (d o) -> o (h d)", o=1).to_broadcast([P, D])))
        x3 = n.x[:, :].rearrange("p (t d) -> p t d", d=D)
        after_zero = [
            (x3[:, 0:xt, :], a["x"][0:xt * P].rearrange("(t p) d -> p t d", p=P)),
            (x3[0:xr, xt, :], a["x"][xt * P:N]),
        ]
        for k, name in enumerate(("src", "dst", "edge_type_16", "edge_type_4")):
            after_zero += [
                (n.erow_i[0:full, k, :], a[name][0:full * GE].rearrange("(g e) -> g e", e=GE)),
                (n.erow_i[full:full + 1, k, 0:rest], a[name][full * GE:E].rearrange("(g e) -> g e", g=1)),
            ]
        w0, w1 = a["edge_weight"], a["edge_weight1"].rearrange("e o -> (e o)")
        for k, w in enumerate((w0, w1)):
            after_zero += [
                (n.erow_w[0:full, k, :], w[0:full * GE].rearrange("(g e) -> g e", e=GE)),
                (n.erow_w[full:full + 1, k, 0:rest], w[full * GE:E].rearrange("(g e) -> g e", g=1)),
            ]

        with nc.allow_non_contiguous_dma(reason="bias vectors, one element per partition"), nc.Block() as block:
            @block.sync
            def _(sp):
                sp.wait_ge(zeroed, 4)
                for dst, src in after_zero:
                    sp.dma_start(dst, src).then_inc(loaded, 16)
                sp.wait_ge(loaded, 16 * (len(plain) + len(after_zero)))

            @block.scalar
            def _(act):
                for dst, src in plain:
                    act.dma_start(dst, src).then_inc(loaded, 16)
                act.wait_ge(turned, 1)
                nc.scalar.copy(n.wagg_t[:, :, :], wt[:, :, :]).then_inc(made, 1)

            @block.vector
            def _(dve):
                nc.vector.memset(n.x[:, :], 0.0).then_inc(zeroed, 1)
                nc.vector.memset(n.erow_i[:, :, :], 0).then_inc(zeroed, 1)
                dve.wait_ge(zeroed, 2)
                nc.vector.memset(n.erow_i[:, 1, :], PAD_NODE).then_inc(zeroed, 1)
                nc.vector.memset(n.erow_w[:, :, :], 0.0).then_inc(zeroed, 1)
                nc.vector.memset(n.ones[:, :], 1.0).then_inc(made, 1)
                nc.vector.memset(n.eps[:, :], EPS).then_inc(made, 1)
                dve.wait_ge(built, 2)
                nc.vector.tensor_copy(n.iota[:, :], iota_i[:, :]).then_inc(made, 1)

            @block.gpsimd
            def _(pool):
                nc.gpsimd.memset(n.ident[:, :], 0.0).then_inc(built, 1)
                nc.gpsimd.iota(iota_i[:, :], pattern=[[1, P]], base=0, channel_multiplier=0).then_inc(built, 1)
                pool.wait_ge(built, 2)
                nc.gpsimd.affine_select(out=n.ident[:, :], in_=n.ident[:, :], compare_op=ALU.not_equal, fill=1.0,
                                        base=0, pattern=[[-1, P]], channel_multiplier=1).then_inc(built, 1)

            @block.tensor
            def _(pe):
                pe.wait_ge(built, 3)
                pe.wait_ge(loaded, 16 * (len(plain) + len(after_zero)))
                for k in range(2):
                    t = nc.tensor.transpose(wt[:, k, :], wagg[:, k * D:(k + 1) * D], n.ident[:, :])
                t.then_inc(turned, 1)


def edge_phase(nc, n):
    with Phase(nc, "edge") as ph:
        link_sem, ready, turned, taken = ph.sem("link"), ph.sem("ready"), ph.sem("turned"), ph.sem("taken")
        f = ph.sb("f", [P, 4, GE])
        idx16 = ph.sb("idx16", [P, GE])
        idx4 = ph.sb("idx4", [P, GE])
        dstc = ph.sb("dstc", [P, GE])
        dstl = ph.sb("dstl", [P, GE])
        ends = ph.sb("ends", [P, 3, H])
        fl = ph.sb("fl", [H, 2, GR])
        same = ph.sb("same", [H, 3, GR])
        wsum = ph.sb("wsum", [P, 1])
        turn = ph.ps("turn", [P, 6, TPG, P])
        ends_t = ph.ps("ends_t", [P, 4, P])

        fields = [f[:, 0, :], idx4[:, :], idx16[:, :], dstc[:, :], dstl[:, :], n.erow_w[:, 1, :]]
        cols = [n.c_src, n.c_i4, n.c_i16, n.c_dst, n.c_dstl, n.c_u]

        with nc.Block() as block:
            @block.vector
            def _(dve):
                v = nc.vector
                link = Link(dve, link_sem)
                link(v.tensor_copy(f[:, :, :], n.erow_i[:, :, :]))
                link.mark(v.scalar_tensor_tensor(out=idx16[:, :], in0=f[:, 0, :], scalar=float(R16), in1=f[:, 2, :], op0=ALU.mult, op1=ALU.add))
                link.mark(v.scalar_tensor_tensor(out=idx4[:, :], in0=f[:, 0, :], scalar=float(R4), in1=f[:, 3, :], op0=ALU.mult, op1=ALU.add))
                link.mark(v.tensor_scalar(dstc[:, :], f[:, 1, :], float(NP - 1), None, ALU.min))
                link.mark(v.tensor_copy(ends[:, 0, :], f[:, 1, 0:1].to_broadcast([P, H])))
                link.mark(v.tensor_copy(ends[:, 1, :], f[:, 1, GE - 1:GE].to_broadcast([P, H])))
                link.mark(v.tensor_scalar(ends[:, 2, :], f[:, 1, 0:1].to_broadcast([P, H]), float(NP - WIN), None, ALU.min))
                link.join()
                link.mark(v.tensor_scalar(dstl[:, :], f[:, 1, :], ends[:, 2, 0:1], None, ALU.subtract))
                link.mark(v.memset(n.rf[:, 0:1], 0.0))
                link.mark(v.memset(n.rb[:, GE - 1:GE], 0.0))
                link(v.tensor_tensor(n.rf[:, 1:GE], f[:, 1, 1:GE], f[:, 1, 0:GE - 1], ALU.not_equal))
                link(v.tensor_scalar(n.rf[:, 1:GE], n.rf[:, 1:GE], -BIG, None, ALU.mult))
                link.mark(v.tensor_copy(n.rb[:, 0:GE - 1], n.rf[:, 1:GE]))
                link.mark(v.reduce_sum(wsum[:, :], n.erow_w[:, 0, :], AX_X))
                link.join()
                v.memset(same[:, :, :], 0.0).then_inc(ready, 1)
                for k, c in enumerate(cols):
                    dve.wait_ge(turned, k + 1)
                    v.tensor_copy(c[:, :].rearrange("p (g k) -> p k g", k=TPG), turn[:, k, :, :]).then_inc(taken, 1)
                dve.wait_ge(turned, 7)
                dve.wait_ge(ready, 1)
                link.mark(v.tensor_copy(n.base[:, :], ends_t[0:1, 2, :]))
                link.mark(v.tensor_scalar(n.tw[:, :], ends_t[:, 3, 0:1], 1.0 / E, None, ALU.mult))
                link(v.tensor_copy(fl[:, :, :], ends_t[0:H, 0:2, :]))
                link.mark(v.tensor_tensor(same[:, 0, 1:GR], fl[:, 0, 1:GR], fl[:, 1, 0:GR - 1], ALU.is_equal))
                link.mark(v.tensor_tensor(same[:, 1, :], fl[:, 0, :], fl[:, 1, :], ALU.is_equal))
                link.mark(v.memset(n.seg[:, :, :], 0.0))
                link.join()
                link.mark(v.tensor_copy(n.seg[:, 0, :], same[:, 0, :]))
                link.mark(v.tensor_tensor(n.seg[:, 1, :], same[:, 0, :], same[:, 1, :], ALU.mult))
                link.mark(v.tensor_tensor(n.seg[:, 2, 0:GR - 1], same[:, 0, 1:GR], same[:, 1, 0:GR - 1], ALU.mult))
                link.join()
                link(v.tensor_scalar(n.seg[:, :, :], n.seg[:, :, :], -1.0, BIG, ALU.add, ALU.mult))

            @block.tensor
            def _(pe):
                pe.wait_ge(ready, 1)
                for k, r in enumerate(fields):
                    for j in range(TPG):
                        t = nc.tensor.transpose(turn[:, k, j, :], r[:, j * P:(j + 1) * P], n.ident[:, :])
                    t.then_inc(turned, 1)
                nc.tensor.transpose(ends_t[0:H, 0, :], ends[:, 0, :], n.ident[:, :])
                nc.tensor.transpose(ends_t[0:H, 1, :], ends[:, 1, :], n.ident[:, :])
                nc.tensor.transpose(ends_t[0:H, 2, :], ends[:, 2, :], n.ident[:, :])
                nc.tensor.matmul(ends_t[:, 3, 0:1], n.ones[:, :], wsum[:, :], start=True, stop=True).then_inc(turned, 1)


def norm_steps(nc, ph, link, dve, src, cen, sum_, sq, root, var_ready, root_ready):
    v = nc.vector
    for c in CH:
        link.mark(v.reduce_sum(sum_[:, 0, c[0]:c[0] + c[1]], chunk3(src, c), AX_X))
    link.join()
    link(v.tensor_scalar(sum_[:, 1, :], sum_[:, 0, :], 1.0 / D, None, ALU.mult))
    for i, c in enumerate(CH):
        t = slice(c[0], c[0] + c[1])
        mean = sum_[:, 1, t].unsqueeze(2).to_broadcast([P, c[1], D])
        link(v.tensor_tensor(chunk3(cen, c), chunk3(src, c), mean, ALU.subtract))
        link(v.tensor_tensor(sq[:, 0:c[1], :], chunk3(cen, c), chunk3(cen, c), ALU.mult))
        link(v.reduce_sum(sum_[:, 2, t], sq[:, 0:c[1], :], AX_X))
    v.tensor_scalar(sum_[:, 3, :], sum_[:, 2, :], 1.0 / D, EPS, ALU.mult, ALU.add).then_inc(var_ready, 1)
    dve.wait_ge(root_ready, 1)
    link(v.reciprocal(root[:, 1, :], root[:, 0, :]))


def norm_root(nc, act, sum_, root, var_ready, root_ready):
    act.wait_ge(var_ready, 1)
    nc.scalar.activation(root[:, 0, :], sum_[:, 3, :], ACT.Sqrt).then_inc(root_ready, 1)


def turn_and_store(nc, block, n, src, table, src_ready, turned, stored, ps):
    @block.tensor
    def _(pe):
        for q, c in enumerate(CH):
            pe.wait_ge(src_ready, q + 1)
            for j in range(c[1]):
                t = nc.tensor.transpose(ps[:, q, j, :], chunk(src, (c[0] + j, 1)), n.ident[:, :])
            t.then_inc(turned, 1)

    @block.sync
    def _(sp):
        for q, c in enumerate(CH):
            sp.wait_ge(src_ready, q + 1)
            sp.dma_start(rows(table, c), chunk3(src, c)).then_inc(stored, 16)
        sp.wait_ge(stored, 16 * NCH)


def norm_phase(nc, n, name, table):
    with Phase(nc, name) as ph:
        link_sem, var_ready, root_ready = ph.sem("link"), ph.sem("var"), ph.sem("root")
        h_ready, turned, stored = ph.sem("h_ready"), ph.sem("turned"), ph.sem("stored")
        sum_, root, sq = ph.sb("sum", [P, 4, NT]), ph.sb("rootv", [P, 2, NT]), ph.sb("sq", [P, 4, D])
        ps = ph.ps("ps", [P, NCH, 4, P])
        with nc.Block() as block:
            @block.vector
            def _(dve):
                link = Link(dve, link_sem)
                norm_steps(nc, ph, link, dve, n.x, n.hn, sum_, sq, root, var_ready, root_ready)
                for c in CH:
                    rstd = root[:, 1, c[0]:c[0] + c[1]].unsqueeze(2).to_broadcast([P, c[1], D])
                    nc.vector.scalar_tensor_tensor(out=chunk3(n.hn, c), in0=chunk3(n.hn, c), scalar=0.0, in1=rstd,
                                                   op0=ALU.max, op1=ALU.mult).then_inc(h_ready, 1)

            @block.scalar
            def _(act):
                norm_root(nc, act, sum_, root, var_ready, root_ready)
                for q, c in enumerate(CH):
                    act.wait_ge(turned, q + 1)
                    nc.scalar.copy(chunk3(n.ht, c), ps[:, q, 0:c[1], :])

            turn_and_store(nc, block, n, n.hn, table, h_ready, turned, stored, ps)


def edge_pass(nc, n, name, table, idx, width, mode):
    regions = {"degree": 2, "spline": 2, "plain": 1, "attend": 3}[mode]
    feats = min(width, D)
    with Phase(nc, name) as ph:
        idx_ready = [ph.sem(f"idx_ready{h}") for h in range(2)]
        got, got0 = n.got, n.got_count
        n.got_count += TURNS * 16 * TPG
        hot = [ph.sem(f"hot{s}") for s in range(RING)]
        used = [ph.sem(f"used{s}") for s in range(RING)]
        added = ph.sem("added")
        cleared, link_sem = ph.sem("cleared"), ph.sem("link")
        idxs = ph.sb("idxs", [P, 2, 2 * TPG], I32)
        g = ph.sb("g", [P, RING, TPG, width])
        oh = ph.sb("oh", [P, RING, TPG, WIN])
        ps = ph.ps("ps", [P, RING, 4 * P])
        if mode == "spline":
            ohw = ph.sb("ohw", [P, RING, TPG, 2, WIN])
        if mode == "attend":
            spread = [ph.sem(f"spread{s}") for s in range(RING)]
            scaled = [ph.sem(f"scaled{s}") for s in range(RING)]
            exs = ph.sb("exs", [P, RING, TPG, D])
            zs = ph.sb("zs", [P, RING, TPG, D])
            exg = n.ex[:, :].rearrange("p (t h) -> p t h", h=H)

        def build_ops():
            return 3 if mode == "spline" else 1

        with nc.Block() as block:
            @block.gpsimd
            def _(pool):
                with pool.Fori(1, TURNS + 1) as turn:
                    for s in range(RING):
                        half, j0 = s // 2, (s % 2) * TPG
                        if s % 2 == 0:
                            pool.wait_ge(used[s], turn)
                            pool.wait_ge(used[s + 1], turn)
                            nc.gpsimd.tensor_copy(idxs[:, half, :], idx[:, bass.ds(turn * (RING * TPG) + (s - RING) * TPG, 2 * TPG)]).then_inc(idx_ready[half], 1)
                            pool.wait_ge(cleared, 1)
                            pool.wait_ge(idx_ready[half], turn)
                        for j in range(TPG):
                            pool.indirect_dma_start(g[:, s, j, :], None, table, bass.IndirectOffsetOnAxis(
                                ap=idxs[:, half, j0 + j:j0 + j + 1], axis=0)).then_inc(got[s], 16)

            @block.tensor
            def _(pe):
                for s in range(RING):
                    pe.sem_inc(used[s], 1)
                with pe.Fori(0, TURNS) as i:
                    for s in range(RING):
                        pe.wait_ge(got[s], i * (16 * TPG) + (got0 + 16 * TPG))
                        pe.wait_ge(hot[s], i * build_ops() + build_ops())
                        pe.wait_ge(added, i * RING + (s + 1))
                        if mode == "attend":
                            pe.wait_ge(spread[s], i + 1)
                            pe.wait_ge(scaled[s], i + 1)
                        for j in range(TPG):
                            first, last = j == 0, j == TPG - 1
                            if mode == "spline":
                                mm = nc.tensor.matmul(ps[:, s, 0:2 * WIN], g[:, s, j, :], ohw[:, s, j, :, :].rearrange("p a w -> p (a w)"),
                                                      start=first, stop=last)
                                continue
                            left = [g[:, s, j, 0:feats]]
                            if mode == "degree":
                                left.append(n.ones[:, :])
                            if mode == "attend":
                                left += [zs[:, s, j, :], exs[:, s, j, :]]
                            for r, lt in enumerate(left):
                                mm = nc.tensor.matmul(ps[0:feats, s, r * WIN:(r + 1) * WIN], lt, oh[:, s, j, :],
                                                      start=first and r == 0, stop=last, skip_group_check=True)
                        mm.then_inc(used[s], 1)

            @block.vector
            def _(dve):
                v = nc.vector
                v.memset(n.acc[:, 0:regions, :], 0.0).then_inc(cleared, 1)
                dve.wait_ge(cleared, 1)
                dve.sem_inc(added, RING)
                iota = n.iota[:, :].unsqueeze(1).to_broadcast([P, TPG, WIN])
                with dve.Fori(0, TURNS) as i:
                    def build(s):
                        tiles = bass.ds(i * (RING * TPG) + s * TPG, TPG)
                        dstl = n.c_dstl[:, tiles].unsqueeze(2).to_broadcast([P, TPG, WIN])
                        dve.wait_ge(used[s], i + 1)
                        v.tensor_tensor(oh[:, s, :, :], iota, dstl, ALU.is_equal).then_inc(hot[s], 1)
                        if mode == "spline":
                            u = n.c_u[:, tiles].unsqueeze(2).to_broadcast([P, TPG, WIN])
                            dve.wait_ge(hot[s], i * 3 + 1)
                            v.tensor_tensor(ohw[:, s, :, 1, :], oh[:, s, :, :], u, ALU.mult).then_inc(hot[s], 1)
                            dve.wait_ge(hot[s], i * 3 + 2)
                            v.tensor_tensor(ohw[:, s, :, 0, :], oh[:, s, :, :], ohw[:, s, :, 1, :], ALU.subtract).then_inc(hot[s], 1)
                        if mode == "attend":
                            dve.wait_ge(got[s], i * (16 * TPG) + (got0 + 16 * TPG))
                            dve.wait_ge(spread[s], i + 1)
                            v.tensor_tensor(zs[:, s, :, :], g[:, s, :, D:2 * D], exs[:, s, :, :], ALU.mult).then_inc(scaled[s], 1)

                    def add(s):
                        base = nc.vector.value_load(n.base[0:1, bass.ds(i * RING + s, 1)], min_val=0, max_val=NP - WIN)
                        dve.wait_ge(used[s], i + 2)
                        dve.wait_ge(added, i * RING + (RING + s))
                        out = n.acc[0:feats, 0:regions, bass.ds(base, WIN)]
                        v.tensor_tensor(out, out, ps[0:feats, s, 0:regions * WIN].rearrange("p (r w) -> p r w", w=WIN),
                                        ALU.add).then_inc(added, 1)

                    for s in range(RING):
                        build(s)
                        if s:
                            add(s - 1)
                    add(RING - 1)

            if mode == "attend":
                @block.scalar
                def _(act):
                    with act.Fori(0, TURNS) as i:
                        for s in range(RING):
                            act.wait_ge(used[s], i + 1)
                            w = exg[:, bass.ds(i * (RING * TPG) + s * TPG, TPG), :]
                            nc.scalar.copy(exs[:, s, :, :].rearrange("p t (h d) -> p t h d", d=DH),
                                           w.unsqueeze(3).to_broadcast([P, TPG, H, DH])).then_inc(spread[s], 1)


def mean_layer(nc, n):
    with Phase(nc, "mean") as ph:
        link_sem, var_ready, root_ready = ph.sem("link"), ph.sem("var"), ph.sem("root")
        agg_ready, mixed = ph.sem("agg_ready"), ph.sem("mixed")
        sum_, root, sq = ph.sb("sum", [P, 4, NT]), ph.sb("rootv", [P, 2, NT]), ph.sb("sq", [P, 4, D])
        ps = ph.ps("ps", [P, NCH, 4, P])
        agg, y = n.acc[:, 0, :], n.acc[:, 1, :]
        with nc.Block() as block:
            @block.vector
            def _(dve):
                v = nc.vector
                link = Link(dve, link_sem)
                for c in CH:
                    link(v.tensor_scalar(chunk(n.rdeg, c), chunk(y, c), 1.0, None, ALU.max))
                    link(v.reciprocal(chunk(n.rdeg, c), chunk(n.rdeg, c)))
                    v.tensor_tensor(chunk(agg, c), chunk(agg, c), chunk(n.rdeg, c), ALU.mult).then_inc(agg_ready, 1)
                for q, c in enumerate(CH):
                    dve.wait_ge(mixed, q + 1)
                    b = n.rowb[:, 0, :].unsqueeze(1).to_broadcast([P, c[1], D])
                    link(v.tensor_tensor(chunk3(y, c), ps[:, q, 0:c[1], :], b, ALU.add))
                    link(v.tensor_tensor(chunk3(y, c), chunk3(y, c), chunk3(n.hn, c), ALU.add))
                norm_steps(nc, ph, link, dve, y, y, sum_, sq, root, var_ready, root_ready)
                for c in CH:
                    rstd = root[:, 1, c[0]:c[0] + c[1]].unsqueeze(2).to_broadcast([P, c[1], D])
                    gamma = n.rowb[:, 1, :].unsqueeze(1).to_broadcast([P, c[1], D])
                    beta = n.rowb[:, 2, :].unsqueeze(1).to_broadcast([P, c[1], D])
                    link(v.tensor_tensor(chunk3(y, c), chunk3(y, c), rstd, ALU.mult))
                    link(v.tensor_tensor(chunk3(y, c), chunk3(y, c), gamma, ALU.mult))
                    link(v.tensor_tensor(chunk3(y, c), chunk3(y, c), beta, ALU.add))
                    link(v.scalar_tensor_tensor(out=chunk3(n.x, c), in0=chunk3(y, c), scalar=0.0, in1=chunk3(n.x, c),
                                                op0=ALU.max, op1=ALU.add))

            @block.scalar
            def _(act):
                norm_root(nc, act, sum_, root, var_ready, root_ready)

            @block.tensor
            def _(pe):
                for q, c in enumerate(CH):
                    pe.wait_ge(agg_ready, q + 1)
                    for j in range(c[1]):
                        t = (c[0] + j, 1)
                        nc.tensor.matmul(ps[:, q, j, :], chunk(n.ht, t), n.wagg_t[:, 0, :], start=True, stop=False)
                        mm = nc.tensor.matmul(ps[:, q, j, :], chunk(agg, t), n.wagg_t[:, 1, :], start=False, stop=True)
                    mm.then_inc(mixed, 1)


def spline_layer(nc, n, name, w, bias_row, table):
    with Phase(nc, name) as ph:
        link_sem, agg_ready, mixed = ph.sem("link"), ph.sem("agg_ready"), ph.sem("mixed")
        out_ready, turned, stored = ph.sem("out_ready"), ph.sem("turned"), ph.sem("stored")
        ps = ph.ps("ps", [P, NCH, 4, P])
        a0, a1 = n.acc[:, 0, :], n.acc[:, 1, :]
        with nc.Block() as block:
            @block.vector
            def _(dve):
                v = nc.vector
                link = Link(dve, link_sem)
                for c in CH:
                    v.tensor_tensor(chunk(a0, c), chunk(a0, c), chunk(n.rdeg, c), ALU.mult).then_inc(agg_ready, 1)
                    v.tensor_tensor(chunk(a1, c), chunk(a1, c), chunk(n.rdeg, c), ALU.mult).then_inc(agg_ready, 1)
                for q, c in enumerate(CH):
                    dve.wait_ge(mixed, q + 1)
                    b = n.rowb[:, bias_row, :].unsqueeze(1).to_broadcast([P, c[1], D])
                    ins = v.tensor_tensor(chunk3(n.hn, c), ps[:, q, 0:c[1], :], b, ALU.add)
                    if table is not None:
                        ins.then_inc(out_ready, 1)
                        continue
                    link(ins)
                    link(v.tensor_tensor(chunk3(n.x, c), chunk3(n.x, c), chunk3(n.hn, c), ALU.add))

            @block.tensor
            def _(pe):
                for q, c in enumerate(CH):
                    pe.wait_ge(agg_ready, 2 * q + 2)
                    for j in range(c[1]):
                        t = (c[0] + j, 1)
                        nc.tensor.matmul(ps[:, q, j, :], chunk(a0, t), w[:, 0, :], start=True, stop=False)
                        nc.tensor.matmul(ps[:, q, j, :], chunk(a1, t), w[:, 1, :], start=False, stop=False)
                        mm = nc.tensor.matmul(ps[:, q, j, :], chunk(n.ht, t), w[:, 2, :], start=False, stop=True)
                    mm.then_inc(mixed, 1)
                if table is not None:
                    for q, c in enumerate(CH):
                        pe.wait_ge(out_ready, q + 1)
                        for j in range(c[1]):
                            t = nc.tensor.transpose(ps[:, q, j, :], chunk(n.hn, (c[0] + j, 1)), n.ident[:, :])
                        t.then_inc(turned, 1)

            if table is not None:
                @block.scalar
                def _(act):
                    for q, c in enumerate(CH):
                        act.wait_ge(turned, q + 1)
                        nc.scalar.copy(chunk3(n.ht, c), ps[:, q, 0:c[1], :])

                @block.sync
                def _(sp):
                    for q, c in enumerate(CH):
                        sp.wait_ge(out_ready, q + 1)
                        sp.dma_start(rows(table, c), chunk3(n.hn, c)).then_inc(stored, 16)
                    sp.wait_ge(stored, 16 * NCH)


def message_phase(nc, n, table):
    with Phase(nc, "msg") as ph:
        made = [ph.sem(f"made{k}") for k in range(4)]
        kept = [ph.sem(f"kept{k}") for k in range(4)]
        stored = ph.sem("stored")
        a1 = ph.sb("a1", [HID, R4, 4 * P])
        a2 = ph.sb("a2", [HID, R4, 4 * P])
        a3 = ph.sb("a3", [P, R4, 4 * P])
        ps = ph.ps("ps", [P, 8, 4 * P])
        m = n.acc[:, 0:2, :].rearrange("p a (t o) -> p (a t o)", o=2 * D).rearrange("p (t r o) -> p t r o", r=R4, o=HID)
        with nc.Block() as block:
            @block.tensor
            def _(pe):
                for q, c in enumerate(CH):
                    w = c[1] * P
                    for r in range(R4):
                        if q:
                            pe.wait_ge(kept[2], R4 * (q - 1) + r + 1)
                        nc.tensor.matmul(ps[0:HID, r, 0:w], n.wr1[:, r, :], chunk(n.ht, c), start=True, stop=True).then_inc(made[0], 1)
                    for r in range(R4):
                        pe.wait_ge(kept[0], R4 * q + r + 1)
                        if q:
                            pe.wait_ge(kept[3], R4 * (q - 1) + r + 1)
                        nc.tensor.matmul(ps[0:HID, R4 + r, 0:w], n.wr2[:, r, :], a1[:, r, 0:w], start=True, stop=True).then_inc(made[1], 1)
                    for r in range(R4):
                        pe.wait_ge(kept[1], R4 * q + r + 1)
                        nc.tensor.matmul(ps[:, r, 0:w], n.wr3[:, r, :], a2[:, r, 0:w], start=True, stop=True).then_inc(made[2], 1)
                    for r in range(R4):
                        pe.wait_ge(kept[2], R4 * q + r + 1)
                        for j in range(c[1]):
                            mm = nc.tensor.matmul(ps[:, R4 + r, j * HID:(j + 1) * HID], a3[:, r, j * P:(j + 1) * P],
                                                  n.wn1[:, 1 + r, :], start=True, stop=True)
                        mm.then_inc(made[3], 1)

            @block.scalar
            def _(act):
                stages = ((a1, n.br1, HID, 0), (a2, n.br2, HID, R4), (a3, n.br3, P, 0))
                for q, c in enumerate(CH):
                    w = c[1] * P
                    for k, (out, bias, rows_, bank) in enumerate(stages):
                        for r in range(R4):
                            act.wait_ge(made[k], R4 * q + r + 1)
                            if q:
                                act.wait_ge(made[k + 1], R4 * (q - 1) + r + 1)
                            nc.scalar.activation(out[:, r, 0:w], ps[0:rows_, bank + r, 0:w], ACT.Relu,
                                                 bias=bias[:, r:r + 1]).then_inc(kept[k], 1)

            @block.vector
            def _(dve):
                for q, c in enumerate(CH):
                    for r in range(R4):
                        dve.wait_ge(made[3], R4 * q + r + 1)
                        nc.vector.tensor_copy(m[:, c[0]:c[0] + c[1], r, :],
                                              ps[:, R4 + r, 0:c[1] * HID].rearrange("p (t o) -> p t o", o=HID)).then_inc(kept[3], 1)

            @block.sync
            def _(sp):
                out = table.rearrange("(t p r) o -> p t (r o)", p=P, r=R4)
                for q, c in enumerate(CH):
                    sp.wait_ge(kept[3], R4 * (q + 1))
                    sp.dma_start(out[:, c[0]:c[0] + c[1], :], m[:, c[0]:c[0] + c[1], :, :].rearrange("p t r o -> p t (r o)")).then_inc(stored, 16)
                sp.wait_ge(stored, 16 * NCH)


def relation_layer(nc, n):
    with Phase(nc, "rel") as ph:
        made = [ph.sem(f"made{k}") for k in range(3)]
        summed, kept, link_sem, out_read = ph.sem("summed"), [ph.sem("kept0"), ph.sem("kept1")], ph.sem("link"), ph.sem("out_read")
        t0 = ph.sb("t0", [HID, 2, 4 * P])
        q1 = ph.sb("q1", [HID, 2, 4 * P])
        q2 = ph.sb("q2", [HID, 2, 4 * P])
        out = ph.sb("out", [P, 4, D])
        ps = ph.ps("ps", [P, 3, 2, 4 * P])
        with nc.Block() as block:
            @block.tensor
            def _(pe):
                def first(q):
                    if q >= 2:
                        pe.wait_ge(summed, q - 1)
                    nc.tensor.matmul(ps[0:HID, 0, q % 2, 0:CH[q][1] * P], n.wn1[:, 0, :], chunk(n.ht, CH[q]), start=True, stop=True).then_inc(made[0], 1)

                first(0)
                for q, c in enumerate(CH):
                    w = c[1] * P
                    if q + 1 < NCH:
                        first(q + 1)
                    pe.wait_ge(kept[0], q + 1)
                    if q >= 2:
                        pe.wait_ge(kept[1], q - 1)
                    nc.tensor.matmul(ps[0:HID, 1, q % 2, 0:w], n.wn2[:, :], q1[:, q % 2, 0:w], start=True, stop=True).then_inc(made[1], 1)
                    pe.wait_ge(kept[1], q + 1)
                    if q >= 2:
                        pe.wait_ge(out_read, q - 1)
                    for j in range(c[1]):
                        mm = nc.tensor.matmul(ps[:, 2, q % 2, j * D:(j + 1) * D], q2[:, q % 2, j * P:(j + 1) * P], n.wn3[:, :],
                                              start=True, stop=True)
                    mm.then_inc(made[2], 1)

            @block.scalar
            def _(act):
                for q, c in enumerate(CH):
                    w = c[1] * P
                    act.wait_ge(summed, q + 1)
                    if q >= 2:
                        act.wait_ge(made[1], q - 1)
                    nc.scalar.activation(q1[:, q % 2, 0:w], t0[:, q % 2, 0:w], ACT.Relu, bias=n.bn12[:, 0:1]).then_inc(kept[0], 1)
                    act.wait_ge(made[1], q + 1)
                    if q >= 2:
                        act.wait_ge(made[2], q - 1)
                    nc.scalar.activation(q2[:, q % 2, 0:w], ps[0:HID, 1, q % 2, 0:w], ACT.Relu, bias=n.bn12[:, 1:2]).then_inc(kept[1], 1)

            @block.vector
            def _(dve):
                v = nc.vector
                link = Link(dve, link_sem)

                def add_sums(q):
                    w = CH[q][1] * P
                    dve.wait_ge(made[0], q + 1)
                    if q >= 2:
                        dve.wait_ge(kept[0], q - 1)
                    v.tensor_tensor(t0[:, q % 2, 0:w], ps[0:HID, 0, q % 2, 0:w], chunk(n.acc[0:HID, 0, :], CH[q]), ALU.add).then_inc(summed, 1)

                add_sums(0)
                for q, c in enumerate(CH):
                    if q + 1 < NCH:
                        add_sums(q + 1)
                    dve.wait_ge(made[2], q + 1)
                    b = n.rowb[:, 5, :].unsqueeze(1).to_broadcast([P, c[1], D])
                    v.tensor_tensor(out[:, 0:c[1], :], ps[:, 2, q % 2, 0:c[1] * D].rearrange("p (t d) -> p t d", d=D), b, ALU.add).then_inc(out_read, 1)
                    dve.wait_ge(out_read, q + 1)
                    link(v.tensor_tensor(chunk3(n.x, c), chunk3(n.x, c), out[:, 0:c[1], :], ALU.add))


def table_phase(nc, n, l, w_rel, table, elr_table):
    with Phase(nc, f"tab{l}") as ph:
        loaded, link_sem = ph.sem("loaded"), ph.sem("link")
        made = ph.sem("made")
        took_a, took_b, took_z = ph.sem("took_a"), ph.sem("took_b"), ph.sem("took_z")
        stored_h = [ph.sem(f"stored_h{k}") for k in range(2)]
        stored_z = [ph.sem(f"stored_z{k}") for k in range(2)]
        scores, stored_e = ph.sem("scores"), ph.sem("stored_e")
        wrel = ph.sb("wrel", [P, R16, D])
        st = ph.sb("st", [P, 2, R16 * D])
        zst = ph.sb("zst", [P, 2, D])
        prod = ph.sb("prod", [P, 2, D])
        elr = ph.sb("elr", [P, NT, 2 * H])
        ps = ph.ps("ps", [P, 3, 1024])
        psz = ph.ps("psz", [P, 2, 512])
        tab = table.rearrange("(t p r) c -> t p r c", p=P, r=R16)
        with nc.Block() as block:
            @block.tensor
            def _(pe):
                pe.wait_ge(loaded, 16)
                for t in range(NT):
                    for half in range(2):
                        u = 2 * t + half
                        if u >= 3:
                            if (u - 3) % 2 == 0:
                                pe.wait_ge(took_a, (u - 3) // 2 + 1)
                            else:
                                pe.wait_ge(took_b, (u - 3) // 2 + 1)
                        for b in range(2):
                            r0 = half * 8 + b * 4
                            mm = nc.tensor.matmul(ps[:, u % 3, b * 512:(b + 1) * 512], chunk(n.ht, (t, 1)),
                                                  wrel[:, r0:r0 + 4, :].rearrange("p r o -> p (r o)"), start=True, stop=True)
                        mm.then_inc(made, 1)
                    if t >= 2:
                        pe.wait_ge(scores, t - 1)
                    nc.tensor.matmul(psz[:, t % 2, 0:D], chunk(n.ht, (t, 1)), n.wgat[:, l, :], start=True, stop=True).then_inc(made, 1)

            @block.scalar
            def _(act):
                for t in range(NT):
                    act.wait_ge(made, 3 * t + 1)
                    if t >= 2:
                        act.wait_ge(stored_h[t % 2], 16 * (t // 2))
                    nc.scalar.copy(st[:, t % 2, 0:1024], ps[:, (2 * t) % 3, :]).then_inc(took_a, 1)
                    act.wait_ge(took_z, t + 1)
                    act.dma_start(tab[t, :, :, D:2 * D], zst[:, t % 2, :].unsqueeze(1).to_broadcast([P, R16, D])).then_inc(stored_z[t % 2], 16)
                for k in range(2):
                    act.wait_ge(stored_z[k], 16 * (NT // 2))

            @block.vector
            def _(dve):
                v = nc.vector
                link = Link(dve, link_sem)
                for t in range(NT):
                    dve.wait_ge(made, 3 * t + 2)
                    if t >= 2:
                        dve.wait_ge(stored_h[t % 2], 16 * (t // 2))
                    v.tensor_copy(st[:, t % 2, 1024:2048], ps[:, (2 * t + 1) % 3, :]).then_inc(took_b, 1)
                    dve.wait_ge(made, 3 * t + 3)
                    if t >= 2:
                        dve.wait_ge(stored_z[t % 2], 16 * (t // 2))
                    v.tensor_copy(zst[:, t % 2, :], psz[:, t % 2, 0:D]).then_inc(took_z, 1)
                    link(v.tensor_tensor(prod[:, :, :], psz[:, t % 2, 0:D].unsqueeze(1).to_broadcast([P, 2, D]), n.attn[:, l, :, :], ALU.mult))
                    v.reduce_sum(elr[:, t, :], prod[:, :, :].rearrange("p s (h d) -> p (s h) d", d=DH), AX_X).then_inc(scores, 1)
                    dve.wait_ge(scores, t + 1)

            @block.sync
            def _(sp):
                sp.dma_start(wrel[:, :, :], w_rel[l].rearrange("r c o -> c r o")).then_inc(loaded, 16)
                for t in range(NT):
                    sp.wait_ge(took_a, t + 1)
                    sp.wait_ge(took_b, t + 1)
                    sp.dma_start(tab[t, :, :, 0:D], st[:, t % 2, :].rearrange("p (r o) -> p r o", o=D)).then_inc(stored_h[t % 2], 16)
                sp.wait_ge(scores, NT)
                sp.dma_start(elr_table.rearrange("(t p) c -> p t c", p=P), elr[:, :, :]).then_inc(stored_e, 16)
                sp.wait_ge(stored_e, 16)
                for k in range(2):
                    sp.wait_ge(stored_h[k], 16 * (NT // 2))


def score_pass(nc, n, l, elr_table):
    HT = 8
    turns = NG * TPG // (2 * HT)
    with Phase(nc, f"sc{l}") as ph:
        src_ready = [ph.sem(f"src_ready{h}") for h in range(2)]
        dst_ready = [ph.sem(f"dst_ready{h}") for h in range(2)]
        started = ph.sem("started")
        got, got0 = n.score_got, n.score_count
        n.score_count += turns * 32 * HT
        used = [ph.sem(f"used{h}") for h in range(2)]
        cleared = ph.sem("cleared")
        idxs = ph.sb("idxs", [P, 2, 2, HT], I32)
        g = ph.sb("g", [P, 2, 2, HT, 2 * H])
        with nc.Block() as block:
            @block.gpsimd
            def _(pool):
                with pool.Fori(0, turns) as i:
                    for h in range(2):
                        tiles = bass.ds(i * (2 * HT) + h * HT, HT)
                        pool.wait_ge(used[h], i + 1)
                        nc.gpsimd.tensor_copy(idxs[:, h, 0, :], n.c_src[:, tiles]).then_inc(src_ready[h], 1)
                        nc.gpsimd.tensor_copy(idxs[:, h, 1, :], n.c_dst[:, tiles]).then_inc(dst_ready[h], 1)
                        for side, ready in enumerate((src_ready[h], dst_ready[h])):
                            pool.wait_ge(ready, i + 1)
                            pool.sem_inc(started, 1)
                            for j in range(HT):
                                pool.indirect_dma_start(g[:, h, side, j, :], None, elr_table, bass.IndirectOffsetOnAxis(
                                    ap=idxs[:, h, side, j:j + 1], axis=0)).then_inc(got[h], 16)

            @block.vector
            def _(dve):
                nc.vector.memset(n.ex[:, :], 0.0).then_inc(cleared, 1)
                dve.wait_ge(cleared, 1)
                for h in range(2):
                    dve.sem_inc(used[h], 1)
                with dve.Fori(0, turns) as i:
                    for h in range(2):
                        dve.wait_ge(got[h], i * (32 * HT) + (got0 + 32 * HT))
                        out = n.ex[:, :].rearrange("p (t h) -> p t h", h=H)[:, bass.ds(i * (2 * HT) + h * HT, HT), :]
                        nc.vector.tensor_tensor(out, g[:, h, 0, :, 0:H], g[:, h, 1, :, H:2 * H], ALU.add).then_inc(used[h], 1)


def softmax_phase(nc, n, l):
    with Phase(nc, f"sm{l}") as ph:
        link_sem, leaky_ready, turned, cut = ph.sem("link"), ph.sem("leaky"), ph.sem("turned"), ph.sem("cut")
        ends_ready, ends_turned, carry_ready, carry_turned = ph.sem("ends"), ph.sem("ends_t"), ph.sem("carry"), ph.sem("carry_t")
        grown, back, spare = ph.sem("grown"), ph.sem("back"), ph.sem("spare")
        r = ph.sb("r", [P, H, GE])
        fwd = ph.sb("fwd", [P, GE])
        bwd = ph.sb("bwd", [P, GE])
        ends = ph.sb("ends_v", [P, 2, H])
        runs = ph.sb("runs", [H, 2, GR])
        carry = ph.sb("carry_v", [H, 2, GR])
        carried = ph.sb("carried", [P, 2, H])
        ps = ph.ps("ps", [P, H, TPG, P])
        pb = ph.ps("pb", [P, H, TPG, P])
        x = n.ex[:, :]
        xv = x.rearrange("p (g k h) -> p g k h", k=TPG, h=H)
        with nc.Block() as block:
            @block.vector
            def _(dve):
                v = nc.vector
                link = Link(dve, link_sem)
                v.scalar_tensor_tensor(out=x, in0=x, scalar=0.2, in1=x, op0=ALU.mult, op1=ALU.max).then_inc(leaky_ready, 1)

                def scans(h, first, last):
                    line = ps[:, h, :, :].rearrange("p k e -> p (k e)")
                    link(v.tensor_tensor_scan(fwd[:, :], n.rf[:, :], line, first, ALU.add, ALU.max))
                    link(v.tensor_tensor_scan(bwd[:, ::-1], n.rb[:, ::-1], fwd[:, ::-1], last, ALU.add, ALU.max))
                    return line

                for h in range(H):
                    dve.wait_ge(turned, h + 1)
                    scans(h, -BIG, -BIG)
                    link.mark(v.tensor_copy(ends[:, 0, h:h + 1], bwd[:, 0:1]))
                    link.mark(v.tensor_copy(ends[:, 1, h:h + 1], fwd[:, GE - 1:GE]))
                    link.join()
                v.memset(carry[:, :, :], -BIG).then_inc(ends_ready, 1)
                dve.wait_ge(ends_turned, 1)
                dve.wait_ge(ends_ready, 1)
                link.mark(v.tensor_tensor_scan(runs[:, 0, :], n.seg[:, 1, :], pb[0:H, 0, 1, :], -BIG, ALU.add, ALU.max))
                link.mark(v.tensor_tensor_scan(runs[:, 1, ::-1], n.seg[:, 2, ::-1], pb[0:H, 0, 0, ::-1], -BIG, ALU.add, ALU.max))
                link.join()
                link.mark(v.tensor_tensor(carry[:, 0, 1:GR], runs[:, 0, 0:GR - 1], n.seg[:, 0, 1:GR], ALU.add))
                link.mark(v.tensor_tensor(carry[:, 1, 0:GR - 1], runs[:, 1, 1:GR], n.seg[:, 0, 1:GR], ALU.add))
                link.join()
                v.tensor_copy(runs[:, :, :], carry[:, :, :]).then_inc(carry_ready, 1)
                dve.wait_ge(carry_turned, 1)
                link(v.tensor_copy(carried[:, :, :], pb[:, 1, 0:2, 0:H]))
                for h in range(H):
                    line = scans(h, carried[:, 0, h:h + 1], carried[:, 1, h:h + 1])
                    v.tensor_tensor(r[:, h, :], line, bwd[:, :], ALU.subtract).then_inc(cut, 1)
                    dve.wait_ge(cut, h + 1)
                for h in range(H):
                    dve.wait_ge(back, h + 1)
                    link.mark(v.tensor_copy(xv[:, :, :, h].rearrange("p g k -> p k g"), pb[:, h, :, :]))

            @block.tensor
            def _(pe):
                pe.wait_ge(leaky_ready, 1)
                for h in range(H):
                    for k in range(TPG):
                        t = nc.tensor.transpose(ps[:, h, k, :], xv[:, :, k, h], n.ident[:, :])
                    t.then_inc(turned, 1)
                pe.wait_ge(ends_ready, 1)
                nc.tensor.transpose(pb[0:H, 0, 0, :], ends[:, 0, :], n.ident[:, :])
                nc.tensor.transpose(pb[0:H, 0, 1, :], ends[:, 1, :], n.ident[:, :]).then_inc(ends_turned, 1)
                pe.wait_ge(carry_ready, 1)
                nc.tensor.transpose(pb[:, 1, 0, 0:H], runs[:, 0, :], n.ident[0:H, 0:H])
                nc.tensor.transpose(pb[:, 1, 1, 0:H], runs[:, 1, :], n.ident[0:H, 0:H]).then_inc(carry_turned, 1)
                for h in range(H):
                    pe.wait_ge(grown, h + 1)
                    for k in range(TPG):
                        t = nc.tensor.transpose(pb[:, h, k, :], r[:, h, k * P:(k + 1) * P], n.ident[:, :])
                    t.then_inc(back, 1)

            @block.scalar
            def _(act):
                for h in range(H):
                    act.wait_ge(cut, h + 1)
                    nc.scalar.activation(r[:, h, :], r[:, h, :], ACT.Exp).then_inc(grown, 1)


def fuse_phase(nc, n, l, out):
    with Phase(nc, f"fuse{l}") as ph:
        link_sem, gat_ready, rel_made, rel_ready = ph.sem("link"), ph.sem("gat"), ph.sem("rel_made"), ph.sem("rel")
        fused, hc_ready, gated, sig, h_ready = ph.sem("fused"), ph.sem("hc"), ph.sem("gated"), ph.sem("sig"), ph.sem("h_ready")
        turned, x_ready, stored, bias_ready, rel_read = ph.sem("turned"), ph.sem("x_ready"), ph.sem("stored"), ph.sem("bias"), ph.sem("rel_read")
        gbias = ph.sb("gbias", [P, 1])
        rel = ph.sb("rel", [P, 2, 4 * P])
        hc = ph.sb("hc_v", [P, 2, 4 * P])
        gate = ph.sb("gate", [P, 2, 4 * P])
        ps = ph.ps("ps", [P, 4, 2, 4 * P])
        a0, a1, a2 = (n.acc[:, k, :] for k in range(3))
        gating, last = l == 0, l == LAYERS - 1
        with nc.Block() as block:
            @block.vector
            def _(dve):
                v = nc.vector
                link = Link(dve, link_sem)
                link(v.tensor_tensor(gbias[:, :], n.cols[:, 8:9], n.tw[:, :], ALU.mult))
                v.tensor_tensor(gbias[:, :], gbias[:, :], n.cols[:, 7:8], ALU.add).then_inc(bias_ready, 1)
                for q, c in enumerate(CH):
                    w = c[1] * P
                    link(v.tensor_scalar(chunk(a2, c), chunk(a2, c), 1e-30, None, ALU.max))
                    link(v.reciprocal(chunk(a2, c), chunk(a2, c)))
                    link(v.tensor_tensor(chunk(a1, c), chunk(a1, c), chunk(a2, c), ALU.mult))
                    v.tensor_scalar(chunk(a1, c), chunk(a1, c), n.cols[:, 3 + l:4 + l], None, ALU.add).then_inc(gat_ready, 1)
                    dve.wait_ge(rel_made, q + 1)
                    if q >= 2:
                        dve.wait_ge(fused, q - 1)
                    v.scalar_tensor_tensor(out=rel[:, q % 2, 0:w], in0=ps[:, 0, q % 2, 0:w], scalar=n.cols[:, l:l + 1],
                                           in1=chunk(a0, c), op0=ALU.add, op1=ALU.add).then_inc(rel_ready, 1)
                    if gating:
                        dve.wait_ge(sig, q + 1)
                        link(v.tensor_tensor(gate[:, q % 2, 0:w], gate[:, q % 2, 0:w], hc[:, q % 2, 0:w], ALU.mult))
                        v.tensor_scalar(chunk(n.ht, c), gate[:, q % 2, 0:w], 0.0, None, ALU.max).then_inc(h_ready, 1)
                    if last:
                        dve.wait_ge(turned, q + 1)
                        v.tensor_tensor(chunk3(n.x, c), chunk3(n.x, c), ps[:, 2, q % 2, 0:w].rearrange("p (t d) -> p t d", d=D),
                                        ALU.add).then_inc(x_ready, 1)

            @block.tensor
            def _(pe):
                for q, c in enumerate(CH):
                    w = c[1] * P
                    if q >= 2:
                        pe.wait_ge(rel_ready, q - 1)
                    nc.tensor.matmul(ps[:, 0, q % 2, 0:w], n.wloop[:, l, :], chunk(n.ht, c), start=True, stop=True).then_inc(rel_made, 1)
                    pe.wait_ge(rel_ready, q + 1)
                    pe.wait_ge(gat_ready, q + 1)
                    if q >= 2:
                        pe.wait_ge(hc_ready, q - 1)
                    nc.tensor.matmul(ps[:, 1, q % 2, 0:w], n.wfuse[:, 0, :], rel[:, q % 2, 0:w], start=True, stop=False)
                    nc.tensor.matmul(ps[:, 1, q % 2, 0:w], n.wfuse[:, 1, :], chunk(a1, c), start=False, stop=True).then_inc(fused, 1)
                    pe.wait_ge(hc_ready, q + 1)
                    if gating:
                        if q >= 2:
                            pe.wait_ge(sig, q - 1)
                        nc.tensor.matmul(ps[:, 2, q % 2, 0:w], n.wgate[:, :], hc[:, q % 2, 0:w], start=True, stop=True).then_inc(gated, 1)
                    if last:
                        if q >= 2:
                            pe.wait_ge(x_ready, q - 1)
                        for j in range(c[1]):
                            t = nc.tensor.transpose(ps[:, 2, q % 2, j * P:(j + 1) * P], chunk(n.ht, (c[0] + j, 1)), n.ident[:, :])
                        t.then_inc(turned, 1)

            @block.scalar
            def _(act):
                act.wait_ge(bias_ready, 1)
                for q, c in enumerate(CH):
                    w = c[1] * P
                    act.wait_ge(fused, q + 1)
                    if not gating:
                        nc.scalar.activation(chunk(n.ht, c), ps[:, 1, q % 2, 0:w], ACT.Relu, bias=n.cols[:, 6:7]).then_inc(hc_ready, 1)
                        continue
                    if q >= 2:
                        act.wait_ge(h_ready, q - 1)
                    nc.scalar.activation(hc[:, q % 2, 0:w], ps[:, 1, q % 2, 0:w], ACT.Identity, bias=n.cols[:, 6:7]).then_inc(hc_ready, 1)
                    act.wait_ge(gated, q + 1)
                    nc.scalar.activation(gate[:, q % 2, 0:w], ps[:, 2, q % 2, 0:w], ACT.Sigmoid, bias=gbias[:, 0:1]).then_inc(sig, 1)

            if last:
                @block.sync
                def _(sp):
                    n_dma = 0
                    for q, c in enumerate(CH):
                        sp.wait_ge(x_ready, q + 1)
                        full = min(c[1], max(0, N // P - c[0]))
                        if full:
                            sp.dma_start(rows(out, (c[0], full)), chunk3(n.x, (c[0], full))).then_inc(stored, 16)
                            n_dma += 1
                        if c[0] <= N // P < c[0] + c[1]:
                            sp.dma_start(out[N // P * P:N, :], chunk(n.x, (N // P, 1))[0:N % P, :]).then_inc(stored, 16)
                            n_dma += 1
                    sp.wait_ge(stored, 16 * n_dma)


def bass_gnn_kernel(nc, a, out):
    n = Net()
    h_table = nc.dram_tensor("h_table", (NP, D), F32).ap()
    m_table = nc.dram_tensor("m_table", (NP * R4, HID), F32).ap()
    g_table = nc.dram_tensor("g_table", (NP * R16, 2 * D), F32).ap()
    elr_table = nc.dram_tensor("elr_table", (NP, 2 * H), F32).ap()
    n.got = [nc.alloc_semaphore(f"got{s}", num=FIRST_GATHER_SEM + s) for s in range(RING)]
    n.score_got = [nc.alloc_semaphore(f"score_got{h}", num=FIRST_GATHER_SEM + RING + h) for h in range(2)]
    n.got_count = n.score_count = 0
    with ExitStack() as ctx:
        def sb(name, shape, dt=F32):
            return ctx.enter_context(nc.sbuf_tensor(name, shape, dt))

        n.ident, n.iota, n.ones = sb("ident", [P, P]), sb("iota", [P, P]), sb("ones", [P, P])
        n.eps = sb("eps", [P, 1])
        n.x, n.ht, n.rdeg = sb("x", [P, NP]), sb("ht", [P, NP]), sb("rdeg", [P, NP])
        n.acc = sb("acc", [P, 3, NP])
        n.hn = n.acc[:, 2, :]
        n.c_src, n.c_i4, n.c_i16, n.c_dst = (sb(k, [P, TILES], I32) for k in ("c_src", "c_i4", "c_i16", "c_dst"))
        n.c_dstl, n.c_u, n.ex = sb("c_dstl", [P, TILES]), sb("c_u", [P, TILES]), sb("ex", [P, TILES * H])
        n.rf, n.rb, n.seg = sb("rf", [P, GE]), sb("rb", [P, GE]), sb("seg", [H, 3, GR])
        n.base, n.tw = sb("base", [1, GR], I32), sb("tw", [P, 1])
        n.wagg_t, n.w1, n.w2 = sb("wagg_t", [P, 2, D]), sb("w1", [P, 3, D]), sb("w2", [P, 3, D])
        n.wr1, n.wr2, n.wr3 = sb("wr1", [P, R4, HID]), sb("wr2", [HID, R4, HID]), sb("wr3", [HID, R4, D])
        n.wn1, n.wn2, n.wn3 = sb("wn1", [P, 1 + R4, HID]), sb("wn2", [HID, HID]), sb("wn3", [HID, D])
        n.br1, n.br2, n.br3, n.bn12 = sb("br1", [HID, R4]), sb("br2", [HID, R4]), sb("br3", [P, R4]), sb("bn12", [HID, 2])
        n.wloop, n.wgat, n.wfuse = sb("wloop", [P, LAYERS, D]), sb("wgat", [P, LAYERS, D]), sb("wfuse", [P, 2, D])
        n.wgate, n.cols = sb("wgate", [P, D]), sb("cols", [P, 9])
        n.rowb, n.attn = sb("rowb", [P, 6, D]), sb("attn", [P, LAYERS, 2, D])
        with ExitStack() as rows_ctx:
            n.erow_i = rows_ctx.enter_context(nc.sbuf_tensor("erow_i", [P, 4, GE], I32))
            n.erow_w = rows_ctx.enter_context(nc.sbuf_tensor("erow_w", [P, 2, GE], F32))
            load_phase(nc, n, a)
            edge_phase(nc, n)
        norm_phase(nc, n, "norm0", h_table)
        edge_pass(nc, n, "pass0", h_table, n.c_src, D, "degree")
        mean_layer(nc, n)
        norm_phase(nc, n, "norm1", h_table)
        edge_pass(nc, n, "pass1", h_table, n.c_src, D, "spline")
        spline_layer(nc, n, "conv1", n.w1, 3, h_table)
        edge_pass(nc, n, "pass2", h_table, n.c_src, D, "spline")
        spline_layer(nc, n, "conv2", n.w2, 4, None)
        norm_phase(nc, n, "norm2", h_table)
        message_phase(nc, n, m_table)
        edge_pass(nc, n, "pass3", m_table, n.c_i4, HID, "plain")
        relation_layer(nc, n)
        norm_phase(nc, n, "norm3", h_table)
        for l in range(LAYERS):
            table_phase(nc, n, l, a["L3_gnn_W_rel"], g_table, elr_table)
            score_pass(nc, n, l, elr_table)
            softmax_phase(nc, n, l)
            edge_pass(nc, n, f"att{l}", g_table, n.c_i16, 2 * D, "attend")
            fuse_phase(nc, n, l, out)


_INS = ['x', 'src', 'dst', 'edge_type_16', 'edge_type_4', 'edge_weight', 'edge_weight1',
        'L0_gnn_W_agg', 'L0_gnn_b_agg', 'L0_gnn_gamma', 'L0_gnn_beta',
        'L1_gnn_W1', 'L1_gnn_root1', 'L1_gnn_b1', 'L1_gnn_W2', 'L1_gnn_root2', 'L1_gnn_b2',
        'L2_gnn_Wr1', 'L2_gnn_br1', 'L2_gnn_Wr2', 'L2_gnn_br2', 'L2_gnn_Wr3', 'L2_gnn_br3',
        'L2_gnn_Wn1', 'L2_gnn_bn1', 'L2_gnn_Wn2', 'L2_gnn_bn2', 'L2_gnn_Wn3', 'L2_gnn_bn3',
        'L3_gnn_W_rel', 'L3_gnn_b_rel', 'L3_gnn_W_loop', 'L3_gnn_W_gat', 'L3_gnn_attn_l', 'L3_gnn_attn_r',
        'L3_gnn_b_gat', 'L3_gnn_W_fuse', 'L3_gnn_b_fuse', 'L3_gnn_W_gate', 'L3_gnn_b_gate']


def kernel(**inputs):
    import numpy as _np
    import concourse.bacc as _bacc
    from concourse import mybir as _mybir
    from concourse.bass_utils import run_bass_kernel_spmd as _run

    nc = _bacc.Bacc("TRN2", target_bir_lowering=False, num_devices=1)
    arrays, args = {}, {}
    for name in _INS:
        v = _np.ascontiguousarray(inputs[name])
        arrays[f"in_{name}_dram"] = v
        args[name] = nc.dram_tensor(f"in_{name}_dram", v.shape, _mybir.dt.from_np(v.dtype), kind="ExternalInput").ap()
    out = nc.dram_tensor("out_0_dram", (N, D), F32, kind="ExternalOutput").ap()
    bass_gnn_kernel(nc, args, out)
    r = _run(nc, [arrays], core_ids=[0])
    return r.results[0]["out_0_dram"]
```

```python
from contextlib import ExitStack

import concourse.bass as bass
from concourse import mybir

P = 128
F32 = mybir.dt.float32
I32 = mybir.dt.int32
ALU = mybir.AluOpType
ACT = mybir.ActivationFunctionType
AX_X = mybir.AxisListType.X

N = 3125
D = 128
E = 53125
NT = 26
NP = NT * P
TPG = 4
GE = TPG * P
NG = -(-E // GE)
GR = P
TILES = GR * TPG
WIN = P
RING = 4
TURNS = NG // RING
R4, R16 = 4, 16
H, DH = 4, 32
HID = 64
LAYERS = 3
EPS = 1e-5
BIG = 1.0e30
BF16 = mybir.dt.bfloat16
ROW = 2 * D + H
PARTS = 3
PAD_NODE = 4000
FIRST_SEM = 110
FIRST_GATHER_SEM = 200
CH = [(4 * q, min(4, NT - 4 * q)) for q in range(-(-NT // 4))]
NCH = len(CH)


class Phase:

    def __init__(self, nc, name):
        self.nc, self.name, self.stack = nc, name, ExitStack()
        self.sems = []

    def __enter__(self):
        return self

    def sem(self, name):
        s = self.nc.alloc_semaphore(f"{self.name}_{name}", num=FIRST_SEM + len(self.sems))
        self.sems.append(s)
        return s

    def sb(self, name, shape, dt=F32):
        return self.stack.enter_context(self.nc.sbuf_tensor(f"{self.name}_{name}", shape, dt))

    def ps(self, name, shape, dt=F32):
        return self.stack.enter_context(self.nc.psum_tensor(f"{self.name}_{name}", shape, dt))

    def __exit__(self, *exc):
        if exc[0] is None:
            self.nc.all_engine_barrier(sems_to_clear=range(FIRST_SEM, FIRST_SEM + len(self.sems)))
            for s in self.sems:
                self.nc.release_semaphore(s)
        self.stack.close()


class Link:

    def __init__(self, eng, sem, before=0):
        self.eng, self.sem, self.before, self.n = eng, sem, before, 0

    def mark(self, ins):
        self.n += 1
        ins.then_inc(self.sem, 1)

    def join(self):
        self.eng.wait_ge(self.sem, self.before + self.n)

    def check(self, n):
        assert self.n == n, self.n

    def __call__(self, ins):
        self.mark(ins)
        self.join()


class Net:
    pass


def chunk(t, c):
    return t[:, c[0] * P:(c[0] + c[1]) * P]


def chunk3(t, c):
    return chunk(t, c).rearrange("p (t d) -> p t d", d=D)


def rows(dram, c):
    return dram[c[0] * P:(c[0] + c[1]) * P].rearrange("(t p) d -> p t d", p=P)


def load_phase(nc, n, a):
    with Phase(nc, "load") as ph:
        loaded, zeroed, built, made = ph.sem("loaded"), ph.sem("zeroed"), ph.sem("built"), ph.sem("made")
        turned = ph.sem("turned")
        iota_i = ph.sb("iota_i", [P, P], I32)
        wagg = ph.sb("wagg", [P, 2 * D])
        wt = ph.ps("wt", [P, 3, D])
        full, rest = NG - 1, E - (NG - 1) * GE
        xt, xr = N // P, N % P

        def col(v):
            return v.rearrange("(p o) -> p o", o=1)

        def bcast(v):
            return v.rearrange("(o d) -> o d", o=1).to_broadcast([P, D])

        plain = [
            (wagg[:, :], a["L0_gnn_W_agg"]),
            (n.w1[:, 0:2, :], a["L1_gnn_W1"].rearrange("k c o -> c k o")), (n.w1[:, 2, :], a["L1_gnn_root1"]),
            (n.w2[:, 0:2, :], a["L1_gnn_W2"].rearrange("k c o -> c k o")), (n.w2[:, 2, :], a["L1_gnn_root2"]),
            (n.wr1[:, :, :], a["L2_gnn_Wr1"].rearrange("r c o -> c r o")),
            (n.wr2[:, :, :], a["L2_gnn_Wr2"].rearrange("r c o -> c r o")),
            (n.wr3[:, :, :], a["L2_gnn_Wr3"].rearrange("r c o -> c r o")),
            (n.wn1[:, :, :], a["L2_gnn_Wn1"].rearrange("(k c) o -> c k o", c=D)),
            (n.wn2[:, :], a["L2_gnn_Wn2"]), (n.wn3[:, :], a["L2_gnn_Wn3"]),
            (n.br1[:, :], a["L2_gnn_br1"].rearrange("r h -> h r")),
            (n.br2[:, :], a["L2_gnn_br2"].rearrange("r h -> h r")),
            (n.br3[:, :], a["L2_gnn_br3"].rearrange("r h -> h r")),
            (n.bn12[:, 0:1], col(a["L2_gnn_bn1"])), (n.bn12[:, 1:2], col(a["L2_gnn_bn2"])),
            (n.wloop[:, :, :], a["L3_gnn_W_loop"].rearrange("l c o -> c l o")),
            (n.wgat[:, :, :], a["L3_gnn_W_gat"].rearrange("l c o -> c l o")),
            (n.wfuse[:, :, :], a["L3_gnn_W_fuse"].rearrange("(k c) o -> c k o", c=D)),
            (n.wgate[:, :], a["L3_gnn_W_gate"][0:D, :]),
            (n.cols[:, 0:3], a["L3_gnn_b_rel"].rearrange("l d -> d l")),
            (n.cols[:, 3:6], a["L3_gnn_b_gat"].rearrange("l d -> d l")),
            (n.cols[:, 6:7], col(a["L3_gnn_b_fuse"])), (n.cols[:, 7:8], col(a["L3_gnn_b_gate"])),
            (n.cols[:, 8:9], a["L3_gnn_W_gate"][D:D + 1, :].rearrange("o d -> d o")),
            (n.rowb[:, 0, :], bcast(a["L0_gnn_b_agg"])), (n.rowb[:, 1, :], bcast(a["L0_gnn_gamma"])),
            (n.rowb[:, 2, :], bcast(a["L0_gnn_beta"])), (n.rowb[:, 3, :], bcast(a["L1_gnn_b1"])),
            (n.rowb[:, 4, :], bcast(a["L1_gnn_b2"])), (n.rowb[:, 5, :], bcast(a["L2_gnn_bn3"])),
        ]
        for l in range(LAYERS):
            for side, w in enumerate(("L3_gnn_attn_l", "L3_gnn_attn_r")):
                plain.append((n.attn[:, l, side, :], a[w][l].rearrange("h (d o) -> o (h d)", o=1).to_broadcast([P, D])))
        x3 = n.x[:, :].rearrange("p (t d) -> p t d", d=D)
        after_zero = [
            (x3[:, 0:xt, :], a["x"][0:xt * P].rearrange("(t p) d -> p t d", p=P)),
            (x3[0:xr, xt, :], a["x"][xt * P:N]),
        ]
        for k, name in enumerate(("src", "dst", "edge_type_16", "edge_type_4")):
            after_zero += [
                (n.erow_i[0:full, k, :], a[name][0:full * GE].rearrange("(g e) -> g e", e=GE)),
                (n.erow_i[full:full + 1, k, 0:rest], a[name][full * GE:E].rearrange("(g e) -> g e", g=1)),
            ]
        w0, w1 = a["edge_weight"], a["edge_weight1"].rearrange("e o -> (e o)")
        for k, w in enumerate((w0, w1)):
            after_zero += [
                (n.erow_w[0:full, k, :], w[0:full * GE].rearrange("(g e) -> g e", e=GE)),
                (n.erow_w[full:full + 1, k, 0:rest], w[full * GE:E].rearrange("(g e) -> g e", g=1)),
            ]

        with nc.allow_non_contiguous_dma(reason="bias vectors, one element per partition"), nc.Block() as block:
            @block.sync
            def _(sp):
                sp.wait_ge(zeroed, 4)
                for dst, src in after_zero:
                    sp.dma_start(dst, src).then_inc(loaded, 16)
                sp.wait_ge(loaded, 16 * (len(plain) + len(after_zero)))

            @block.scalar
            def _(act):
                for dst, src in plain:
                    act.dma_start(dst, src).then_inc(loaded, 16)
                act.wait_ge(turned, 1)
                nc.scalar.copy(n.wagg_t[:, :, :], wt[:, 0:2, :]).then_inc(made, 1)
                nc.scalar.copy(n.same_head[:, :], wt[:, 2, :]).then_inc(made, 1)

            @block.vector
            def _(dve):
                nc.vector.memset(n.x[:, :], 0.0).then_inc(zeroed, 1)
                nc.vector.memset(n.erow_i[:, :, :], 0).then_inc(zeroed, 1)
                dve.wait_ge(zeroed, 2)
                nc.vector.memset(n.erow_i[:, 1, :], PAD_NODE).then_inc(zeroed, 1)
                nc.vector.memset(n.erow_w[:, :, :], 0.0).then_inc(zeroed, 1)
                nc.vector.memset(n.ones[:, :], 1.0).then_inc(made, 1)
                nc.vector.memset(n.eps[:, :], EPS).then_inc(made, 1)
                dve.wait_ge(built, 2)
                nc.vector.tensor_copy(n.iota[:, :], iota_i[:, :]).then_inc(made, 1)
                dve.wait_ge(built, 3)
                nc.vector.tensor_copy(n.identb[:, :], n.ident[:, :]).then_inc(made, 1)

            @block.gpsimd
            def _(pool):
                nc.gpsimd.memset(n.ident[:, :], 0.0).then_inc(built, 1)
                nc.gpsimd.iota(iota_i[:, :], pattern=[[1, P]], base=0, channel_multiplier=0).then_inc(built, 1)
                pool.wait_ge(built, 2)
                nc.gpsimd.affine_select(out=n.ident[:, :], in_=n.ident[:, :], compare_op=ALU.not_equal, fill=1.0,
                                        base=0, pattern=[[-1, P]], channel_multiplier=1).then_inc(built, 1)
                nc.gpsimd.memset(n.selh[:, :], 0.0).then_inc(built, 1)
                nc.gpsimd.memset(n.gmask[:, :], 0.0).then_inc(built, 1)
                pool.wait_ge(built, 5)
                sel = n.selh[:, :].rearrange("q (h d) -> q h d", d=DH)
                for k in range(4):
                    nc.gpsimd.affine_select(out=sel, in_=sel, compare_op=ALU.not_equal, fill=1.0, base=-H * k,
                                            pattern=[[-1, H], [0, DH]], channel_multiplier=1).then_inc(built, 1)
                    nc.gpsimd.affine_select(out=n.gmask[:, :], in_=n.gmask[:, :], compare_op=ALU.not_equal, fill=1.0, base=-k,
                                            pattern=[[-H, RING]], channel_multiplier=1).then_inc(built, 1)
                    pool.wait_ge(built, 2 * k + 7)

            @block.tensor
            def _(pe):
                pe.wait_ge(built, 13)
                pe.wait_ge(loaded, 16 * (len(plain) + len(after_zero)))
                for k in range(2):
                    nc.tensor.transpose(wt[:, k, :], wagg[:, k * D:(k + 1) * D], n.ident[:, :])
                nc.tensor.matmul(wt[:, 2, :], n.selh[0:H, :], n.selh[0:H, :], start=True, stop=True).then_inc(turned, 1)


def edge_phase(nc, n, flag_table):
    with Phase(nc, "edge") as ph:
        link_sem, ready, turned, taken = ph.sem("link"), ph.sem("ready"), ph.sem("turned"), ph.sem("taken")
        f = ph.sb("f", [P, 4, GE])
        idx16 = ph.sb("idx16", [P, GE])
        idx4 = ph.sb("idx4", [P, GE])
        dstl = ph.sb("dstl", [P, GE])
        ends = ph.sb("ends", [P, 3, P])
        fl = ph.sb("fl", [P, 2, GR])
        same = ph.sb("same", [P, 2, GR])
        wsum = ph.sb("wsum", [P, 1])
        rf = ph.sb("rf", [P, GE])
        rb = ph.sb("rb", [P, GE])
        stored = ph.sem("stored")
        turn = ph.ps("turn", [P, 5, TPG, P])
        ends_t = ph.ps("ends_t", [P, 4, P])

        fields = [f[:, 0, :], idx4[:, :], idx16[:, :], dstl[:, :], n.erow_w[:, 1, :]]
        cols = [n.c_src, n.c_i4, n.c_i16, n.c_dstl, n.c_u]

        with nc.Block() as block:
            @block.vector
            def _(dve):
                v = nc.vector
                link = Link(dve, link_sem)
                link(v.tensor_copy(f[:, :, :], n.erow_i[:, :, :]))
                link.mark(v.scalar_tensor_tensor(out=idx16[:, :], in0=f[:, 0, :], scalar=float(R16), in1=f[:, 2, :], op0=ALU.mult, op1=ALU.add))
                link.mark(v.scalar_tensor_tensor(out=idx4[:, :], in0=f[:, 0, :], scalar=float(R4), in1=f[:, 3, :], op0=ALU.mult, op1=ALU.add))
                link.mark(v.tensor_copy(ends[:, 0, :], f[:, 1, 0:1].to_broadcast([P, P])))
                link.mark(v.tensor_copy(ends[:, 1, :], f[:, 1, GE - 1:GE].to_broadcast([P, P])))
                link.mark(v.tensor_scalar(ends[:, 2, :], f[:, 1, 0:1].to_broadcast([P, P]), float(NP - WIN), None, ALU.min))
                link.join()
                link.mark(v.tensor_scalar(dstl[:, :], f[:, 1, :], ends[:, 2, 0:1], None, ALU.subtract))
                link.mark(v.memset(rf[:, 0:1], 0.0))
                link.mark(v.memset(rb[:, GE - 1:GE], 0.0))
                link(v.tensor_tensor(rf[:, 1:GE], f[:, 1, 1:GE], f[:, 1, 0:GE - 1], ALU.not_equal))
                link(v.tensor_scalar(rf[:, 1:GE], rf[:, 1:GE], -BIG, None, ALU.mult))
                link.mark(v.tensor_copy(rb[:, 0:GE - 1], rf[:, 1:GE]))
                link.mark(v.reduce_sum(wsum[:, :], n.erow_w[:, 0, :], AX_X))
                link.join()
                v.memset(same[:, :, :], 0.0).then_inc(ready, 1)
                for k, c in enumerate(cols):
                    dve.wait_ge(turned, k + 1)
                    v.tensor_copy(c[:, :].rearrange("p (g k) -> p k g", k=TPG), turn[:, k, :, :]).then_inc(taken, 1)
                dve.wait_ge(turned, 6)
                dve.wait_ge(ready, 1)
                link.mark(v.tensor_copy(n.base[:, :], ends_t[0:1, 2, :]))
                link.mark(v.tensor_scalar(n.tw[:, :], ends_t[:, 3, 0:1], 1.0 / E, None, ALU.mult))
                link(v.tensor_copy(fl[:, :, :], ends_t[:, 0:2, :]))
                link.mark(v.tensor_tensor(same[:, 0, 1:GR], fl[:, 0, 1:GR], fl[:, 1, 0:GR - 1], ALU.is_equal))
                link.mark(v.tensor_tensor(same[:, 1, :], fl[:, 0, :], fl[:, 1, :], ALU.is_equal))
                link.mark(v.memset(n.seg[:, :, :], 0.0))
                link.join()
                link.mark(v.tensor_copy(n.seg[:, 0, :], same[:, 0, :]))
                link.mark(v.tensor_tensor(n.seg[:, 1, :], same[:, 0, :], same[:, 1, :], ALU.mult))
                link.join()
                link(v.tensor_scalar(n.seg[:, :, :], n.seg[:, :, :], -1.0, BIG, ALU.add, ALU.mult))

            @block.sync
            def _(sp):
                sp.wait_ge(ready, 1)
                out = flag_table.rearrange("(g h) e -> h g e", h=H)
                for h in range(H):
                    sp.dma_start(out[h, :, 0:GE], rf[:, :]).then_inc(stored, 16)
                    sp.dma_start(out[h, :, GE:2 * GE], rb[:, :]).then_inc(stored, 16)
                sp.wait_ge(stored, 16 * 2 * H)

            @block.tensor
            def _(pe):
                pe.wait_ge(ready, 1)
                for k, r in enumerate(fields):
                    for j in range(TPG):
                        t = nc.tensor.transpose(turn[:, k, j, :], r[:, j * P:(j + 1) * P], n.ident[:, :])
                    t.then_inc(turned, 1)
                nc.tensor.transpose(ends_t[:, 0, :], ends[:, 0, :], n.ident[:, :])
                nc.tensor.transpose(ends_t[:, 1, :], ends[:, 1, :], n.ident[:, :])
                nc.tensor.transpose(ends_t[:, 2, :], ends[:, 2, :], n.ident[:, :])
                nc.tensor.matmul(ends_t[:, 3, 0:1], n.ones[:, :], wsum[:, :], start=True, stop=True).then_inc(turned, 1)


def norm_steps(nc, ph, link, dve, src, cen, sum_, sq, root, var_ready, root_ready):
    v = nc.vector
    for c in CH:
        link.mark(v.reduce_sum(sum_[:, 0, c[0]:c[0] + c[1]], chunk3(src, c), AX_X))
    link.join()
    link(v.tensor_scalar(sum_[:, 1, :], sum_[:, 0, :], 1.0 / D, None, ALU.mult))
    for i, c in enumerate(CH):
        t = slice(c[0], c[0] + c[1])
        mean = sum_[:, 1, t].unsqueeze(2).to_broadcast([P, c[1], D])
        link(v.tensor_tensor(chunk3(cen, c), chunk3(src, c), mean, ALU.subtract))
        link(v.tensor_tensor(sq[:, 0:c[1], :], chunk3(cen, c), chunk3(cen, c), ALU.mult))
        link(v.reduce_sum(sum_[:, 2, t], sq[:, 0:c[1], :], AX_X))
    v.tensor_scalar(sum_[:, 3, :], sum_[:, 2, :], 1.0 / D, EPS, ALU.mult, ALU.add).then_inc(var_ready, 1)
    dve.wait_ge(root_ready, 1)
    link(v.reciprocal(root[:, 1, :], root[:, 0, :]))


def norm_root(nc, act, sum_, root, var_ready, root_ready):
    act.wait_ge(var_ready, 1)
    nc.scalar.activation(root[:, 0, :], sum_[:, 3, :], ACT.Sqrt).then_inc(root_ready, 1)


def turn_and_store(nc, block, n, src, table, src_ready, turned, stored, ps):
    @block.tensor
    def _(pe):
        for q, c in enumerate(CH):
            pe.wait_ge(src_ready, q + 1)
            for j in range(c[1]):
                t = nc.tensor.transpose(ps[:, q, j, :], chunk(src, (c[0] + j, 1)), n.ident[:, :])
            t.then_inc(turned, 1)

    @block.sync
    def _(sp):
        for q, c in enumerate(CH):
            sp.wait_ge(src_ready, q + 1)
            sp.dma_start(rows(table, c), chunk3(src, c)).then_inc(stored, 16)
        sp.wait_ge(stored, 16 * NCH)


def norm_phase(nc, n, name, table):
    with Phase(nc, name) as ph:
        link_sem, var_ready, root_ready = ph.sem("link"), ph.sem("var"), ph.sem("root")
        h_ready, turned, stored = ph.sem("h_ready"), ph.sem("turned"), ph.sem("stored")
        sum_, root, sq = ph.sb("sum", [P, 4, NT]), ph.sb("rootv", [P, 2, NT]), ph.sb("sq", [P, 4, D])
        ps = ph.ps("ps", [P, NCH, 4, P])
        with nc.Block() as block:
            @block.vector
            def _(dve):
                link = Link(dve, link_sem)
                norm_steps(nc, ph, link, dve, n.x, n.hn, sum_, sq, root, var_ready, root_ready)
                for c in CH:
                    rstd = root[:, 1, c[0]:c[0] + c[1]].unsqueeze(2).to_broadcast([P, c[1], D])
                    nc.vector.scalar_tensor_tensor(out=chunk3(n.hn, c), in0=chunk3(n.hn, c), scalar=0.0, in1=rstd,
                                                   op0=ALU.max, op1=ALU.mult).then_inc(h_ready, 1)

            @block.scalar
            def _(act):
                norm_root(nc, act, sum_, root, var_ready, root_ready)
                for q, c in enumerate(CH):
                    act.wait_ge(turned, q + 1)
                    nc.scalar.copy(chunk3(n.ht, c), ps[:, q, 0:c[1], :])

            turn_and_store(nc, block, n, n.hn, table, h_ready, turned, stored, ps)


def edge_pass(nc, n, name, table, idx, width, mode):
    regions = {"degree": 2, "spline": 2, "plain": 1}[mode]
    feats = min(width, D)
    with Phase(nc, name) as ph:
        idx_ready = [ph.sem(f"idx_ready{h}") for h in range(2)]
        got, got0 = n.got, n.got_count
        n.got_count += TURNS * 16 * TPG
        hot = [ph.sem(f"hot{s}") for s in range(RING)]
        used = [ph.sem(f"used{s}") for s in range(RING)]
        added = ph.sem("added")
        cleared, link_sem = ph.sem("cleared"), ph.sem("link")
        idxs = ph.sb("idxs", [P, 2, 2 * TPG], I32)
        g = ph.sb("g", [P, RING, TPG, width])
        oh = ph.sb("oh", [P, RING, TPG, WIN])
        ps = ph.ps("ps", [P, RING, 4 * P])
        if mode == "spline":
            ohw = ph.sb("ohw", [P, RING, TPG, 2, WIN])
        def build_ops():
            return 3 if mode == "spline" else 1

        with nc.Block() as block:
            @block.gpsimd
            def _(pool):
                with pool.Fori(1, TURNS + 1) as turn:
                    for s in range(RING):
                        half, j0 = s // 2, (s % 2) * TPG
                        if s % 2 == 0:
                            pool.wait_ge(used[s], turn)
                            pool.wait_ge(used[s + 1], turn)
                            nc.gpsimd.tensor_copy(idxs[:, half, :], idx[:, bass.ds(turn * (RING * TPG) + (s - RING) * TPG, 2 * TPG)]).then_inc(idx_ready[half], 1)
                            pool.wait_ge(cleared, 1)
                            pool.wait_ge(idx_ready[half], turn)
                        for j in range(TPG):
                            pool.indirect_dma_start(g[:, s, j, :], None, table, bass.IndirectOffsetOnAxis(
                                ap=idxs[:, half, j0 + j:j0 + j + 1], axis=0)).then_inc(got[s], 16)

            @block.tensor
            def _(pe):
                for s in range(RING):
                    pe.sem_inc(used[s], 1)
                with pe.Fori(0, TURNS) as i:
                    for s in range(RING):
                        pe.wait_ge(got[s], i * (16 * TPG) + (got0 + 16 * TPG))
                        pe.wait_ge(hot[s], i * build_ops() + build_ops())
                        pe.wait_ge(added, i * RING + (s + 1))
                        for j in range(TPG):
                            first, last = j == 0, j == TPG - 1
                            if mode == "spline":
                                mm = nc.tensor.matmul(ps[:, s, 0:2 * WIN], g[:, s, j, :], ohw[:, s, j, :, :].rearrange("p a w -> p (a w)"),
                                                      start=first, stop=last)
                                continue
                            left = [g[:, s, j, 0:feats]]
                            if mode == "degree":
                                left.append(n.ones[:, :])
                            for r, lt in enumerate(left):
                                mm = nc.tensor.matmul(ps[0:feats, s, r * WIN:(r + 1) * WIN], lt, oh[:, s, j, :],
                                                      start=first and r == 0, stop=last, skip_group_check=True)
                        mm.then_inc(used[s], 1)

            @block.vector
            def _(dve):
                v = nc.vector
                v.memset(n.acc[:, 0:regions, :], 0.0).then_inc(cleared, 1)
                dve.wait_ge(cleared, 1)
                dve.sem_inc(added, RING)
                iota = n.iota[:, :].unsqueeze(1).to_broadcast([P, TPG, WIN])
                with dve.Fori(0, TURNS) as i:
                    def build(s):
                        tiles = bass.ds(i * (RING * TPG) + s * TPG, TPG)
                        dstl = n.c_dstl[:, tiles].unsqueeze(2).to_broadcast([P, TPG, WIN])
                        dve.wait_ge(used[s], i + 1)
                        v.tensor_tensor(oh[:, s, :, :], iota, dstl, ALU.is_equal).then_inc(hot[s], 1)
                        if mode == "spline":
                            u = n.c_u[:, tiles].unsqueeze(2).to_broadcast([P, TPG, WIN])
                            dve.wait_ge(hot[s], i * 3 + 1)
                            v.tensor_tensor(ohw[:, s, :, 1, :], oh[:, s, :, :], u, ALU.mult).then_inc(hot[s], 1)
                            dve.wait_ge(hot[s], i * 3 + 2)
                            v.tensor_tensor(ohw[:, s, :, 0, :], oh[:, s, :, :], ohw[:, s, :, 1, :], ALU.subtract).then_inc(hot[s], 1)

                    def add(s):
                        base = nc.vector.value_load(n.base[0:1, bass.ds(i * RING + s, 1)], min_val=0, max_val=NP - WIN)
                        dve.wait_ge(used[s], i + 2)
                        dve.wait_ge(added, i * RING + (RING + s))
                        out = n.acc[0:feats, 0:regions, bass.ds(base, WIN)]
                        v.tensor_tensor(out, out, ps[0:feats, s, 0:regions * WIN].rearrange("p (r w) -> p r w", w=WIN),
                                        ALU.add).then_inc(added, 1)

                    for s in range(RING):
                        build(s)
                        if s:
                            add(s - 1)
                    add(RING - 1)


def mean_layer(nc, n):
    with Phase(nc, "mean") as ph:
        link_sem, var_ready, root_ready = ph.sem("link"), ph.sem("var"), ph.sem("root")
        agg_ready, mixed = ph.sem("agg_ready"), ph.sem("mixed")
        sum_, root, sq = ph.sb("sum", [P, 4, NT]), ph.sb("rootv", [P, 2, NT]), ph.sb("sq", [P, 4, D])
        ps = ph.ps("ps", [P, NCH, 4, P])
        agg, y = n.acc[:, 0, :], n.acc[:, 1, :]
        with nc.Block() as block:
            @block.vector
            def _(dve):
                v = nc.vector
                link = Link(dve, link_sem)
                for c in CH:
                    link(v.tensor_scalar(chunk(n.rdeg, c), chunk(y, c), 1.0, None, ALU.max))
                    link(v.reciprocal(chunk(n.rdeg, c), chunk(n.rdeg, c)))
                    v.tensor_tensor(chunk(agg, c), chunk(agg, c), chunk(n.rdeg, c), ALU.mult).then_inc(agg_ready, 1)
                for q, c in enumerate(CH):
                    dve.wait_ge(mixed, q + 1)
                    b = n.rowb[:, 0, :].unsqueeze(1).to_broadcast([P, c[1], D])
                    link(v.tensor_tensor(chunk3(y, c), ps[:, q, 0:c[1], :], b, ALU.add))
                    link(v.tensor_tensor(chunk3(y, c), chunk3(y, c), chunk3(n.hn, c), ALU.add))
                norm_steps(nc, ph, link, dve, y, y, sum_, sq, root, var_ready, root_ready)
                for c in CH:
                    rstd = root[:, 1, c[0]:c[0] + c[1]].unsqueeze(2).to_broadcast([P, c[1], D])
                    gamma = n.rowb[:, 1, :].unsqueeze(1).to_broadcast([P, c[1], D])
                    beta = n.rowb[:, 2, :].unsqueeze(1).to_broadcast([P, c[1], D])
                    link(v.tensor_tensor(chunk3(y, c), chunk3(y, c), rstd, ALU.mult))
                    link(v.tensor_tensor(chunk3(y, c), chunk3(y, c), gamma, ALU.mult))
                    link(v.tensor_tensor(chunk3(y, c), chunk3(y, c), beta, ALU.add))
                    link(v.scalar_tensor_tensor(out=chunk3(n.x, c), in0=chunk3(y, c), scalar=0.0, in1=chunk3(n.x, c),
                                                op0=ALU.max, op1=ALU.add))

            @block.scalar
            def _(act):
                norm_root(nc, act, sum_, root, var_ready, root_ready)

            @block.tensor
            def _(pe):
                for q, c in enumerate(CH):
                    pe.wait_ge(agg_ready, q + 1)
                    for j in range(c[1]):
                        t = (c[0] + j, 1)
                        nc.tensor.matmul(ps[:, q, j, :], chunk(n.ht, t), n.wagg_t[:, 0, :], start=True, stop=False)
                        mm = nc.tensor.matmul(ps[:, q, j, :], chunk(agg, t), n.wagg_t[:, 1, :], start=False, stop=True)
                    mm.then_inc(mixed, 1)


def spline_layer(nc, n, name, w, bias_row, table):
    with Phase(nc, name) as ph:
        link_sem, agg_ready, mixed = ph.sem("link"), ph.sem("agg_ready"), ph.sem("mixed")
        out_ready, turned, stored = ph.sem("out_ready"), ph.sem("turned"), ph.sem("stored")
        ps = ph.ps("ps", [P, NCH, 4, P])
        a0, a1 = n.acc[:, 0, :], n.acc[:, 1, :]
        with nc.Block() as block:
            @block.vector
            def _(dve):
                v = nc.vector
                link = Link(dve, link_sem)
                for c in CH:
                    v.tensor_tensor(chunk(a0, c), chunk(a0, c), chunk(n.rdeg, c), ALU.mult).then_inc(agg_ready, 1)
                    v.tensor_tensor(chunk(a1, c), chunk(a1, c), chunk(n.rdeg, c), ALU.mult).then_inc(agg_ready, 1)
                for q, c in enumerate(CH):
                    dve.wait_ge(mixed, q + 1)
                    b = n.rowb[:, bias_row, :].unsqueeze(1).to_broadcast([P, c[1], D])
                    ins = v.tensor_tensor(chunk3(n.hn, c), ps[:, q, 0:c[1], :], b, ALU.add)
                    if table is not None:
                        ins.then_inc(out_ready, 1)
                        continue
                    link(ins)
                    link(v.tensor_tensor(chunk3(n.x, c), chunk3(n.x, c), chunk3(n.hn, c), ALU.add))

            @block.tensor
            def _(pe):
                for q, c in enumerate(CH):
                    pe.wait_ge(agg_ready, 2 * q + 2)
                    for j in range(c[1]):
                        t = (c[0] + j, 1)
                        nc.tensor.matmul(ps[:, q, j, :], chunk(a0, t), w[:, 0, :], start=True, stop=False)
                        nc.tensor.matmul(ps[:, q, j, :], chunk(a1, t), w[:, 1, :], start=False, stop=False)
                        mm = nc.tensor.matmul(ps[:, q, j, :], chunk(n.ht, t), w[:, 2, :], start=False, stop=True)
                    mm.then_inc(mixed, 1)
                if table is not None:
                    for q, c in enumerate(CH):
                        pe.wait_ge(out_ready, q + 1)
                        for j in range(c[1]):
                            t = nc.tensor.transpose(ps[:, q, j, :], chunk(n.hn, (c[0] + j, 1)), n.ident[:, :])
                        t.then_inc(turned, 1)

            if table is not None:
                @block.scalar
                def _(act):
                    for q, c in enumerate(CH):
                        act.wait_ge(turned, q + 1)
                        nc.scalar.copy(chunk3(n.ht, c), ps[:, q, 0:c[1], :])

                @block.sync
                def _(sp):
                    for q, c in enumerate(CH):
                        sp.wait_ge(out_ready, q + 1)
                        sp.dma_start(rows(table, c), chunk3(n.hn, c)).then_inc(stored, 16)
                    sp.wait_ge(stored, 16 * NCH)


def message_phase(nc, n, table):
    with Phase(nc, "msg") as ph:
        made = [ph.sem(f"made{k}") for k in range(4)]
        kept = [ph.sem(f"kept{k}") for k in range(4)]
        stored = ph.sem("stored")
        a1 = ph.sb("a1", [HID, R4, 4 * P])
        a2 = ph.sb("a2", [HID, R4, 4 * P])
        a3 = ph.sb("a3", [P, R4, 4 * P])
        ps = ph.ps("ps", [P, 8, 4 * P])
        m = n.acc[:, 0:2, :].rearrange("p a (t o) -> p (a t o)", o=2 * D).rearrange("p (t r o) -> p t r o", r=R4, o=HID)
        with nc.Block() as block:
            @block.tensor
            def _(pe):
                for q, c in enumerate(CH):
                    w = c[1] * P
                    for r in range(R4):
                        if q:
                            pe.wait_ge(kept[2], R4 * (q - 1) + r + 1)
                        nc.tensor.matmul(ps[0:HID, r, 0:w], n.wr1[:, r, :], chunk(n.ht, c), start=True, stop=True).then_inc(made[0], 1)
                    for r in range(R4):
                        pe.wait_ge(kept[0], R4 * q + r + 1)
                        if q:
                            pe.wait_ge(kept[3], R4 * (q - 1) + r + 1)
                        nc.tensor.matmul(ps[0:HID, R4 + r, 0:w], n.wr2[:, r, :], a1[:, r, 0:w], start=True, stop=True).then_inc(made[1], 1)
                    for r in range(R4):
                        pe.wait_ge(kept[1], R4 * q + r + 1)
                        nc.tensor.matmul(ps[:, r, 0:w], n.wr3[:, r, :], a2[:, r, 0:w], start=True, stop=True).then_inc(made[2], 1)
                    for r in range(R4):
                        pe.wait_ge(kept[2], R4 * q + r + 1)
                        for j in range(c[1]):
                            mm = nc.tensor.matmul(ps[:, R4 + r, j * HID:(j + 1) * HID], a3[:, r, j * P:(j + 1) * P],
                                                  n.wn1[:, 1 + r, :], start=True, stop=True)
                        mm.then_inc(made[3], 1)

            @block.scalar
            def _(act):
                stages = ((a1, n.br1, HID, 0), (a2, n.br2, HID, R4), (a3, n.br3, P, 0))
                for q, c in enumerate(CH):
                    w = c[1] * P
                    for k, (out, bias, rows_, bank) in enumerate(stages):
                        for r in range(R4):
                            act.wait_ge(made[k], R4 * q + r + 1)
                            if q:
                                act.wait_ge(made[k + 1], R4 * (q - 1) + r + 1)
                            nc.scalar.activation(out[:, r, 0:w], ps[0:rows_, bank + r, 0:w], ACT.Relu,
                                                 bias=bias[:, r:r + 1]).then_inc(kept[k], 1)

            @block.vector
            def _(dve):
                for q, c in enumerate(CH):
                    for r in range(R4):
                        dve.wait_ge(made[3], R4 * q + r + 1)
                        nc.vector.tensor_copy(m[:, c[0]:c[0] + c[1], r, :],
                                              ps[:, R4 + r, 0:c[1] * HID].rearrange("p (t o) -> p t o", o=HID)).then_inc(kept[3], 1)

            @block.sync
            def _(sp):
                out = table.rearrange("(t p r) o -> p t (r o)", p=P, r=R4)
                for q, c in enumerate(CH):
                    sp.wait_ge(kept[3], R4 * (q + 1))
                    sp.dma_start(out[:, c[0]:c[0] + c[1], :], m[:, c[0]:c[0] + c[1], :, :].rearrange("p t r o -> p t (r o)")).then_inc(stored, 16)
                sp.wait_ge(stored, 16 * NCH)


def relation_layer(nc, n):
    with Phase(nc, "rel") as ph:
        made = [ph.sem(f"made{k}") for k in range(3)]
        summed, kept, link_sem, out_read = ph.sem("summed"), [ph.sem("kept0"), ph.sem("kept1")], ph.sem("link"), ph.sem("out_read")
        t0 = ph.sb("t0", [HID, 2, 4 * P])
        q1 = ph.sb("q1", [HID, 2, 4 * P])
        q2 = ph.sb("q2", [HID, 2, 4 * P])
        out = ph.sb("out", [P, 4, D])
        ps = ph.ps("ps", [P, 3, 2, 4 * P])
        with nc.Block() as block:
            @block.tensor
            def _(pe):
                def first(q):
                    if q >= 2:
                        pe.wait_ge(summed, q - 1)
                    nc.tensor.matmul(ps[0:HID, 0, q % 2, 0:CH[q][1] * P], n.wn1[:, 0, :], chunk(n.ht, CH[q]), start=True, stop=True).then_inc(made[0], 1)

                first(0)
                for q, c in enumerate(CH):
                    w = c[1] * P
                    if q + 1 < NCH:
                        first(q + 1)
                    pe.wait_ge(kept[0], q + 1)
                    if q >= 2:
                        pe.wait_ge(kept[1], q - 1)
                    nc.tensor.matmul(ps[0:HID, 1, q % 2, 0:w], n.wn2[:, :], q1[:, q % 2, 0:w], start=True, stop=True).then_inc(made[1], 1)
                    pe.wait_ge(kept[1], q + 1)
                    if q >= 2:
                        pe.wait_ge(out_read, q - 1)
                    for j in range(c[1]):
                        mm = nc.tensor.matmul(ps[:, 2, q % 2, j * D:(j + 1) * D], q2[:, q % 2, j * P:(j + 1) * P], n.wn3[:, :],
                                              start=True, stop=True)
                    mm.then_inc(made[2], 1)

            @block.scalar
            def _(act):
                for q, c in enumerate(CH):
                    w = c[1] * P
                    act.wait_ge(summed, q + 1)
                    if q >= 2:
                        act.wait_ge(made[1], q - 1)
                    nc.scalar.activation(q1[:, q % 2, 0:w], t0[:, q % 2, 0:w], ACT.Relu, bias=n.bn12[:, 0:1]).then_inc(kept[0], 1)
                    act.wait_ge(made[1], q + 1)
                    if q >= 2:
                        act.wait_ge(made[2], q - 1)
                    nc.scalar.activation(q2[:, q % 2, 0:w], ps[0:HID, 1, q % 2, 0:w], ACT.Relu, bias=n.bn12[:, 1:2]).then_inc(kept[1], 1)

            @block.vector
            def _(dve):
                v = nc.vector
                link = Link(dve, link_sem)

                def add_sums(q):
                    w = CH[q][1] * P
                    dve.wait_ge(made[0], q + 1)
                    if q >= 2:
                        dve.wait_ge(kept[0], q - 1)
                    v.tensor_tensor(t0[:, q % 2, 0:w], ps[0:HID, 0, q % 2, 0:w], chunk(n.acc[0:HID, 0, :], CH[q]), ALU.add).then_inc(summed, 1)

                add_sums(0)
                for q, c in enumerate(CH):
                    if q + 1 < NCH:
                        add_sums(q + 1)
                    dve.wait_ge(made[2], q + 1)
                    b = n.rowb[:, 5, :].unsqueeze(1).to_broadcast([P, c[1], D])
                    v.tensor_tensor(out[:, 0:c[1], :], ps[:, 2, q % 2, 0:c[1] * D].rearrange("p (t d) -> p t d", d=D), b, ALU.add).then_inc(out_read, 1)
                    dve.wait_ge(out_read, q + 1)
                    link(v.tensor_tensor(chunk3(n.x, c), chunk3(n.x, c), out[:, 0:c[1], :], ALU.add))


def table_phase(nc, n, l, w_rel, table, er_table):
    with Phase(nc, f"tab{l}") as ph:
        loaded, link_sem = ph.sem("loaded"), ph.sem("link")
        made = ph.sem("made")
        took_a, took_b, took_z = ph.sem("took_a"), ph.sem("took_b"), ph.sem("took_z")
        stored_h = [ph.sem(f"stored_h{k}") for k in range(2)]
        stored_z = [ph.sem(f"stored_z{k}") for k in range(2)]
        scores, stored_e = ph.sem("scores"), ph.sem("stored_e")
        wrel = ph.sb("wrel", [P, R16, D])
        st = ph.sb("st", [P, 2, R16 * D])
        zst = ph.sb("zst", [P, 2, D + H])
        prod = ph.sb("prod", [P, 2, D])
        elr = ph.sb("elr", [P, NT, 2 * H])
        rest = ph.sb("rest", [P, NT, H])
        parts = ph.sb("parts", [P, NT, H, PARTS], BF16)
        ps = ph.ps("ps", [P, 3, 1024])
        psz = ph.ps("psz", [P, 2, 512])
        tab = table.rearrange("(t p r) c -> t p r c", p=P, r=R16)
        with nc.Block() as block:
            @block.tensor
            def _(pe):
                pe.wait_ge(loaded, 16)
                for t in range(NT):
                    for half in range(2):
                        u = 2 * t + half
                        if u >= 3:
                            if (u - 3) % 2 == 0:
                                pe.wait_ge(took_a, (u - 3) // 2 + 1)
                            else:
                                pe.wait_ge(took_b, (u - 3) // 2 + 1)
                        for b in range(2):
                            r0 = half * 8 + b * 4
                            mm = nc.tensor.matmul(ps[:, u % 3, b * 512:(b + 1) * 512], chunk(n.ht, (t, 1)),
                                                  wrel[:, r0:r0 + 4, :].rearrange("p r o -> p (r o)"), start=True, stop=True)
                        mm.then_inc(made, 1)
                    if t >= 2:
                        pe.wait_ge(scores, t - 1)
                    nc.tensor.matmul(psz[:, t % 2, 0:D], chunk(n.ht, (t, 1)), n.wgat[:, l, :], start=True, stop=True).then_inc(made, 1)

            @block.scalar
            def _(act):
                for t in range(NT):
                    act.wait_ge(made, 3 * t + 1)
                    if t >= 2:
                        act.wait_ge(stored_h[t % 2], 16 * (t // 2))
                    nc.scalar.copy(st[:, t % 2, 0:1024], ps[:, (2 * t) % 3, :]).then_inc(took_a, 1)
                    act.wait_ge(took_z, 2 * t + 2)
                    act.dma_start(tab[t, :, :, D:ROW], zst[:, t % 2, :].unsqueeze(1).to_broadcast([P, R16, ROW - D])).then_inc(stored_z[t % 2], 16)
                for k in range(2):
                    act.wait_ge(stored_z[k], 16 * (NT // 2))

            @block.vector
            def _(dve):
                v = nc.vector
                link = Link(dve, link_sem)
                for t in range(NT):
                    dve.wait_ge(made, 3 * t + 2)
                    if t >= 2:
                        dve.wait_ge(stored_h[t % 2], 16 * (t // 2))
                    v.tensor_copy(st[:, t % 2, 1024:2048], ps[:, (2 * t + 1) % 3, :]).then_inc(took_b, 1)
                    dve.wait_ge(made, 3 * t + 3)
                    if t >= 2:
                        dve.wait_ge(stored_z[t % 2], 16 * (t // 2))
                    v.tensor_copy(zst[:, t % 2, 0:D], psz[:, t % 2, 0:D]).then_inc(took_z, 1)
                    link(v.tensor_tensor(prod[:, :, :], psz[:, t % 2, 0:D].unsqueeze(1).to_broadcast([P, 2, D]), n.attn[:, l, :, :], ALU.mult))
                    v.reduce_sum(elr[:, t, :], prod[:, :, :].rearrange("p s (h d) -> p (s h) d", d=DH), AX_X).then_inc(scores, 1)
                    dve.wait_ge(scores, t + 1)
                    v.tensor_copy(zst[:, t % 2, D:D + H], elr[:, t, 0:H]).then_inc(took_z, 1)
                link(v.tensor_copy(parts[:, :, :, 0], elr[:, :, H:2 * H]))
                link(v.tensor_tensor(rest[:, :, :], elr[:, :, H:2 * H], parts[:, :, :, 0], ALU.subtract))
                link(v.tensor_copy(parts[:, :, :, 1], rest[:, :, :]))
                link(v.tensor_tensor(rest[:, :, :], rest[:, :, :], parts[:, :, :, 1], ALU.subtract))
                v.tensor_copy(parts[:, :, :, 2], rest[:, :, :]).then_inc(scores, 1)

            @block.sync
            def _(sp):
                sp.dma_start(wrel[:, :, :], w_rel[l].rearrange("r c o -> c r o")).then_inc(loaded, 16)
                for t in range(NT):
                    sp.wait_ge(took_a, t + 1)
                    sp.wait_ge(took_b, t + 1)
                    sp.dma_start(tab[t, :, :, 0:D], st[:, t % 2, :].rearrange("p (r o) -> p r o", o=D)).then_inc(stored_h[t % 2], 16)
                sp.wait_ge(scores, NT + 1)
                sp.dma_start(er_table.rearrange("(t p) c -> p t c", p=P), parts[:, :, :, :].rearrange("p t h k -> p t (h k)")).then_inc(stored_e, 16)
                sp.wait_ge(stored_e, 16)
                for k in range(2):
                    sp.wait_ge(stored_h[k], 16 * (NT // 2))


def attend_pass(nc, n, l, table, er_table, flag_table):
    turns = NG // RING
    KC, KA = 12, 2
    with Phase(nc, f"att{l}") as ph:
        got, got0 = n.att_got, n.att_count
        n.att_count += (turns // 2) * 16 * TPG
        landed = [ph.sem(f"landed{p}") for p in range(2)]
        idx_ready = [ph.sem(f"idx_ready{p}") for p in range(2)]
        used = [ph.sem(f"used{k}") for k in range(2 * RING)]
        hot = [ph.sem(f"hot{p}") for p in range(2)]
        er_in = [ph.sem(f"er_in{k}") for k in range(2 * RING)]
        flags_in = [ph.sem(f"flags_in{p}") for p in range(2)]
        half_hot, hot_turned, hot_t = ph.sem("half_hot"), ph.sem("hot_turned"), ph.sem("hot_t")
        er_done, x_ready, x_turned, cut = ph.sem("er_done"), ph.sem("x_ready"), ph.sem("x_turned"), ph.sem("cut")
        ends_ready, grown, back, spread = ph.sem("ends_ready"), ph.sem("grown"), ph.sem("back"), ph.sem("spread")
        parted = ph.sem("parted")
        gap, fac_ready, scaled, added = ph.sem("gap"), ph.sem("fac_ready"), ph.sem("scaled"), ph.sem("added")
        cleared, link_c, link_a = ph.sem("cleared"), ph.sem("link_c"), ph.sem("link_a")

        idxs = ph.sb("idxs", [P, 2, RING * TPG], I32)
        g = ph.sb("g", [P, 2 * RING, TPG, ROW])
        oh = ph.sb("oh", [P, 2 * RING, TPG, WIN])
        ohb = ph.sb("ohb", [P, 2 * RING, TPG, WIN], BF16)
        oht = ph.sb("oht", [P, RING, TPG, P], BF16)
        erw = ph.sb("erw", [P, 2 * RING, H * PARTS], BF16)
        flags = ph.sb("flags", [RING * H, 2, 2, GE])
        er = ph.sb("er", [P, RING * TPG, H])
        x = ph.sb("x_v", [P, TPG, RING, H])
        fwd = ph.sb("fwd", [RING * H, GE])
        bwd = ph.sb("bwd", [RING * H, GE])
        ex = ph.sb("ex_v", [RING * H, GE])
        ends = ph.sb("ends_v", [RING * H, 2, RING])
        run = ph.sb("run", [P, RING + 1])
        cin = ph.sb("cin", [P, RING])
        top = ph.sb("top", [P, RING])
        diff = ph.sb("diff", [P, 2, 2, RING])
        fac = ph.sb("fac", [P, 2, 2, RING])
        exc = ph.sb("exc", [P, TPG, RING, H])
        exr = ph.sb("exr", [P, RING, TPG, H])
        exd = ph.sb("exd", [P, RING, TPG, H, DH], BF16)
        zs = ph.sb("zs", [P, RING, TPG, D])
        ps = ph.ps("ps", [P, RING, 4 * P])
        ps_two = ph.ps("ps_two", [P, 2, 512])
        ps_x = ph.ps("ps_x", [P, GE])
        ps_w = ph.ps("ps_w", [P, 512])
        ps_t = [ps_two[:, k, 0:TPG * P // 2].bitcast(BF16).rearrange("p (t e) -> p t e", e=P) for k in range(2)]
        er_ps = ps_two[:, 1, 256:256 + RING * TPG * H * PARTS]
        ex_ps = ps_w[:, 0:TPG * RING * H].rearrange("p (k g h) -> p k g h", k=TPG, h=H)
        end_ps = ps_x[:, 0:2 * RING]

        def after(i, p):
            return (i, 1) if p == 0 else (i + 1, 0)

        def steps(eng, step, finish):
            step(0, 0, True, False)
            with eng.Fori(0, turns // 2 - 1) as i:
                step(i, 1, False, False)
                step(i + 1, 0, False, False)
            step(turns // 2 - 1, 1, False, True)
            finish(turns // 2 - 1, 1)

        with nc.Block() as block:
            @block.gpsimd
            def _(pool):
                with pool.Fori(1, turns // 2 + 1) as lap:
                    for p in range(2):
                        pool.wait_ge(landed[p], lap)
                        nc.gpsimd.tensor_copy(idxs[:, p, :], n.c_i16[:, bass.ds(lap * (2 * RING * TPG) + (p - 2) * RING * TPG, RING * TPG)]).then_inc(idx_ready[p], 1)
                        for s in range(RING):
                            k = RING * p + s
                            pool.wait_ge(cleared, 1)
                            if s == 0:
                                pool.wait_ge(idx_ready[p], lap)
                            pool.wait_ge(used[k], lap)
                            for j in range(TPG):
                                pool.indirect_dma_start(g[:, k, j, :], None, table, bass.IndirectOffsetOnAxis(
                                    ap=idxs[:, p, s * TPG + j:s * TPG + j + 1], axis=0)).then_inc(got[k], 16)

            @block.sync
            def _(sp):
                with sp.Fori(0, turns // 2) as i:
                    for p in range(2):
                        sp.wait_ge(cut, i * 2 + (p + 1))
                        sp.dma_start(flags[:, p, :, :].rearrange("q a e -> q (a e)"),
                                     flag_table[bass.ds(i * (2 * RING * H) + p * RING * H, RING * H), :]).then_inc(flags_in[p], 16)
                        for s in range(RING):
                            k = RING * p + s
                            base = sp.value_load(n.base[0:1, bass.ds(i * (2 * RING) + k, 1)], min_val=0, max_val=NP - WIN)
                            sp.wait_ge(er_done, i * 8 + (4 * p + s + 1))
                            sp.dma_start(erw[:, k, :], er_table[bass.ds(base, WIN), :]).then_inc(er_in[k], 16)

            @block.tensor
            def _(pe):
                def multiply(i, p, s):
                    k = RING * p + s
                    pe.wait_ge(hot[p], i * RING + (s + 1))
                    pe.wait_ge(got[k], i * (16 * TPG) + (got0 + 16 * TPG))
                    pe.wait_ge(scaled, i * 8 + (4 * p + s + 1))
                    if s == 0:
                        pe.wait_ge(parted, i * 2 + (p + 2))
                    pe.wait_ge(added, i * 8 + (4 * p + s + 1))
                    for j in range(TPG):
                        nc.tensor.matmul(ps[:, s, 0:WIN], g[:, k, j, 0:D], oh[:, k, j, :], start=j == 0, stop=j == TPG - 1, skip_group_check=True)
                        nc.tensor.matmul(ps[:, s, WIN:2 * WIN], zs[:, s, j, :], oh[:, k, j, :], start=False, stop=j == TPG - 1, skip_group_check=True)
                        mm = nc.tensor.matmul(ps[:, s, 2 * WIN:3 * WIN], exd[:, s, j, :, :].rearrange("p h d -> p (h d)"), ohb[:, k, j, :],
                                              start=False, stop=j == TPG - 1, skip_group_check=True)
                    mm.then_inc(used[k], 1)

                def look_up(i, p):
                    for s in range(RING):
                        c = 4 * p + s
                        pe.wait_ge(half_hot, i * 8 + (c + 1))
                        pe.wait_ge(hot_t, i * 8 + (c + 1))
                        for j in range(TPG):
                            t = nc.tensor.transpose(ps_t[s % 2][:, j, :], ohb[:, RING * p + s, j, :], n.identb[:, :])
                        t.then_inc(hot_turned, 1)
                    for s in range(RING):
                        if s == 0:
                            pe.wait_ge(hot_t, i * 8 + (4 * p + 6))
                            pe.wait_ge(x_ready, i * 2 + (p + 1))
                        pe.wait_ge(er_in[RING * p + s], i * 16 + 16)
                        for j in range(TPG):
                            q = (s * TPG + j) * H * PARTS
                            mm = nc.tensor.matmul(er_ps[:, q:q + H * PARTS], oht[:, s, j, :], erw[:, RING * p + s, :], start=True, stop=True)
                        mm.then_inc(er_done, 1)

                def step(i, p, first, last):
                    pe.wait_ge(x_ready, i * 2 + (p + 2))
                    pe.wait_ge(cut, i * 2 + (p + 2))
                    for j in range(TPG):
                        t = nc.tensor.transpose(ps_x[0:RING * H, j * P:(j + 1) * P], x[:, j, :, :].rearrange("p s h -> p (s h)"), n.ident[:, :])
                    t.then_inc(x_turned, 1)
                    if not first:
                        multiply(*((i, 0) if p else (i - 1, 1)), RING - 1)
                    pe.wait_ge(grown, i * 2 + (p + 1))
                    pe.wait_ge(ends_ready, i * 4 + (2 * p + 2))
                    pe.wait_ge(spread, i * 2 + (p + 1))
                    pe.wait_ge(fac_ready, i * 2 + (p + 1))
                    nc.tensor.matmul(end_ps, n.selh[:, :], ends[:, :, :].rearrange("q a g -> q (a g)"), start=True, stop=True)
                    for j in range(TPG):
                        t = nc.tensor.transpose(ex_ps[:, j, :, :], ex[:, j * P:(j + 1) * P], n.ident[0:RING * H, 0:RING * H])
                    t.then_inc(back, 1)
                    multiply(i, p, 0)
                    if not last:
                        look_up(*after(i, p))
                    multiply(i, p, 1)
                    multiply(i, p, 2)

                for k in range(2 * RING):
                    pe.sem_inc(used[k], 1)
                pe.sem_inc(er_done, 2 * RING)
                pe.sem_inc(x_turned, 1)
                pe.sem_inc(back, 1)
                look_up(0, 0)
                steps(pe, step, lambda i, p: multiply(i, p, RING - 1))

            @block.scalar
            def _(act):
                def look_up(i, p):
                    def keep_turned(s):
                        c = 4 * p + s
                        act.wait_ge(hot_turned, i * 8 + (c + 1))
                        act.wait_ge(er_done, i * 8 + (c + 1 + RING))
                        nc.scalar.copy(oht[:, s, :, :], ps_t[s % 2][:, :, :]).then_inc(hot_t, 1)

                    for s in range(RING):
                        act.wait_ge(hot[p], i * RING + (s + 1))
                        nc.scalar.copy(ohb[:, RING * p + s, :, :], oh[:, RING * p + s, :, :]).then_inc(half_hot, 1)
                        if s:
                            keep_turned(s - 1)
                    keep_turned(RING - 1)

                def step(i, p, first, last):
                    act.wait_ge(cut, i * 2 + (p + 3))
                    nc.scalar.activation(ex[:, :], ex[:, :], ACT.Exp).then_inc(grown, 1)
                    act.wait_ge(back, i * 2 + (p + 2))
                    act.wait_ge(parted, i * 2 + (p + 1))
                    nc.scalar.copy(exc[:, :, :, :], ex_ps).then_inc(spread, 1)
                    act.wait_ge(gap, i * 4 + (2 * p + 2))
                    nc.scalar.activation(fac[:, p, :, :], diff[:, p, :, :], ACT.Exp).then_inc(fac_ready, 1)
                    if not last:
                        look_up(*after(i, p))

                act.sem_inc(hot_t, 2)
                act.sem_inc(spread, 1)
                act.sem_inc(fac_ready, 1)
                look_up(0, 0)
                steps(act, step, lambda i, p: None)

            @block.vector
            def _(dve):
                v = nc.vector
                iota = n.iota[:, :].unsqueeze(1).to_broadcast([P, TPG, WIN])

                def build(i, p):
                    for s in range(RING):
                        k = RING * p + s
                        dstl = n.c_dstl[:, bass.ds(i * (2 * RING * TPG) + k * TPG, TPG)].unsqueeze(2).to_broadcast([P, TPG, WIN])
                        dve.wait_ge(used[k], i + 1)
                        v.tensor_tensor(oh[:, k, :, :], iota, dstl, ALU.is_equal).then_inc(hot[p], 1)

                def add(i, p, s):
                    link = Link(dve, link_a, i * (8 * KA) + (4 * p + s) * KA)
                    k = RING * p + s
                    base = v.value_load(n.base[0:1, bass.ds(i * (2 * RING) + k, 1)], min_val=0, max_val=NP - WIN)
                    if s == 0:
                        dve.wait_ge(fac_ready, i * 2 + (p + 2))
                    dve.wait_ge(used[k], i + 2)
                    dve.wait_ge(added, i * 8 + (4 * p + s + RING))
                    new = ps[:, s, 0:3 * WIN].rearrange("p (r w) -> p r w", w=WIN)
                    old = n.acc[:, 1:3, bass.ds(base, 1)]
                    link.mark(v.tensor_scalar(new[:, 1:3, 0:1], new[:, 1:3, 0:1], fac[:, p, 1, s:s + 1], None, ALU.mult))
                    link.mark(v.tensor_scalar(old, old, fac[:, p, 0, s:s + 1], None, ALU.mult))
                    link.join()
                    link.check(KA)
                    out = n.acc[:, :, bass.ds(base, WIN)]
                    v.tensor_tensor(out, out, new, ALU.add).then_inc(added, 1)

                def scale(i, p, s):
                    w = exc[:, :, s, :].unsqueeze(3).to_broadcast([P, TPG, H, DH])
                    v.tensor_tensor(zs[:, s, :, :].rearrange("p t (h d) -> p t h d", d=DH),
                                    g[:, RING * p + s, :, D:2 * D].rearrange("p t (h d) -> p t h d", d=DH), w, ALU.mult).then_inc(scaled, 1)

                def step(i, p, first, last):
                    link = Link(dve, link_c, i * (2 * KC) + p * KC)
                    groups = bass.ds(i * (2 * RING) + p * RING, RING)
                    for s in range(RING):
                        dve.wait_ge(got[RING * p + s], i * (16 * TPG) + (got0 + 16 * TPG))
                    dve.wait_ge(er_done, i * 8 + (4 * p + 3 * RING))
                    dve.wait_ge(x_turned, i * 2 + (p + 1))
                    link(v.reduce_sum(er[:, :, :].rearrange("p t h -> p (t h)"), er_ps.rearrange("p (c k) -> p c k", k=PARTS), AX_X))
                    el = g[:, RING * p:RING * (p + 1), :, 2 * D:ROW]
                    link(v.tensor_tensor(x[:, :, :, :].rearrange("p t s h -> p s t h"), el, er[:, :, :].rearrange("p (s t) h -> p s t h", t=TPG), ALU.add))
                    xf = x[:, :, :, :].rearrange("p t s h -> p (t s h)")
                    dve.sem_inc(landed[p], 1)
                    v.scalar_tensor_tensor(out=xf, in0=xf, scalar=0.2, in1=xf, op0=ALU.mult, op1=ALU.max).then_inc(x_ready, 1)
                    dve.wait_ge(x_turned, i * 2 + (p + 2))
                    dve.wait_ge(flags_in[p], i * 16 + 16)
                    line = ps_x[0:RING * H, :]
                    link(v.tensor_tensor_scan(fwd[:, :], flags[:, p, 0, :], line, -BIG, ALU.add, ALU.max))
                    link(v.tensor_tensor_scan(bwd[:, ::-1], flags[:, p, 1, ::-1], fwd[:, ::-1], -BIG, ALU.add, ALU.max))
                    dve.wait_ge(back, i * 2 + (p + 1))
                    v.tensor_tensor(ex[:, :], line, bwd[:, :], ALU.subtract).then_inc(cut, 1)
                    v.tensor_scalar(ends[:, 0, :], n.gmask[:, :], bwd[:, 0:1], None, ALU.mult).then_inc(ends_ready, 1)
                    v.tensor_scalar(ends[:, 1, :], n.gmask[:, :], fwd[:, GE - 1:GE], None, ALU.mult).then_inc(ends_ready, 1)
                    if not first:
                        add(*((i, 0) if p else (i - 1, 1)), RING - 1)
                    dve.wait_ge(spread, i * 2 + (p + 2))
                    scale(i, p, 0)
                    w = exc[:, :, :, :].rearrange("p t s h -> p s t h")
                    link(v.tensor_copy(exd[:, :, :, :, 0], w))
                    link(v.tensor_tensor(exr[:, :, :, :], w, exd[:, :, :, :, 0], ALU.subtract))
                    link(v.tensor_copy(exd[:, :, :, :, 1], exr[:, :, :, :]))
                    link(v.tensor_tensor(exr[:, :, :, :], exr[:, :, :, :], exd[:, :, :, :, 1], ALU.subtract))
                    for s in range(1, RING):
                        scale(i, p, s)
                    dve.wait_ge(scaled, i * 8 + (4 * p + 4))
                    v.tensor_copy(exd[:, :, :, :, 2], exr[:, :, :, :]).then_inc(parted, 1)
                    dve.wait_ge(back, i * 2 + (p + 2))
                    link(v.tensor_tensor_scan(run[:, 1:RING + 1], n.seg[:, 1, groups], end_ps[:, RING:2 * RING], run[:, 0:1], ALU.add, ALU.max))
                    link(v.tensor_tensor(cin[:, :], run[:, 0:RING], n.seg[:, 0, groups], ALU.add))
                    link(v.tensor_tensor(top[:, :], cin[:, :], end_ps[:, 0:RING], ALU.max))
                    link.mark(v.tensor_copy(run[:, 0:1], run[:, RING:RING + 1]))
                    v.tensor_tensor(diff[:, p, 0, :], cin[:, :], top[:, :], ALU.subtract).then_inc(gap, 1)
                    v.tensor_tensor(diff[:, p, 1, :], end_ps[:, 0:RING], top[:, :], ALU.subtract).then_inc(gap, 1)
                    link.join()
                    dve.wait_ge(gap, i * 4 + (2 * p + 2))
                    link.check(KC)
                    if not last:
                        build(*after(i, p))
                    for s in range(RING - 1):
                        add(i, p, s)

                v.memset(n.acc[:, :, :], 0.0).then_inc(cleared, 1)
                v.memset(run[:, :], -BIG).then_inc(cleared, 1)
                v.memset(exd[:, :, :, :, :], 0.0).then_inc(cleared, 1)
                dve.wait_ge(cleared, 3)
                for p in range(2):
                    dve.sem_inc(landed[p], 1)
                dve.sem_inc(x_ready, 1)
                dve.sem_inc(cut, 2)
                dve.sem_inc(parted, 1)
                dve.sem_inc(added, RING)
                build(0, 0)
                steps(dve, step, lambda i, p: add(i, p, RING - 1))


def fuse_phase(nc, n, l, out):
    with Phase(nc, f"fuse{l}") as ph:
        link_sem, gat_ready, rel_made, rel_ready = ph.sem("link"), ph.sem("gat"), ph.sem("rel_made"), ph.sem("rel")
        fused, hc_ready, gated, sig, h_ready = ph.sem("fused"), ph.sem("hc"), ph.sem("gated"), ph.sem("sig"), ph.sem("h_ready")
        turned, x_ready, stored, bias_ready, rel_read = ph.sem("turned"), ph.sem("x_ready"), ph.sem("stored"), ph.sem("bias"), ph.sem("rel_read")
        den_made, den_read = ph.sem("den_made"), ph.sem("den_read")
        gbias = ph.sb("gbias", [P, 1])
        rel = ph.sb("rel", [P, 2, 4 * P])
        hc = ph.sb("hc_v", [P, 2, 4 * P])
        gate = ph.sb("gate", [P, 2, 4 * P])
        ps = ph.ps("ps", [P, 4, 2, 4 * P])
        a0, a1, a2 = (n.acc[:, k, :] for k in range(3))
        gating, last = l == 0, l == LAYERS - 1
        with nc.Block() as block:
            @block.vector
            def _(dve):
                v = nc.vector
                link = Link(dve, link_sem)
                link(v.tensor_tensor(gbias[:, :], n.cols[:, 8:9], n.tw[:, :], ALU.mult))
                v.tensor_tensor(gbias[:, :], gbias[:, :], n.cols[:, 7:8], ALU.add).then_inc(bias_ready, 1)
                for q, c in enumerate(CH):
                    w = c[1] * P
                    dve.wait_ge(den_made, q + 1)
                    v.tensor_scalar(chunk(a2, c), ps[:, 3, q % 2, 0:w], 1e-30, None, ALU.max).then_inc(den_read, 1)
                    dve.wait_ge(den_read, q + 1)
                    link(v.reciprocal(chunk(a2, c), chunk(a2, c)))
                    link(v.tensor_tensor(chunk(a1, c), chunk(a1, c), chunk(a2, c), ALU.mult))
                    v.tensor_scalar(chunk(a1, c), chunk(a1, c), n.cols[:, 3 + l:4 + l], None, ALU.add).then_inc(gat_ready, 1)
                    dve.wait_ge(rel_made, q + 1)
                    if q >= 2:
                        dve.wait_ge(fused, q - 1)
                    v.scalar_tensor_tensor(out=rel[:, q % 2, 0:w], in0=ps[:, 0, q % 2, 0:w], scalar=n.cols[:, l:l + 1],
                                           in1=chunk(a0, c), op0=ALU.add, op1=ALU.add).then_inc(rel_ready, 1)
                    if gating:
                        dve.wait_ge(sig, q + 1)
                        link(v.tensor_tensor(gate[:, q % 2, 0:w], gate[:, q % 2, 0:w], hc[:, q % 2, 0:w], ALU.mult))
                        v.tensor_scalar(chunk(n.ht, c), gate[:, q % 2, 0:w], 0.0, None, ALU.max).then_inc(h_ready, 1)
                    if last:
                        dve.wait_ge(turned, q + 1)
                        v.tensor_tensor(chunk3(n.x, c), chunk3(n.x, c), ps[:, 2, q % 2, 0:w].rearrange("p (t d) -> p t d", d=D),
                                        ALU.add).then_inc(x_ready, 1)

            @block.tensor
            def _(pe):
                for q, c in enumerate(CH):
                    w = c[1] * P
                    if q >= 2:
                        pe.wait_ge(rel_ready, q - 1)
                    if q >= 2:
                        pe.wait_ge(den_read, q - 1)
                    nc.tensor.matmul(ps[:, 3, q % 2, 0:w], n.same_head[:, :], chunk(a2, c), start=True, stop=True).then_inc(den_made, 1)
                    nc.tensor.matmul(ps[:, 0, q % 2, 0:w], n.wloop[:, l, :], chunk(n.ht, c), start=True, stop=True).then_inc(rel_made, 1)
                    pe.wait_ge(rel_ready, q + 1)
                    pe.wait_ge(gat_ready, q + 1)
                    if q >= 2:
                        pe.wait_ge(hc_ready, q - 1)
                    nc.tensor.matmul(ps[:, 1, q % 2, 0:w], n.wfuse[:, 0, :], rel[:, q % 2, 0:w], start=True, stop=False)
                    nc.tensor.matmul(ps[:, 1, q % 2, 0:w], n.wfuse[:, 1, :], chunk(a1, c), start=False, stop=True).then_inc(fused, 1)
                    pe.wait_ge(hc_ready, q + 1)
                    if gating:
                        if q >= 2:
                            pe.wait_ge(sig, q - 1)
                        nc.tensor.matmul(ps[:, 2, q % 2, 0:w], n.wgate[:, :], hc[:, q % 2, 0:w], start=True, stop=True).then_inc(gated, 1)
                    if last:
                        if q >= 2:
                            pe.wait_ge(x_ready, q - 1)
                        for j in range(c[1]):
                            t = nc.tensor.transpose(ps[:, 2, q % 2, j * P:(j + 1) * P], chunk(n.ht, (c[0] + j, 1)), n.ident[:, :])
                        t.then_inc(turned, 1)

            @block.scalar
            def _(act):
                act.wait_ge(bias_ready, 1)
                for q, c in enumerate(CH):
                    w = c[1] * P
                    act.wait_ge(fused, q + 1)
                    if not gating:
                        nc.scalar.activation(chunk(n.ht, c), ps[:, 1, q % 2, 0:w], ACT.Relu, bias=n.cols[:, 6:7]).then_inc(hc_ready, 1)
                        continue
                    if q >= 2:
                        act.wait_ge(h_ready, q - 1)
                    nc.scalar.activation(hc[:, q % 2, 0:w], ps[:, 1, q % 2, 0:w], ACT.Identity, bias=n.cols[:, 6:7]).then_inc(hc_ready, 1)
                    act.wait_ge(gated, q + 1)
                    nc.scalar.activation(gate[:, q % 2, 0:w], ps[:, 2, q % 2, 0:w], ACT.Sigmoid, bias=gbias[:, 0:1]).then_inc(sig, 1)

            if last:
                @block.sync
                def _(sp):
                    n_dma = 0
                    for q, c in enumerate(CH):
                        sp.wait_ge(x_ready, q + 1)
                        full = min(c[1], max(0, N // P - c[0]))
                        if full:
                            sp.dma_start(rows(out, (c[0], full)), chunk3(n.x, (c[0], full))).then_inc(stored, 16)
                            n_dma += 1
                        if c[0] <= N // P < c[0] + c[1]:
                            sp.dma_start(out[N // P * P:N, :], chunk(n.x, (N // P, 1))[0:N % P, :]).then_inc(stored, 16)
                            n_dma += 1
                    sp.wait_ge(stored, 16 * n_dma)


def bass_gnn_kernel(nc, a, out):
    n = Net()
    h_table = nc.dram_tensor("h_table", (NP, D), F32).ap()
    m_table = nc.dram_tensor("m_table", (NP * R4, HID), F32).ap()
    g_table = nc.dram_tensor("g_table", (NP * R16, ROW), F32).ap()
    er_table = nc.dram_tensor("er_table", (NP, H * PARTS), BF16).ap()
    flag_table = nc.dram_tensor("flag_table", (GR * H, 2 * GE), F32).ap()
    n.got = [nc.alloc_semaphore(f"got{s}", num=FIRST_GATHER_SEM + s) for s in range(RING)]
    n.att_got = [nc.alloc_semaphore(f"att_got{k}", num=FIRST_GATHER_SEM + RING + k) for k in range(2 * RING)]
    n.got_count = n.att_count = 0
    with ExitStack() as whole, ExitStack() as early:
        def sb(name, shape, dt=F32, ctx=whole):
            return ctx.enter_context(nc.sbuf_tensor(name, shape, dt))

        n.ident, n.iota, n.ones = sb("ident", [P, P]), sb("iota", [P, P]), sb("ones", [P, P])
        n.identb, n.selh, n.gmask = sb("identb", [P, P], BF16), sb("selh", [RING * H, P]), sb("gmask", [RING * H, RING])
        n.same_head = sb("same_head", [P, P])
        n.x, n.ht = sb("x", [P, NP]), sb("ht", [P, NP])
        n.acc = sb("acc", [P, 3, NP])
        n.hn = n.acc[:, 2, :]
        n.c_i16, n.c_dstl = sb("c_i16", [P, TILES], I32), sb("c_dstl", [P, TILES])
        n.seg, n.base, n.tw = sb("seg", [P, 2, GR]), sb("base", [1, GR], I32), sb("tw", [P, 1])
        n.wloop, n.wgat, n.wfuse = sb("wloop", [P, LAYERS, D]), sb("wgat", [P, LAYERS, D]), sb("wfuse", [P, 2, D])
        n.wgate, n.cols, n.attn = sb("wgate", [P, D]), sb("cols", [P, 9]), sb("attn", [P, LAYERS, 2, D])

        def sb0(name, shape, dt=F32):
            return sb(name, shape, dt, early)

        n.rdeg, n.rowb, n.eps = sb0("rdeg", [P, NP]), sb0("rowb", [P, 6, D]), sb0("eps", [P, 1])
        n.c_src, n.c_i4, n.c_u = sb0("c_src", [P, TILES], I32), sb0("c_i4", [P, TILES], I32), sb0("c_u", [P, TILES])
        n.wagg_t, n.w1, n.w2 = sb0("wagg_t", [P, 2, D]), sb0("w1", [P, 3, D]), sb0("w2", [P, 3, D])
        n.wr1, n.wr2, n.wr3 = sb0("wr1", [P, R4, HID]), sb0("wr2", [HID, R4, HID]), sb0("wr3", [HID, R4, D])
        n.wn1, n.wn2, n.wn3 = sb0("wn1", [P, 1 + R4, HID]), sb0("wn2", [HID, HID]), sb0("wn3", [HID, D])
        n.br1, n.br2, n.br3, n.bn12 = sb0("br1", [HID, R4]), sb0("br2", [HID, R4]), sb0("br3", [P, R4]), sb0("bn12", [HID, 2])
        with ExitStack() as rows_ctx:
            n.erow_i = rows_ctx.enter_context(nc.sbuf_tensor("erow_i", [P, 4, GE], I32))
            n.erow_w = rows_ctx.enter_context(nc.sbuf_tensor("erow_w", [P, 2, GE], F32))
            load_phase(nc, n, a)
            edge_phase(nc, n, flag_table)
        norm_phase(nc, n, "norm0", h_table)
        edge_pass(nc, n, "pass0", h_table, n.c_src, D, "degree")
        mean_layer(nc, n)
        norm_phase(nc, n, "norm1", h_table)
        edge_pass(nc, n, "pass1", h_table, n.c_src, D, "spline")
        spline_layer(nc, n, "conv1", n.w1, 3, h_table)
        edge_pass(nc, n, "pass2", h_table, n.c_src, D, "spline")
        spline_layer(nc, n, "conv2", n.w2, 4, None)
        norm_phase(nc, n, "norm2", h_table)
        message_phase(nc, n, m_table)
        edge_pass(nc, n, "pass3", m_table, n.c_i4, HID, "plain")
        relation_layer(nc, n)
        norm_phase(nc, n, "norm3", h_table)
        early.close()
        for l in range(LAYERS):
            table_phase(nc, n, l, a["L3_gnn_W_rel"], g_table, er_table)
            attend_pass(nc, n, l, g_table, er_table, flag_table)
            fuse_phase(nc, n, l, out)


_INS = ['x', 'src', 'dst', 'edge_type_16', 'edge_type_4', 'edge_weight', 'edge_weight1',
        'L0_gnn_W_agg', 'L0_gnn_b_agg', 'L0_gnn_gamma', 'L0_gnn_beta',
        'L1_gnn_W1', 'L1_gnn_root1', 'L1_gnn_b1', 'L1_gnn_W2', 'L1_gnn_root2', 'L1_gnn_b2',
        'L2_gnn_Wr1', 'L2_gnn_br1', 'L2_gnn_Wr2', 'L2_gnn_br2', 'L2_gnn_Wr3', 'L2_gnn_br3',
        'L2_gnn_Wn1', 'L2_gnn_bn1', 'L2_gnn_Wn2', 'L2_gnn_bn2', 'L2_gnn_Wn3', 'L2_gnn_bn3',
        'L3_gnn_W_rel', 'L3_gnn_b_rel', 'L3_gnn_W_loop', 'L3_gnn_W_gat', 'L3_gnn_attn_l', 'L3_gnn_attn_r',
        'L3_gnn_b_gat', 'L3_gnn_W_fuse', 'L3_gnn_b_fuse', 'L3_gnn_W_gate', 'L3_gnn_b_gate']


def kernel(**inputs):
    import numpy as _np
    import concourse.bacc as _bacc
    from concourse import mybir as _mybir
    from concourse.bass_utils import run_bass_kernel_spmd as _run

    nc = _bacc.Bacc("TRN2", target_bir_lowering=False, num_devices=1)
    arrays, args = {}, {}
    for name in _INS:
        v = _np.ascontiguousarray(inputs[name])
        arrays[f"in_{name}_dram"] = v
        args[name] = nc.dram_tensor(f"in_{name}_dram", v.shape, _mybir.dt.from_np(v.dtype), kind="ExternalInput").ap()
    out = nc.dram_tensor("out_0_dram", (N, D), F32, kind="ExternalOutput").ap()
    bass_gnn_kernel(nc, args, out)
    r = _run(nc, [arrays], core_ids=[0])
    return r.results[0]["out_0_dram"]
```

```python
from contextlib import ExitStack, nullcontext

import concourse.bass as bass
from concourse import mybir

P = 128
F32 = mybir.dt.float32
I32 = mybir.dt.int32
ALU = mybir.AluOpType
ACT = mybir.ActivationFunctionType
AX_X = mybir.AxisListType.X

N = 3125
D = 128
E = 53125
NT = 26
NP = NT * P
NTABLE = -(-N // P)
TPG = 4
GE = TPG * P
NG = -(-E // GE)
GR = P
TILES = GR * TPG
WIN = P
RING = 4
AHEAD = 2 * RING * TPG
R4, R16 = 4, 16
H, DH = 4, 32
HID = 64
LAYERS = 3
EPS = 1e-5
BIG = 1.0e30
BF16 = mybir.dt.bfloat16
ROW = 2 * D + H
PARTS = 3
PAD_NODE = 4000
FIRST_SEM = 110
FIRST_GATHER_SEM = 200
NB = -(-N // WIN)
assert E // GE + NB <= GR and NG % (2 * RING) == 0 and GR % (2 * RING) == 0
FIELDS = 6
BATCH = 16
CH = [(4 * q, min(4, NT - 4 * q)) for q in range(-(-NT // 4))]
NCH = len(CH)


class Phase:

    def __init__(self, nc, name):
        self.nc, self.name, self.stack = nc, name, ExitStack()
        self.sems = []

    def __enter__(self):
        return self

    def sem(self, name):
        s = self.nc.alloc_semaphore(f"{self.name}_{name}", num=FIRST_SEM + len(self.sems))
        self.sems.append(s)
        return s

    def sb(self, name, shape, dt=F32):
        return self.stack.enter_context(self.nc.sbuf_tensor(f"{self.name}_{name}", shape, dt))

    def ps(self, name, shape, dt=F32):
        return self.stack.enter_context(self.nc.psum_tensor(f"{self.name}_{name}", shape, dt))

    def __exit__(self, *exc):
        if exc[0] is None:
            self.nc.all_engine_barrier(sems_to_clear=range(FIRST_SEM, FIRST_SEM + len(self.sems)))
            for s in self.sems:
                self.nc.release_semaphore(s)
        self.stack.close()


class Link:

    def __init__(self, eng, sem, before=0):
        self.eng, self.sem, self.before, self.n = eng, sem, before, 0

    def mark(self, ins):
        self.n += 1
        ins.then_inc(self.sem, 1)

    def join(self):
        self.eng.wait_ge(self.sem, self.before + self.n)

    def check(self, n):
        assert self.n == n, self.n

    def __call__(self, ins):
        self.mark(ins)
        self.join()


class Net:
    pass


class Part:

    def __init__(self, n, first, stop, got, got0, extra):
        self.n, self.first, self.stop, self.got, self.got0, self.extra = n, first, stop, got, got0, extra

    def only(self, eng):
        if not self.extra:
            return nullcontext()
        return eng.If(eng.value_load(self.n.wide[0:1, 0:1], min_val=0, max_val=1) != 0)

    def arrived(self, eng, k, i):
        eng.wait_ge(self.got[k], i * (16 * TPG) + (self.got0 - 16 * TPG * self.first + 16 * TPG))


def parts(n, per_turn, got, extra_got, counts):
    out, first = [], 0
    for extra, sems, stop in ((False, got, NG // per_turn), (True, extra_got, GR // per_turn)):
        out.append(Part(n, first, stop, sems, counts[extra], extra))
        counts[extra] += (stop - first) * 16 * TPG
        first = stop
    return out


def chunk(t, c):
    return t[:, c[0] * P:(c[0] + c[1]) * P]


def chunk3(t, c):
    return chunk(t, c).rearrange("p (t d) -> p t d", d=D)


def rows(dram, c):
    return dram[c[0] * P:(c[0] + c[1]) * P].rearrange("(t p) d -> p t d", p=P)


def load_phase(nc, n, a):
    with Phase(nc, "load") as ph:
        loaded, zeroed, built, made = ph.sem("loaded"), ph.sem("zeroed"), ph.sem("built"), ph.sem("made")
        turned = ph.sem("turned")
        iota_i = ph.sb("iota_i", [P, P], I32)
        wagg = ph.sb("wagg", [P, 2 * D])
        wt = ph.ps("wt", [P, 3, D])
        full, rest = NG - 1, E - (NG - 1) * GE
        xt, xr = N // P, N % P

        def col(v):
            return v.rearrange("(p o) -> p o", o=1)

        def bcast(v):
            return v.rearrange("(o d) -> o d", o=1).to_broadcast([P, D])

        plain = [
            (wagg[:, :], a["L0_gnn_W_agg"]),
            (n.w1[:, 0:2, :], a["L1_gnn_W1"].rearrange("k c o -> c k o")), (n.w1[:, 2, :], a["L1_gnn_root1"]),
            (n.w2[:, 0:2, :], a["L1_gnn_W2"].rearrange("k c o -> c k o")), (n.w2[:, 2, :], a["L1_gnn_root2"]),
            (n.wr1[:, :, :], a["L2_gnn_Wr1"].rearrange("r c o -> c r o")),
            (n.wn1[:, :, :], a["L2_gnn_Wn1"].rearrange("(k c) o -> c k o", c=D)),
            (n.wn2[:, :], a["L2_gnn_Wn2"]), (n.wn3[:, :], a["L2_gnn_Wn3"]),
            (n.br1[:, :], a["L2_gnn_br1"].rearrange("(a s) h -> (s h) a", s=2)),
            (n.br2[:, :], a["L2_gnn_br2"].rearrange("(a s) h -> (s h) a", s=2)),
            (n.br3[:, :], a["L2_gnn_br3"].rearrange("r h -> h r")),
            (n.bn12[:, 0:1], col(a["L2_gnn_bn1"])), (n.bn12[:, 1:2], col(a["L2_gnn_bn2"])),
            (n.wloop[:, :, :], a["L3_gnn_W_loop"].rearrange("l c o -> c l o")),
            (n.wgat[:, :, :], a["L3_gnn_W_gat"].rearrange("l c o -> c l o")),
            (n.wfuse[:, :, :], a["L3_gnn_W_fuse"].rearrange("(k c) o -> c k o", c=D)),
            (n.wgate[:, :], a["L3_gnn_W_gate"][0:D, :]),
            (n.cols[:, 0:3], a["L3_gnn_b_rel"].rearrange("l d -> d l")),
            (n.cols[:, 3:6], a["L3_gnn_b_gat"].rearrange("l d -> d l")),
            (n.cols[:, 6:7], col(a["L3_gnn_b_fuse"])), (n.cols[:, 7:8], col(a["L3_gnn_b_gate"])),
            (n.cols[:, 8:9], a["L3_gnn_W_gate"][D:D + 1, :].rearrange("o d -> d o")),
            (n.rowb[:, 0, :], bcast(a["L0_gnn_b_agg"])), (n.rowb[:, 1, :], bcast(a["L0_gnn_gamma"])),
            (n.rowb[:, 2, :], bcast(a["L0_gnn_beta"])), (n.rowb[:, 3, :], bcast(a["L1_gnn_b1"])),
            (n.rowb[:, 4, :], bcast(a["L1_gnn_b2"])), (n.rowb[:, 5, :], bcast(a["L2_gnn_bn3"])),
        ]
        for l in range(LAYERS):
            for side, w in enumerate(("L3_gnn_attn_l", "L3_gnn_attn_r")):
                plain.append((n.attn[:, l, side, :], a[w][l].rearrange("h (d o) -> o (h d)", o=1).to_broadcast([P, D])))
        x3 = n.x[:, :].rearrange("p (t d) -> p t d", d=D)
        after_zero = [
            (x3[:, 0:xt, :], a["x"][0:xt * P].rearrange("(t p) d -> p t d", p=P)),
            (x3[0:xr, xt, :], a["x"][xt * P:N]),
        ]
        for r in range(R4):
            half = slice(r % 2 * HID, (r % 2 + 1) * HID)
            after_zero.append((n.wr2[half, r // 2, half], a["L2_gnn_Wr2"][r]))
            after_zero.append((n.wr3[half, r, :], a["L2_gnn_Wr3"][r]))
        for k, name in enumerate(("src", "dst", "edge_type_16", "edge_type_4")):
            after_zero += [
                (n.erow_i[0:full, k, :], a[name][0:full * GE].rearrange("(g e) -> g e", e=GE)),
                (n.erow_i[full:full + 1, k, 0:rest], a[name][full * GE:E].rearrange("(g e) -> g e", g=1)),
            ]
        w0, w1 = a["edge_weight"], a["edge_weight1"].rearrange("e o -> (e o)")
        for k, w in enumerate((w0, w1)):
            after_zero += [
                (n.erow_w[0:full, k, :], w[0:full * GE].rearrange("(g e) -> g e", e=GE)),
                (n.erow_w[full:full + 1, k, 0:rest], w[full * GE:E].rearrange("(g e) -> g e", g=1)),
            ]

        with nc.allow_non_contiguous_dma(reason="bias vectors, one element per partition"), nc.Block() as block:
            @block.sync
            def _(sp):
                sp.wait_ge(zeroed, 6)
                for dst, src in after_zero:
                    sp.dma_start(dst, src).then_inc(loaded, 16)
                sp.wait_ge(loaded, 16 * (len(plain) + len(after_zero)))

            @block.scalar
            def _(act):
                for dst, src in plain:
                    act.dma_start(dst, src).then_inc(loaded, 16)
                act.wait_ge(turned, 1)
                nc.scalar.copy(n.wagg_t[:, :, :], wt[:, 0:2, :]).then_inc(made, 1)
                nc.scalar.copy(n.same_head[:, :], wt[:, 2, :]).then_inc(made, 1)

            @block.vector
            def _(dve):
                nc.vector.memset(n.x[:, :], 0.0).then_inc(zeroed, 1)
                nc.vector.memset(n.wr2[:, :, :], 0.0).then_inc(zeroed, 1)
                nc.vector.memset(n.wr3[:, :, :], 0.0).then_inc(zeroed, 1)
                nc.vector.memset(n.erow_i[:, :, :], 0).then_inc(zeroed, 1)
                dve.wait_ge(zeroed, 4)
                nc.vector.memset(n.erow_i[:, 1, :], PAD_NODE).then_inc(zeroed, 1)
                nc.vector.memset(n.erow_w[:, :, :], 0.0).then_inc(zeroed, 1)
                nc.vector.memset(n.ones[:, :], 1.0).then_inc(made, 1)
                nc.vector.memset(n.eps[:, :], EPS).then_inc(made, 1)
                dve.wait_ge(built, 2)
                nc.vector.tensor_copy(n.iota[:, :], iota_i[:, :]).then_inc(made, 1)
                dve.wait_ge(built, 3)
                nc.vector.tensor_copy(n.identb[:, :], n.ident[:, :]).then_inc(made, 1)

            @block.gpsimd
            def _(pool):
                nc.gpsimd.memset(n.ident[:, :], 0.0).then_inc(built, 1)
                nc.gpsimd.iota(iota_i[:, :], pattern=[[1, P]], base=0, channel_multiplier=0).then_inc(built, 1)
                pool.wait_ge(built, 2)
                nc.gpsimd.affine_select(out=n.ident[:, :], in_=n.ident[:, :], compare_op=ALU.not_equal, fill=1.0,
                                        base=0, pattern=[[-1, P]], channel_multiplier=1).then_inc(built, 1)
                nc.gpsimd.memset(n.selh[:, :], 0.0).then_inc(built, 1)
                nc.gpsimd.memset(n.gmask[:, :], 0.0).then_inc(built, 1)
                pool.wait_ge(built, 5)
                sel = n.selh[:, :].rearrange("q (h d) -> q h d", d=DH)
                for k in range(4):
                    nc.gpsimd.affine_select(out=sel, in_=sel, compare_op=ALU.not_equal, fill=1.0, base=-H * k,
                                            pattern=[[-1, H], [0, DH]], channel_multiplier=1).then_inc(built, 1)
                    nc.gpsimd.affine_select(out=n.gmask[:, :], in_=n.gmask[:, :], compare_op=ALU.not_equal, fill=1.0, base=-k,
                                            pattern=[[-H, RING]], channel_multiplier=1).then_inc(built, 1)
                    pool.wait_ge(built, 2 * k + 7)

            @block.tensor
            def _(pe):
                pe.wait_ge(built, 13)
                pe.wait_ge(loaded, 16 * (len(plain) + len(after_zero)))
                for k in range(2):
                    nc.tensor.transpose(wt[:, k, :], wagg[:, k * D:(k + 1) * D], n.ident[:, :])
                nc.tensor.matmul(wt[:, 2, :], n.selh[0:H, :], n.selh[0:H, :], start=True, stop=True).then_inc(turned, 1)


def span_phase(nc, n):
    with Phase(nc, "span") as ph:
        link_sem, counted, summed = ph.sem("link"), ph.sem("counted"), ph.sem("summed")
        dst, far, edge = ph.sb("dst", [P, GE]), ph.sb("far", [P, GE]), ph.sb("edge", [P, GE])
        count, any_far = ph.sb("count", [P, 1]), ph.sb("any_far", [1, 1])
        ps = ph.ps("ps", [P, 1])
        with nc.Block() as block:
            @block.vector
            def _(dve):
                v = nc.vector
                link = Link(dve, link_sem)
                link(v.tensor_copy(dst[:, :], n.erow_i[:, 1, :]))
                link.mark(v.tensor_scalar(far[:, :], dst[:, :], dst[:, 0:1], float(WIN), ALU.subtract, ALU.is_ge))
                link(v.tensor_scalar(edge[:, :], dst[:, :], float(PAD_NODE), None, ALU.is_lt))
                link(v.tensor_tensor(far[:, :], far[:, :], edge[:, :], ALU.mult))
                v.reduce_sum(count[:, :], far[:, :], AX_X).then_inc(counted, 1)
                dve.wait_ge(summed, 1)
                link(v.tensor_scalar(any_far[:, :], ps[0:1, :], 1.0, None, ALU.min))
                link(v.tensor_copy(n.wide[:, :], any_far[:, :]))

            @block.tensor
            def _(pe):
                pe.wait_ge(counted, 1)
                nc.tensor.matmul(ps[:, :], n.ones[:, :], count[:, :], start=True, stop=True).then_inc(summed, 1)


def deal_phase(nc, n, dealt_table):
    with Phase(nc, "deal") as ph:
        link_sem, numbered, counted, summed = ph.sem("link"), ph.sem("numbered"), ph.sem("counted"), ph.sem("summed")
        blank_ready, blanked, ready, back = ph.sem("blank_ready"), ph.sem("blanked"), ph.sem("ready"), ph.sem("back")
        free, idx_in, record_in, all_dealt = ph.sem("free"), ph.sem("idx_in"), ph.sem("record_in"), ph.sem("all_dealt")
        number, slot_i = ph.sb("number", [P, GE], I32), ph.sb("slot_i", [P, GE], I32)
        dst, slot, tmp = ph.sb("dst", [P, GE]), ph.sb("slot", [P, GE]), ph.sb("tmp", [P, GE])
        count, below = ph.sb("count", [P, NB + 1]), ph.sb("below", [P, NB + 1])
        edges, room, ends = ph.sb("edges", [P, NB]), ph.sb("room", [P, NB]), ph.sb("ends", [P, NB])
        over, shift, more = ph.sb("over", [P, NB]), ph.sb("shift", [P, NB]), ph.sb("more", [P, NB])
        record = ph.sb("record", [P, GE, FIELDS], I32)
        batch_idx, batch = ph.sb("batch_idx", [P, BATCH], I32), ph.sb("batch", [P, BATCH, FIELDS], I32)
        blank = ph.sb("blank", [P, BATCH, FIELDS], I32)
        ps = ph.ps("ps", [P, NB + 1])
        slots = dealt_table[0:GR * GE, :].rearrange("(g e) k -> g e k", e=GE)
        batches = GE // BATCH
        whole = Part(n, 0, 1, None, 0, True)

        with nc.Block() as block:
            @block.vector
            def _(dve):
                v = nc.vector
                with whole.only(dve):
                    link = Link(dve, link_sem)
                    link(v.memset(blank[:, :, :], 0))
                    v.memset(blank[:, :, 1:2], PAD_NODE).then_inc(blank_ready, 1)
                    link(v.tensor_copy(dst[:, :], n.erow_i[:, 1, :]))
                    link(v.memset(count[:, :], 0.0))
                    for b in range(1, NB + 1):
                        link(v.tensor_scalar(tmp[:, :], dst[:, :], float(WIN * b), None, ALU.is_lt))
                        link(v.reduce_sum(count[:, b:b + 1], tmp[:, :], AX_X))
                    dve.sem_inc(counted, 1)
                    dve.wait_ge(summed, 1)
                    link(v.tensor_copy(below[:, :], ps[:, :]))
                    link(v.tensor_tensor(edges[:, :], below[:, 1:NB + 1], below[:, 0:NB], ALU.subtract))
                    link(v.memset(room[:, :], 0.0))
                    for k in range(NG):
                        link(v.tensor_scalar(over[:, :], edges[:, :], float(GE * k), float(GE), ALU.is_gt, ALU.mult))
                        link(v.tensor_tensor(room[:, :], room[:, :], over[:, :], ALU.add))
                    link(v.memset(over[:, :], 0.0))
                    link(v.tensor_tensor_scan(ends[:, :], room[:, :], over[:, :], 0.0, ALU.add, ALU.add))
                    link(v.tensor_tensor(shift[:, :], ends[:, :], room[:, :], ALU.subtract))
                    link(v.tensor_tensor(shift[:, :], shift[:, :], below[:, 0:NB], ALU.subtract))
                    link(v.tensor_tensor(more[:, 1:NB], shift[:, 1:NB], shift[:, 0:NB - 1], ALU.subtract))
                    dve.wait_ge(numbered, 1)
                    link(v.tensor_copy(slot[:, :], number[:, :]))
                    for b in range(1, NB):
                        link(v.tensor_scalar(tmp[:, :], dst[:, :], float(WIN * b), more[:, b:b + 1], ALU.is_ge, ALU.mult))
                        link(v.tensor_tensor(slot[:, :], slot[:, :], tmp[:, :], ALU.add))
                    link(v.tensor_copy(slot_i[:, :], slot[:, :]))
                    for k in range(4):
                        link(v.tensor_copy(record[:, :, k], n.erow_i[:, k, :]))
                    for k in range(2):
                        link(v.tensor_copy(record[:, :, 4 + k], n.erow_w[:, k, :].bitcast(I32)))
                    dve.sem_inc(ready, 1)
                    dve.sem_inc(free, 1)
                    with dve.Fori(0, batches) as i:
                        dve.wait_ge(n.dealt, i * (16 * BATCH) + 16 * BATCH)
                        dve.sem_inc(free, 1)
                    dve.sem_inc(all_dealt, 1)
                    dve.wait_ge(back, 16)
                    for k in range(4):
                        link(v.tensor_copy(n.erow_i[:, k, :], record[:, :, k]))
                    for k in range(2):
                        link(v.tensor_copy(n.erow_w[:, k, :].bitcast(I32), record[:, :, 4 + k]))

            @block.tensor
            def _(pe):
                with whole.only(pe):
                    pe.wait_ge(counted, 1)
                    nc.tensor.matmul(ps[:, :], n.ones[:, :], count[:, :], start=True, stop=True).then_inc(summed, 1)

            @block.gpsimd
            def _(pool):
                with whole.only(pool):
                    nc.gpsimd.iota(number[:, :], pattern=[[1, GE]], base=0, channel_multiplier=GE).then_inc(numbered, 1)
                    pool.wait_ge(ready, 1)
                    with pool.Fori(1, batches + 1) as lap:
                        pool.wait_ge(free, lap)
                        nc.gpsimd.tensor_copy(batch_idx[:, :], slot_i[:, bass.ds(lap * BATCH - BATCH, BATCH)]).then_inc(idx_in, 1)
                        nc.gpsimd.tensor_copy(batch[:, :, :], record[:, bass.ds(lap * BATCH - BATCH, BATCH), :]).then_inc(record_in, 1)
                        pool.wait_ge(blanked, 16 * batches)
                        pool.wait_ge(idx_in, lap)
                        pool.wait_ge(record_in, lap)
                        for j in range(BATCH):
                            pool.indirect_dma_start(dealt_table, bass.IndirectOffsetOnAxis(ap=batch_idx[0:NG, j:j + 1], axis=0),
                                                    batch[0:NG, j, :], None).then_inc(n.dealt, 16)

            @block.sync
            def _(sp):
                with whole.only(sp):
                    sp.wait_ge(blank_ready, 1)
                    for c in range(batches):
                        sp.dma_start(slots[:, c * BATCH:(c + 1) * BATCH, :], blank[:, :, :]).then_inc(blanked, 16)
                    sp.wait_ge(all_dealt, 1)
                    sp.dma_start(record[:, :, :], slots[:, :, :]).then_inc(back, 16)
                    sp.wait_ge(back, 16)


def edge_phase(nc, n, flag_table):
    with Phase(nc, "edge") as ph:
        link_sem, ready, turned, taken = ph.sem("link"), ph.sem("ready"), ph.sem("turned"), ph.sem("taken")
        f = ph.sb("f", [P, 4, GE])
        idx16 = ph.sb("idx16", [P, GE])
        idx4 = ph.sb("idx4", [P, GE])
        dstl = ph.sb("dstl", [P, GE])
        ends = ph.sb("ends", [P, 3, P])
        fl = ph.sb("fl", [P, 2, GR])
        same = ph.sb("same", [P, 2, GR])
        wsum = ph.sb("wsum", [P, 1])
        rf = ph.sb("rf", [P, GE])
        rb = ph.sb("rb", [P, GE])
        stored = ph.sem("stored")
        turn = ph.ps("turn", [P, 5, TPG, P])
        ends_t = ph.ps("ends_t", [P, 4, P])

        fields = [f[:, 0, :], idx4[:, :], idx16[:, :], dstl[:, :], n.erow_w[:, 1, :]]
        cols = [n.c_src, n.c_i4, n.c_i16, n.c_dstl, n.c_u]

        with nc.Block() as block:
            @block.vector
            def _(dve):
                v = nc.vector
                link = Link(dve, link_sem)
                link(v.tensor_copy(f[:, :, :], n.erow_i[:, :, :]))
                link.mark(v.scalar_tensor_tensor(out=idx16[:, :], in0=f[:, 0, :], scalar=float(R16), in1=f[:, 2, :], op0=ALU.mult, op1=ALU.add))
                link.mark(v.scalar_tensor_tensor(out=idx4[:, :], in0=f[:, 0, :], scalar=float(R4), in1=f[:, 3, :], op0=ALU.mult, op1=ALU.add))
                link.mark(v.tensor_copy(ends[:, 0, :], f[:, 1, 0:1].to_broadcast([P, P])))
                link.mark(v.tensor_copy(ends[:, 1, :], f[:, 1, GE - 1:GE].to_broadcast([P, P])))
                link.mark(v.tensor_scalar(ends[:, 2, :], f[:, 1, 0:1].to_broadcast([P, P]), float(NP - WIN), None, ALU.min))
                link.join()
                link.mark(v.tensor_scalar(dstl[:, :], f[:, 1, :], ends[:, 2, 0:1], None, ALU.subtract))
                link.mark(v.memset(rf[:, 0:1], 0.0))
                link.mark(v.memset(rb[:, GE - 1:GE], 0.0))
                link(v.tensor_tensor(rf[:, 1:GE], f[:, 1, 1:GE], f[:, 1, 0:GE - 1], ALU.not_equal))
                link(v.tensor_scalar(rf[:, 1:GE], rf[:, 1:GE], -BIG, None, ALU.mult))
                link.mark(v.tensor_copy(rb[:, 0:GE - 1], rf[:, 1:GE]))
                link.mark(v.reduce_sum(wsum[:, :], n.erow_w[:, 0, :], AX_X))
                link.join()
                v.memset(same[:, :, :], 0.0).then_inc(ready, 1)
                for c in (n.c_src, n.c_i4, n.c_i16):
                    v.memset(c[:, TILES:TILES + AHEAD], 0)
                for k, c in enumerate(cols):
                    dve.wait_ge(turned, k + 1)
                    v.tensor_copy(c[:, 0:TILES].rearrange("p (g k) -> p k g", k=TPG), turn[:, k, :, :]).then_inc(taken, 1)
                dve.wait_ge(turned, 6)
                dve.wait_ge(ready, 1)
                link.mark(v.tensor_copy(n.base[:, :], ends_t[0:1, 2, :]))
                link.mark(v.tensor_scalar(n.tw[:, :], ends_t[:, 3, 0:1], 1.0 / E, None, ALU.mult))
                link(v.tensor_copy(fl[:, :, :], ends_t[:, 0:2, :]))
                link.mark(v.tensor_tensor(same[:, 0, 1:GR], fl[:, 0, 1:GR], fl[:, 1, 0:GR - 1], ALU.is_equal))
                link.mark(v.tensor_tensor(same[:, 1, :], fl[:, 0, :], fl[:, 1, :], ALU.is_equal))
                link.mark(v.memset(n.seg[:, :, :], 0.0))
                link.join()
                link.mark(v.tensor_copy(n.seg[:, 0, :], same[:, 0, :]))
                link.mark(v.tensor_tensor(n.seg[:, 1, :], same[:, 0, :], same[:, 1, :], ALU.mult))
                link.join()
                link(v.tensor_scalar(n.seg[:, :, :], n.seg[:, :, :], -1.0, BIG, ALU.add, ALU.mult))

            @block.sync
            def _(sp):
                sp.wait_ge(ready, 1)
                out = flag_table.rearrange("(g h) e -> h g e", h=H)
                for h in range(H):
                    sp.dma_start(out[h, :, 0:GE], rf[:, :]).then_inc(stored, 16)
                    sp.dma_start(out[h, :, GE:2 * GE], rb[:, :]).then_inc(stored, 16)
                sp.wait_ge(stored, 16 * 2 * H)

            @block.tensor
            def _(pe):
                pe.wait_ge(ready, 1)
                for k, r in enumerate(fields):
                    for j in range(TPG):
                        t = nc.tensor.transpose(turn[:, k, j, :], r[:, j * P:(j + 1) * P], n.ident[:, :])
                    t.then_inc(turned, 1)
                nc.tensor.transpose(ends_t[:, 0, :], ends[:, 0, :], n.ident[:, :])
                nc.tensor.transpose(ends_t[:, 1, :], ends[:, 1, :], n.ident[:, :])
                nc.tensor.transpose(ends_t[:, 2, :], ends[:, 2, :], n.ident[:, :])
                nc.tensor.matmul(ends_t[:, 3, 0:1], n.ones[:, :], wsum[:, :], start=True, stop=True).then_inc(turned, 1)


def norm_steps(nc, link, dve, src, stats, mv, root, var_ready, root_ready):
    v = nc.vector
    for t in range(NT):
        link.mark(v.bn_stats(stats[:, t, :], chunk(src, (t, 1))))
    link.join()
    for t in range(NT - 1):
        link.mark(v.bn_aggr(mv[:, t, :], stats[:, t, :]))
    link.join()
    v.bn_aggr(mv[:, NT - 1, :], stats[:, NT - 1, :]).then_inc(var_ready, 1)
    dve.wait_ge(root_ready, 1)
    link(v.reciprocal(root[:, 1, :], root[:, 0, :]))
    link(v.scalar_tensor_tensor(out=root[:, 2, :], in0=mv[:, :, 0], scalar=-1.0, in1=root[:, 1, :], op0=ALU.mult, op1=ALU.mult))


def norm_root(nc, act, n, mv, root, var_ready, root_ready):
    act.wait_ge(var_ready, 1)
    nc.scalar.activation(root[:, 0, :], mv[:, :, 1], ACT.Sqrt, bias=n.eps[:, 0:1]).then_inc(root_ready, 1)


def normalise(nc, src, out, c, root, func, done):
    for t in range(c[0], c[0] + c[1]):
        ins = nc.scalar.activation(chunk(out, (t, 1)), chunk(src, (t, 1)), func, bias=root[:, 2, t:t + 1], scale=root[:, 1, t:t + 1])
    ins.then_inc(done, 1)


def turn_and_store(nc, block, n, src, table, src_ready, turned, stored, ps):
    @block.tensor
    def _(pe):
        for q, c in enumerate(CH):
            pe.wait_ge(src_ready, q + 1)
            for j in range(c[1]):
                t = nc.tensor.transpose(ps[:, q, j, :], chunk(src, (c[0] + j, 1)), n.ident[:, :])
            t.then_inc(turned, 1)

    @block.sync
    def _(sp):
        for q, c in enumerate(CH):
            sp.wait_ge(src_ready, q + 1)
            sp.dma_start(rows(table, c), chunk3(src, c)).then_inc(stored, 16)
        sp.wait_ge(stored, 16 * NCH)


def norm_phase(nc, n, name, table):
    with Phase(nc, name) as ph:
        link_sem, var_ready, root_ready = ph.sem("link"), ph.sem("var"), ph.sem("root")
        h_ready, turned, stored, scales = ph.sem("h_ready"), ph.sem("turned"), ph.sem("stored"), ph.sem("scales")
        stats, mv, root = ph.sb("stats", [P, NT, 6]), ph.sb("mv", [P, NT, 2]), ph.sb("rootv", [P, 3, NT])
        ps = ph.ps("ps", [P, NCH, 4, P])
        with nc.Block() as block:
            @block.vector
            def _(dve):
                link = Link(dve, link_sem)
                norm_steps(nc, link, dve, n.x, stats, mv, root, var_ready, root_ready)
                dve.sem_inc(scales, 1)
                for q, c in enumerate(CH):
                    dve.wait_ge(turned, q + 1)
                    nc.vector.tensor_copy(chunk3(n.ht, c), ps[:, q, 0:c[1], :])

            @block.scalar
            def _(act):
                norm_root(nc, act, n, mv, root, var_ready, root_ready)
                act.wait_ge(scales, 1)
                for c in CH:
                    normalise(nc, n.x, n.hn, c, root, ACT.Relu, h_ready)

            turn_and_store(nc, block, n, n.hn, table, h_ready, turned, stored, ps)


def edge_pass(nc, n, name, table, idx, width, mode):
    regions = {"degree": 2, "spline": 2, "plain": 1}[mode]
    feats = min(width, D)
    with Phase(nc, name) as ph:
        idx_ready = [ph.sem(f"idx_ready{s}") for s in range(RING)]
        both = parts(n, RING, n.got, n.extra_got, n.got_counts)
        hot = [ph.sem(f"hot{s}") for s in range(RING)]
        used = [ph.sem(f"used{s}") for s in range(RING)]
        added = ph.sem("added")
        cleared, started = ph.sem("cleared"), ph.sem("started")
        idxs = ph.sb("idxs", [P, RING, TPG], I32)
        g = ph.sb("g", [P, RING, TPG, width])
        oh = ph.sb("oh", [P, RING, TPG, WIN])
        ps = ph.ps("ps", [P, RING, 4 * P])
        if mode == "spline":
            ohw = ph.sb("ohw", [P, RING, TPG, 2, WIN])
        def build_ops():
            return 3 if mode == "spline" else 1

        with nc.Block() as block:
            @block.gpsimd
            def _(pool):
                for part in both:
                    with part.only(pool):
                        with pool.Fori(part.first + 1, part.stop + 1) as turn:
                            for s in range(RING):
                                pool.wait_ge(started, 1)
                                pool.wait_ge(idx_ready[s], turn)
                                for j in range(TPG):
                                    pool.indirect_dma_start(g[:, s, j, :], None, table, bass.IndirectOffsetOnAxis(
                                        ap=idxs[:, s, j:j + 1], axis=0)).then_inc(part.got[s], 16)

            @block.tensor
            def _(pe):
                pe.sem_inc(started, 1)
                for s in range(RING):
                    pe.sem_inc(used[s], 1)
                for part in both:
                    with part.only(pe):
                        with pe.Fori(part.first, part.stop) as i:
                            for s in range(RING):
                                part.arrived(pe, s, i)
                                pe.wait_ge(hot[s], i * build_ops() + build_ops())
                                pe.wait_ge(added, i * RING + (s + 1))
                                for j in range(TPG):
                                    first, last = j == 0, j == TPG - 1
                                    if mode == "spline":
                                        mm = nc.tensor.matmul(ps[:, s, 0:2 * WIN], g[:, s, j, :], ohw[:, s, j, :, :].rearrange("p a w -> p (a w)"),
                                                              start=first, stop=last)
                                        continue
                                    left = [g[:, s, j, 0:feats]]
                                    if mode == "degree":
                                        left.append(n.ones[:, :])
                                    for r, lt in enumerate(left):
                                        mm = nc.tensor.matmul(ps[0:feats, s, r * WIN:(r + 1) * WIN], lt, oh[:, s, j, :],
                                                              start=first and r == 0, stop=last, skip_group_check=True)
                                mm.then_inc(used[s], 1)

            @block.vector
            def _(dve):
                v = nc.vector
                for s in range(RING):
                    v.tensor_copy(idxs[:, s, :], idx[:, s * TPG:(s + 1) * TPG]).then_inc(idx_ready[s], 1)
                v.memset(n.acc[:, 0:regions, :], 0.0).then_inc(cleared, 1)
                dve.wait_ge(cleared, 1)
                dve.sem_inc(added, RING)
                iota = n.iota[:, :].unsqueeze(1).to_broadcast([P, TPG, WIN])
                for part in both:
                    with part.only(dve):
                        with dve.Fori(part.first, part.stop) as i:
                            def build(s):
                                tiles = bass.ds(i * (RING * TPG) + s * TPG, TPG)
                                dstl = n.c_dstl[:, tiles].unsqueeze(2).to_broadcast([P, TPG, WIN])
                                dve.wait_ge(used[s], i + 1)
                                v.tensor_tensor(oh[:, s, :, :], iota, dstl, ALU.is_equal).then_inc(hot[s], 1)
                                if mode == "spline":
                                    u = n.c_u[:, tiles].unsqueeze(2).to_broadcast([P, TPG, WIN])
                                    dve.wait_ge(hot[s], i * 3 + 1)
                                    v.tensor_tensor(ohw[:, s, :, 1, :], oh[:, s, :, :], u, ALU.mult).then_inc(hot[s], 1)
                                    dve.wait_ge(hot[s], i * 3 + 2)
                                    v.tensor_tensor(ohw[:, s, :, 0, :], oh[:, s, :, :], ohw[:, s, :, 1, :], ALU.subtract).then_inc(hot[s], 1)

                            def add(s):
                                base = nc.vector.value_load(n.base[0:1, bass.ds(i * RING + s, 1)], min_val=0, max_val=NP - WIN)
                                dve.wait_ge(used[s], i + 2)
                                v.tensor_copy(idxs[:, s, :], idx[:, bass.ds(i * (RING * TPG) + (RING + s) * TPG, TPG)]).then_inc(idx_ready[s], 1)
                                dve.wait_ge(added, i * RING + (RING + s))
                                out = n.acc[0:feats, 0:regions, bass.ds(base, WIN)]
                                v.tensor_tensor(out, out, ps[0:feats, s, 0:regions * WIN].rearrange("p (r w) -> p r w", w=WIN),
                                                ALU.add).then_inc(added, 1)

                            for s in range(RING):
                                build(s)
                                if s:
                                    add(s - 1)
                            add(RING - 1)


def mean_layer(nc, n):
    with Phase(nc, "mean") as ph:
        link_sem, var_ready, root_ready = ph.sem("link"), ph.sem("var"), ph.sem("root")
        agg_ready, mixed, scales, scaled = ph.sem("agg_ready"), ph.sem("mixed"), ph.sem("scales"), ph.sem("scaled")
        stats, mv, root = ph.sb("stats", [P, NT, 6]), ph.sb("mv", [P, NT, 2]), ph.sb("rootv", [P, 3, NT])
        ps = ph.ps("ps", [P, NCH, 4, P])
        agg, y = n.acc[:, 0, :], n.acc[:, 1, :]
        with nc.Block() as block:
            @block.vector
            def _(dve):
                v = nc.vector
                link = Link(dve, link_sem)
                for c in CH:
                    link(v.tensor_scalar(chunk(n.rdeg, c), chunk(y, c), 1.0, None, ALU.max))
                    link(v.reciprocal(chunk(n.rdeg, c), chunk(n.rdeg, c)))
                    v.tensor_tensor(chunk(agg, c), chunk(agg, c), chunk(n.rdeg, c), ALU.mult).then_inc(agg_ready, 1)
                for q, c in enumerate(CH):
                    dve.wait_ge(mixed, q + 1)
                    b = n.rowb[:, 0, :].unsqueeze(1).to_broadcast([P, c[1], D])
                    link(v.tensor_tensor(chunk3(y, c), ps[:, q, 0:c[1], :], b, ALU.add))
                    link(v.tensor_tensor(chunk3(y, c), chunk3(y, c), chunk3(n.hn, c), ALU.add))
                norm_steps(nc, link, dve, y, stats, mv, root, var_ready, root_ready)
                dve.sem_inc(scales, 1)
                for q, c in enumerate(CH):
                    gamma = n.rowb[:, 1, :].unsqueeze(1).to_broadcast([P, c[1], D])
                    beta = n.rowb[:, 2, :].unsqueeze(1).to_broadcast([P, c[1], D])
                    dve.wait_ge(scaled, q + 1)
                    link(v.tensor_tensor(chunk3(y, c), chunk3(y, c), gamma, ALU.mult))
                    link(v.tensor_tensor(chunk3(y, c), chunk3(y, c), beta, ALU.add))
                    link(v.scalar_tensor_tensor(out=chunk3(n.x, c), in0=chunk3(y, c), scalar=0.0, in1=chunk3(n.x, c),
                                                op0=ALU.max, op1=ALU.add))

            @block.scalar
            def _(act):
                norm_root(nc, act, n, mv, root, var_ready, root_ready)
                act.wait_ge(scales, 1)
                for c in CH:
                    normalise(nc, y, y, c, root, ACT.Identity, scaled)

            @block.tensor
            def _(pe):
                for q, c in enumerate(CH):
                    pe.wait_ge(agg_ready, q + 1)
                    for j in range(c[1]):
                        t = (c[0] + j, 1)
                        nc.tensor.matmul(ps[:, q, j, :], chunk(n.ht, t), n.wagg_t[:, 0, :], start=True, stop=False)
                        mm = nc.tensor.matmul(ps[:, q, j, :], chunk(agg, t), n.wagg_t[:, 1, :], start=False, stop=True)
                    mm.then_inc(mixed, 1)


def spline_layer(nc, n, name, w, bias_row, table):
    with Phase(nc, name) as ph:
        link_sem, agg_ready, mixed = ph.sem("link"), ph.sem("agg_ready"), ph.sem("mixed")
        out_ready, turned, stored = ph.sem("out_ready"), ph.sem("turned"), ph.sem("stored")
        ps = ph.ps("ps", [P, NCH, 4, P])
        a0, a1 = n.acc[:, 0, :], n.acc[:, 1, :]
        with nc.Block() as block:
            @block.vector
            def _(dve):
                v = nc.vector
                link = Link(dve, link_sem)
                for c in CH:
                    v.tensor_tensor(chunk(a0, c), chunk(a0, c), chunk(n.rdeg, c), ALU.mult).then_inc(agg_ready, 1)
                    v.tensor_tensor(chunk(a1, c), chunk(a1, c), chunk(n.rdeg, c), ALU.mult).then_inc(agg_ready, 1)
                for q, c in enumerate(CH):
                    dve.wait_ge(mixed, q + 1)
                    b = n.rowb[:, bias_row, :].unsqueeze(1).to_broadcast([P, c[1], D])
                    ins = v.tensor_tensor(chunk3(n.hn, c), ps[:, q, 0:c[1], :], b, ALU.add)
                    if table is not None:
                        ins.then_inc(out_ready, 1)
                        continue
                    link(ins)
                    link(v.tensor_tensor(chunk3(n.x, c), chunk3(n.x, c), chunk3(n.hn, c), ALU.add))

            @block.tensor
            def _(pe):
                for q, c in enumerate(CH):
                    pe.wait_ge(agg_ready, 2 * q + 2)
                    for j in range(c[1]):
                        t = (c[0] + j, 1)
                        nc.tensor.matmul(ps[:, q, j, :], chunk(a0, t), w[:, 0, :], start=True, stop=False)
                        nc.tensor.matmul(ps[:, q, j, :], chunk(a1, t), w[:, 1, :], start=False, stop=False)
                        mm = nc.tensor.matmul(ps[:, q, j, :], chunk(n.ht, t), w[:, 2, :], start=False, stop=True)
                    mm.then_inc(mixed, 1)
                if table is not None:
                    for q, c in enumerate(CH):
                        pe.wait_ge(out_ready, q + 1)
                        for j in range(c[1]):
                            t = nc.tensor.transpose(ps[:, q, j, :], chunk(n.hn, (c[0] + j, 1)), n.ident[:, :])
                        t.then_inc(turned, 1)

            if table is not None:
                @block.scalar
                def _(act):
                    for q, c in enumerate(CH):
                        act.wait_ge(turned, q + 1)
                        nc.scalar.copy(chunk3(n.ht, c), ps[:, q, 0:c[1], :])

                @block.sync
                def _(sp):
                    for q, c in enumerate(CH):
                        sp.wait_ge(out_ready, q + 1)
                        sp.dma_start(rows(table, c), chunk3(n.hn, c)).then_inc(stored, 16)
                    sp.wait_ge(stored, 16 * NCH)


def message_phase(nc, n, table):
    with Phase(nc, "msg") as ph:
        made = [ph.sem(f"made{k}") for k in range(4)]
        kept = [ph.sem(f"kept{k}") for k in range(4)]
        stored = ph.sem("stored")
        a1 = ph.sb("a1", [P, R4 // 2, 4 * P])
        a2 = ph.sb("a2", [P, R4 // 2, 4 * P])
        a3 = ph.sb("a3", [P, R4, 4 * P])
        ps = ph.ps("ps", [P, 8, 4 * P])
        m = n.acc[:, 0:2, :].rearrange("p a (t o) -> p (a t o)", o=2 * D).rearrange("p (t r o) -> p t r o", r=R4, o=HID)
        with nc.Block() as block:
            @block.tensor
            def _(pe):
                for q, c in enumerate(CH):
                    w = c[1] * P
                    for a in range(R4 // 2):
                        if q:
                            pe.wait_ge(kept[2], R4 * (q - 1) + a + 1)
                        nc.tensor.matmul(ps[:, a, 0:w], n.wr1[:, 2 * a:2 * a + 2, :].rearrange("p r h -> p (r h)"), chunk(n.ht, c),
                                         start=True, stop=True).then_inc(made[0], 1)
                    for a in range(R4 // 2):
                        pe.wait_ge(kept[0], 2 * q + a + 1)
                        if q:
                            pe.wait_ge(kept[3], R4 * (q - 1) + a + 1)
                        nc.tensor.matmul(ps[:, R4 + a, 0:w], n.wr2[:, a, :], a1[:, a, 0:w], start=True, stop=True).then_inc(made[1], 1)
                    for r in range(R4):
                        pe.wait_ge(kept[1], 2 * q + r // 2 + 1)
                        if q:
                            pe.wait_ge(kept[2], R4 * (q - 1) + r + 1)
                        nc.tensor.matmul(ps[:, r, 0:w], n.wr3[:, r, :], a2[:, r // 2, 0:w], start=True, stop=True).then_inc(made[2], 1)
                    for r in range(R4):
                        pe.wait_ge(kept[2], R4 * q + r + 1)
                        if q:
                            pe.wait_ge(kept[3], R4 * (q - 1) + r + 1)
                        for j in range(c[1]):
                            mm = nc.tensor.matmul(ps[:, R4 + r, j * HID:(j + 1) * HID], a3[:, r, j * P:(j + 1) * P],
                                                  n.wn1[:, 1 + r, :], start=True, stop=True)
                        mm.then_inc(made[3], 1)

            @block.scalar
            def _(act):
                stages = ((a1, n.br1, 2, 0), (a2, n.br2, 2, R4), (a3, n.br3, 1, 0))
                later = (R4 // 2, R4, R4)
                for q, c in enumerate(CH):
                    w = c[1] * P
                    for k, (out, bias, at_once, bank) in enumerate(stages):
                        units = R4 // at_once
                        for u in range(units):
                            act.wait_ge(made[k], units * q + u + 1)
                            if q:
                                act.wait_ge(made[k + 1], later[k] * (q - 1) + (u + 1) * later[k] // units)
                            nc.scalar.activation(out[:, u, 0:w], ps[:, bank + u, 0:w], ACT.Relu,
                                                 bias=bias[:, u:u + 1]).then_inc(kept[k], 1)

            @block.vector
            def _(dve):
                for q, c in enumerate(CH):
                    for r in range(R4):
                        dve.wait_ge(made[3], R4 * q + r + 1)
                        nc.vector.tensor_copy(m[:, c[0]:c[0] + c[1], r, :],
                                              ps[:, R4 + r, 0:c[1] * HID].rearrange("p (t o) -> p t o", o=HID)).then_inc(kept[3], 1)

            @block.sync
            def _(sp):
                out = table.rearrange("(t p r) o -> p t (r o)", p=P, r=R4)
                for q, c in enumerate(CH):
                    sp.wait_ge(kept[3], R4 * (q + 1))
                    sp.dma_start(out[:, c[0]:c[0] + c[1], :], m[:, c[0]:c[0] + c[1], :, :].rearrange("p t r o -> p t (r o)")).then_inc(stored, 16)
                sp.wait_ge(stored, 16 * NCH)


def relation_layer(nc, n):
    with Phase(nc, "rel") as ph:
        made = [ph.sem(f"made{k}") for k in range(3)]
        summed, kept, link_sem, out_read = ph.sem("summed"), [ph.sem("kept0"), ph.sem("kept1")], ph.sem("link"), ph.sem("out_read")
        t0 = ph.sb("t0", [HID, 2, 4 * P])
        q1 = ph.sb("q1", [HID, 2, 4 * P])
        q2 = ph.sb("q2", [HID, 2, 4 * P])
        out = ph.sb("out", [P, 4, D])
        ps = ph.ps("ps", [P, 3, 2, 4 * P])
        with nc.Block() as block:
            @block.tensor
            def _(pe):
                def first(q):
                    if q >= 2:
                        pe.wait_ge(summed, q - 1)
                    nc.tensor.matmul(ps[0:HID, 0, q % 2, 0:CH[q][1] * P], n.wn1[:, 0, :], chunk(n.ht, CH[q]), start=True, stop=True).then_inc(made[0], 1)

                first(0)
                for q, c in enumerate(CH):
                    w = c[1] * P
                    if q + 1 < NCH:
                        first(q + 1)
                    pe.wait_ge(kept[0], q + 1)
                    if q >= 2:
                        pe.wait_ge(kept[1], q - 1)
                    nc.tensor.matmul(ps[0:HID, 1, q % 2, 0:w], n.wn2[:, :], q1[:, q % 2, 0:w], start=True, stop=True).then_inc(made[1], 1)
                    pe.wait_ge(kept[1], q + 1)
                    if q >= 2:
                        pe.wait_ge(out_read, q - 1)
                    for j in range(c[1]):
                        mm = nc.tensor.matmul(ps[:, 2, q % 2, j * D:(j + 1) * D], q2[:, q % 2, j * P:(j + 1) * P], n.wn3[:, :],
                                              start=True, stop=True)
                    mm.then_inc(made[2], 1)

            @block.scalar
            def _(act):
                for q, c in enumerate(CH):
                    w = c[1] * P
                    act.wait_ge(summed, q + 1)
                    if q >= 2:
                        act.wait_ge(made[1], q - 1)
                    nc.scalar.activation(q1[:, q % 2, 0:w], t0[:, q % 2, 0:w], ACT.Relu, bias=n.bn12[:, 0:1]).then_inc(kept[0], 1)
                    act.wait_ge(made[1], q + 1)
                    if q >= 2:
                        act.wait_ge(made[2], q - 1)
                    nc.scalar.activation(q2[:, q % 2, 0:w], ps[0:HID, 1, q % 2, 0:w], ACT.Relu, bias=n.bn12[:, 1:2]).then_inc(kept[1], 1)

            @block.vector
            def _(dve):
                v = nc.vector
                link = Link(dve, link_sem)

                def add_sums(q):
                    w = CH[q][1] * P
                    dve.wait_ge(made[0], q + 1)
                    if q >= 2:
                        dve.wait_ge(kept[0], q - 1)
                    v.tensor_tensor(t0[:, q % 2, 0:w], ps[0:HID, 0, q % 2, 0:w], chunk(n.acc[0:HID, 0, :], CH[q]), ALU.add).then_inc(summed, 1)

                add_sums(0)
                for q, c in enumerate(CH):
                    if q + 1 < NCH:
                        add_sums(q + 1)
                    dve.wait_ge(made[2], q + 1)
                    b = n.rowb[:, 5, :].unsqueeze(1).to_broadcast([P, c[1], D])
                    v.tensor_tensor(out[:, 0:c[1], :], ps[:, 2, q % 2, 0:c[1] * D].rearrange("p (t d) -> p t d", d=D), b, ALU.add).then_inc(out_read, 1)
                    dve.wait_ge(out_read, q + 1)
                    link(v.tensor_tensor(chunk3(n.x, c), chunk3(n.x, c), out[:, 0:c[1], :], ALU.add))


def attend_pass(nc, n, l, table, er_table, flag_table):
    KC, KA = 12, 2
    with Phase(nc, f"att{l}") as ph:
        both = parts(n, 2 * RING, n.att_got, n.extra_att_got, n.att_counts)
        idx_ready = [ph.sem(f"idx_ready{p}") for p in range(2)]
        used = [ph.sem(f"used{k}") for k in range(2 * RING)]
        hot = [ph.sem(f"hot{p}") for p in range(2)]
        er_in = [ph.sem(f"er_in{k}") for k in range(2 * RING)]
        flags_in = [ph.sem(f"flags_in{p}") for p in range(2)]
        half_hot, hot_turned, hot_t = ph.sem("half_hot"), ph.sem("hot_turned"), ph.sem("hot_t")
        er_done, x_ready, x_turned, cut = ph.sem("er_done"), ph.sem("x_ready"), ph.sem("x_turned"), ph.sem("cut")
        ends_ready, grown, back, spread = ph.sem("ends_ready"), ph.sem("grown"), ph.sem("back"), ph.sem("spread")
        parted = ph.sem("parted")
        gap, fac_ready, scaled, added = ph.sem("gap"), ph.sem("fac_ready"), ph.sem("scaled"), ph.sem("added")
        cleared, started, link_c, link_a = ph.sem("cleared"), ph.sem("started"), ph.sem("link_c"), ph.sem("link_a")

        idxs = ph.sb("idxs", [P, 2, RING * TPG], I32)
        g = ph.sb("g", [P, 2 * RING, TPG, ROW])
        oh = ph.sb("oh", [P, 2 * RING, TPG, WIN])
        ohb = ph.sb("ohb", [P, 2 * RING, TPG, WIN], BF16)
        oht = ph.sb("oht", [P, RING, TPG, P], BF16)
        erw = ph.sb("erw", [P, 2 * RING, H * PARTS], BF16)
        flags = ph.sb("flags", [RING * H, 2, 2, GE])
        er = ph.sb("er", [P, RING * TPG, H])
        x = ph.sb("x_v", [P, TPG, RING, H])
        fwd = ph.sb("fwd", [RING * H, GE])
        bwd = ph.sb("bwd", [RING * H, GE])
        ex = ph.sb("ex_v", [RING * H, GE])
        ends = ph.sb("ends_v", [RING * H, 2, RING])
        run = ph.sb("run", [P, RING + 1])
        cin = ph.sb("cin", [P, RING])
        top = ph.sb("top", [P, RING])
        diff = ph.sb("diff", [P, 2, 2, RING])
        fac = ph.sb("fac", [P, 2, 2, RING])
        exc = ph.sb("exc", [P, TPG, RING, H])
        exr = ph.sb("exr", [P, RING, TPG, H])
        exd = ph.sb("exd", [P, 2, RING, TPG, H, DH], BF16)
        zs = ph.sb("zs", [P, RING, TPG, D])
        ps = ph.ps("ps", [P, RING, 4 * P])
        ps_two = ph.ps("ps_two", [P, 2, 512])
        ps_x = ph.ps("ps_x", [P, GE])
        ps_w = ph.ps("ps_w", [P, 512])
        ps_t = [ps_two[:, k, 0:TPG * P // 2].bitcast(BF16).rearrange("p (t e) -> p t e", e=P) for k in range(2)]
        er_ps = ps_two[:, 1, 256:256 + RING * TPG * H * PARTS]
        ex_ps = ps_w[:, 0:TPG * RING * H].rearrange("p (k g h) -> p k g h", k=TPG, h=H)
        end_ps = ps_x[:, 0:2 * RING]

        def after(i, p):
            return (i, 1) if p == 0 else (i + 1, 0)

        def before(i, p):
            return (i, 0) if p else (i - 1, 1)

        def steps(eng, part, step, finish):
            step(part.first, 0, True, False)
            with eng.Fori(part.first, part.stop - 1) as i:
                step(i, 1, False, False)
                step(i + 1, 0, False, False)
            step(part.stop - 1, 1, False, True)
            finish(part.stop - 1, 1)

        with nc.Block() as block:
            @block.gpsimd
            def _(pool):
                for part in both:
                    with part.only(pool):
                        with pool.Fori(part.first + 1, part.stop + 1) as lap:
                            for p in range(2):
                                for s in range(RING):
                                    k = RING * p + s
                                    pool.wait_ge(started, 1)
                                    if s == 0:
                                        pool.wait_ge(idx_ready[p], lap)
                                    pool.wait_ge(used[k], lap)
                                    for j in range(TPG):
                                        pool.indirect_dma_start(g[:, k, j, :], None, table, bass.IndirectOffsetOnAxis(
                                            ap=idxs[:, p, s * TPG + j:s * TPG + j + 1], axis=0)).then_inc(part.got[k], 16)

            @block.sync
            def _(sp):
                for part in both:
                    with part.only(sp):
                        with sp.Fori(part.first, part.stop) as i:
                            for p in range(2):
                                sp.wait_ge(cut, i * 2 + (p + 1))
                                sp.dma_start(flags[:, p, :, :].rearrange("q a e -> q (a e)"),
                                             flag_table[bass.ds(i * (2 * RING * H) + p * RING * H, RING * H), :]).then_inc(flags_in[p], 16)
                                for s in range(RING):
                                    k = RING * p + s
                                    base = sp.value_load(n.base[0:1, bass.ds(i * (2 * RING) + k, 1)], min_val=0, max_val=NP - WIN)
                                    sp.wait_ge(er_done, i * 8 + (4 * p + s + 1))
                                    sp.dma_start(erw[:, k, :], er_table[bass.ds(base, WIN), :]).then_inc(er_in[k], 16)

            @block.tensor
            def _(pe):
                def multiply(i, p, s):
                    k = RING * p + s
                    pe.wait_ge(hot[p], i * RING + (s + 1))
                    part.arrived(pe, k, i)
                    pe.wait_ge(scaled, i * 8 + (4 * p + s + 1 + RING))
                    pe.wait_ge(parted, i * 2 + (p + 1))
                    pe.wait_ge(added, i * 8 + (4 * p + s + 1))
                    for j in range(TPG):
                        nc.tensor.matmul(ps[:, s, 0:WIN], g[:, k, j, 0:D], oh[:, k, j, :], start=j == 0, stop=j == TPG - 1, skip_group_check=True)
                        nc.tensor.matmul(ps[:, s, WIN:2 * WIN], zs[:, s, j, :], oh[:, k, j, :], start=False, stop=j == TPG - 1, skip_group_check=True)
                        mm = nc.tensor.matmul(ps[:, s, 2 * WIN:3 * WIN], exd[:, p, s, j, :, :].rearrange("p h d -> p (h d)"), ohb[:, k, j, :],
                                              start=False, stop=j == TPG - 1, skip_group_check=True)
                    mm.then_inc(used[k], 1)

                def turn_hot(i, p, s):
                    c = 4 * p + s
                    pe.wait_ge(half_hot, i * 8 + (c + 1))
                    pe.wait_ge(hot_t, i * 8 + (c + 1))
                    pe.wait_ge(x_ready, i * 2 + (p + 1))
                    for j in range(TPG):
                        t = nc.tensor.transpose(ps_t[s % 2][:, j, :], ohb[:, RING * p + s, j, :], n.identb[:, :])
                    t.then_inc(hot_turned, 1)

                def look_up(i, p):
                    pe.wait_ge(hot_t, i * 8 + (4 * p + 6))
                    for s in range(RING):
                        pe.wait_ge(er_in[RING * p + s], i * 16 + 16)
                        for j in range(TPG):
                            q = (s * TPG + j) * H * PARTS
                            mm = nc.tensor.matmul(er_ps[:, q:q + H * PARTS], oht[:, s, j, :], erw[:, RING * p + s, :], start=True, stop=True)
                        mm.then_inc(er_done, 1)

                def step(i, p, first, last):
                    pe.wait_ge(x_ready, i * 2 + (p + 2))
                    pe.wait_ge(cut, i * 2 + (p + 2))
                    for j in range(TPG):
                        t = nc.tensor.transpose(ps_x[0:RING * H, j * P:(j + 1) * P], x[:, j, :, :].rearrange("p s h -> p (s h)"), n.ident[:, :])
                    t.then_inc(x_turned, 1)
                    if not first:
                        multiply(*before(i, p), 2)
                    pe.wait_ge(grown, i * 2 + (p + 1))
                    pe.wait_ge(ends_ready, i * 4 + (2 * p + 2))
                    pe.wait_ge(spread, i * 2 + (p + 1))
                    pe.wait_ge(fac_ready, i * 2 + (p + 1))
                    nc.tensor.matmul(end_ps, n.selh[:, :], ends[:, :, :].rearrange("q a g -> q (a g)"), start=True, stop=True)
                    for j in range(TPG):
                        t = nc.tensor.transpose(ex_ps[:, j, :, :], ex[:, j * P:(j + 1) * P], n.ident[0:RING * H, 0:RING * H])
                    t.then_inc(back, 1)
                    if not first:
                        multiply(*before(i, p), 3)
                    multiply(i, p, 0)
                    if not last:
                        turn_hot(*after(i, p), 0)
                    multiply(i, p, 1)
                    if not last:
                        for s in range(1, RING):
                            turn_hot(*after(i, p), s)
                        look_up(*after(i, p))

                def finish(i, p):
                    multiply(i, p, 2)
                    multiply(i, p, 3)

                pe.sem_inc(started, 1)
                for k in range(2 * RING):
                    pe.sem_inc(used[k], 1)
                pe.sem_inc(er_done, 2 * RING)
                pe.sem_inc(x_turned, 1)
                pe.sem_inc(back, 1)
                for part in both:
                    with part.only(pe):
                        for s in range(RING):
                            turn_hot(part.first, 0, s)
                        look_up(part.first, 0)
                        steps(pe, part, step, finish)

            @block.scalar
            def _(act):
                def look_up(i, p):
                    def keep_turned(s):
                        c = 4 * p + s
                        act.wait_ge(hot_turned, i * 8 + (c + 1))
                        act.wait_ge(er_done, i * 8 + (c + 1 + RING))
                        nc.scalar.copy(oht[:, s, :, :], ps_t[s % 2][:, :, :]).then_inc(hot_t, 1)

                    for s in range(RING):
                        act.wait_ge(hot[p], i * RING + (s + 1))
                        nc.scalar.copy(ohb[:, RING * p + s, :, :], oh[:, RING * p + s, :, :]).then_inc(half_hot, 1)
                        if s:
                            keep_turned(s - 1)
                    keep_turned(RING - 1)

                def step(i, p, first, last):
                    act.wait_ge(cut, i * 2 + (p + 3))
                    nc.scalar.activation(ex[:, :], ex[:, :], ACT.Exp).then_inc(grown, 1)
                    act.wait_ge(back, i * 2 + (p + 2))
                    act.wait_ge(scaled, i * 8 + (4 * p + 4))
                    nc.scalar.copy(exc[:, :, :, :], ex_ps).then_inc(spread, 1)
                    act.wait_ge(gap, i * 4 + (2 * p + 2))
                    nc.scalar.activation(fac[:, p, :, :], diff[:, p, :, :], ACT.Exp).then_inc(fac_ready, 1)
                    if not last:
                        look_up(*after(i, p))

                act.sem_inc(hot_t, 2)
                act.sem_inc(spread, 1)
                act.sem_inc(fac_ready, 1)
                for part in both:
                    with part.only(act):
                        look_up(part.first, 0)
                        steps(act, part, step, lambda i, p: None)

            @block.vector
            def _(dve):
                v = nc.vector
                iota = n.iota[:, :].unsqueeze(1).to_broadcast([P, TPG, WIN])

                def build(i, p, s):
                    k = RING * p + s
                    dstl = n.c_dstl[:, bass.ds(i * (2 * RING * TPG) + k * TPG, TPG)].unsqueeze(2).to_broadcast([P, TPG, WIN])
                    dve.wait_ge(used[k], i + 1)
                    v.tensor_tensor(oh[:, k, :, :], iota, dstl, ALU.is_equal).then_inc(hot[p], 1)

                def add(i, p, s):
                    link = Link(dve, link_a, i * (8 * KA) + (4 * p + s) * KA)
                    k = RING * p + s
                    base = v.value_load(n.base[0:1, bass.ds(i * (2 * RING) + k, 1)], min_val=0, max_val=NP - WIN)
                    if s == 0:
                        dve.wait_ge(fac_ready, i * 2 + (p + 2))
                    dve.wait_ge(used[k], i + 2)
                    dve.wait_ge(added, i * 8 + (4 * p + s + RING))
                    new = ps[:, s, 0:3 * WIN].rearrange("p (r w) -> p r w", w=WIN)
                    old = n.acc[:, 1:3, bass.ds(base, 1)]
                    link.mark(v.tensor_scalar(new[:, 1:3, 0:1], new[:, 1:3, 0:1], fac[:, p, 1, s:s + 1], None, ALU.mult))
                    link.mark(v.tensor_scalar(old, old, fac[:, p, 0, s:s + 1], None, ALU.mult))
                    link.join()
                    link.check(KA)
                    out = n.acc[:, :, bass.ds(base, WIN)]
                    v.tensor_tensor(out, out, new, ALU.add).then_inc(added, 1)

                def scale(i, p, s):
                    w = exc[:, :, s, :].unsqueeze(3).to_broadcast([P, TPG, H, DH])
                    v.tensor_tensor(zs[:, s, :, :].rearrange("p t (h d) -> p t h d", d=DH),
                                    g[:, RING * p + s, :, D:2 * D].rearrange("p t (h d) -> p t h d", d=DH), w, ALU.mult).then_inc(scaled, 1)

                def step(i, p, first, last):
                    link = Link(dve, link_c, i * (2 * KC) + p * KC)
                    groups = bass.ds(i * (2 * RING) + p * RING, RING)
                    for s in range(RING):
                        part.arrived(dve, RING * p + s, i)
                    dve.wait_ge(er_done, i * 8 + (4 * p + 3 * RING))
                    dve.wait_ge(x_turned, i * 2 + (p + 1))
                    v.tensor_copy(idxs[:, p, :], n.c_i16[:, bass.ds(i * AHEAD + (2 + p) * RING * TPG, RING * TPG)]).then_inc(idx_ready[p], 1)
                    link(v.reduce_sum(er[:, :, :].rearrange("p t h -> p (t h)"), er_ps.rearrange("p (c k) -> p c k", k=PARTS), AX_X))
                    el = g[:, RING * p:RING * (p + 1), :, 2 * D:ROW]
                    link(v.tensor_tensor(x[:, :, :, :].rearrange("p t s h -> p s t h"), el, er[:, :, :].rearrange("p (s t) h -> p s t h", t=TPG), ALU.add))
                    xf = x[:, :, :, :].rearrange("p t s h -> p (t s h)")
                    v.scalar_tensor_tensor(out=xf, in0=xf, scalar=0.2, in1=xf, op0=ALU.mult, op1=ALU.max).then_inc(x_ready, 1)
                    if not first:
                        add(*before(i, p), 1)
                    dve.wait_ge(x_turned, i * 2 + (p + 2))
                    dve.wait_ge(flags_in[p], i * 16 + 16)
                    line = ps_x[0:RING * H, :]
                    link(v.tensor_tensor_scan(fwd[:, :], flags[:, p, 0, :], line, -BIG, ALU.add, ALU.max))
                    link(v.tensor_tensor_scan(bwd[:, ::-1], flags[:, p, 1, ::-1], fwd[:, ::-1], -BIG, ALU.add, ALU.max))
                    dve.wait_ge(back, i * 2 + (p + 1))
                    v.tensor_tensor(ex[:, :], line, bwd[:, :], ALU.subtract).then_inc(cut, 1)
                    v.tensor_scalar(ends[:, 0, :], n.gmask[:, :], bwd[:, 0:1], None, ALU.mult).then_inc(ends_ready, 1)
                    v.tensor_scalar(ends[:, 1, :], n.gmask[:, :], fwd[:, GE - 1:GE], None, ALU.mult).then_inc(ends_ready, 1)
                    if not first:
                        add(*before(i, p), 2)
                    dve.wait_ge(spread, i * 2 + (p + 2))
                    scale(i, p, 0)
                    w = exc[:, :, :, :].rearrange("p t s h -> p s t h")
                    split = exd[:, p, :, :, :, :]
                    link(v.tensor_copy(split[:, :, :, :, 0], w))
                    link(v.tensor_tensor(exr[:, :, :, :], w, split[:, :, :, :, 0], ALU.subtract))
                    link(v.tensor_copy(split[:, :, :, :, 1], exr[:, :, :, :]))
                    link(v.tensor_tensor(exr[:, :, :, :], exr[:, :, :, :], split[:, :, :, :, 1], ALU.subtract))
                    v.tensor_copy(split[:, :, :, :, 2], exr[:, :, :, :]).then_inc(parted, 1)
                    scale(i, p, 1)
                    dve.wait_ge(back, i * 2 + (p + 2))
                    link(v.tensor_tensor_scan(run[:, 1:RING + 1], n.seg[:, 1, groups], end_ps[:, RING:2 * RING], run[:, 0:1], ALU.add, ALU.max))
                    link(v.tensor_tensor(cin[:, :], run[:, 0:RING], n.seg[:, 0, groups], ALU.add))
                    link(v.tensor_tensor(top[:, :], cin[:, :], end_ps[:, 0:RING], ALU.max))
                    link.mark(v.tensor_copy(run[:, 0:1], run[:, RING:RING + 1]))
                    v.tensor_tensor(diff[:, p, 0, :], cin[:, :], top[:, :], ALU.subtract).then_inc(gap, 1)
                    v.tensor_tensor(diff[:, p, 1, :], end_ps[:, 0:RING], top[:, :], ALU.subtract).then_inc(gap, 1)
                    link.join()
                    dve.wait_ge(gap, i * 4 + (2 * p + 2))
                    link.check(KC)
                    dve.wait_ge(parted, i * 2 + (p + 1))
                    if not last:
                        build(*after(i, p), 0)
                        build(*after(i, p), 1)
                    scale(i, p, 2)
                    if not first:
                        add(*before(i, p), 3)
                    if not last:
                        build(*after(i, p), 2)
                        build(*after(i, p), 3)
                    scale(i, p, 3)
                    add(i, p, 0)

                def finish(i, p):
                    for s in range(1, RING):
                        add(i, p, s)

                for p in range(2):
                    v.tensor_copy(idxs[:, p, :], n.c_i16[:, p * RING * TPG:(p + 1) * RING * TPG]).then_inc(idx_ready[p], 1)
                v.memset(run[:, :], -BIG).then_inc(cleared, 1)
                v.memset(exd[:, :, :, :, :, :], 0.0).then_inc(cleared, 1)
                dve.wait_ge(cleared, 2)
                dve.sem_inc(x_ready, 1)
                dve.sem_inc(cut, 2)
                dve.sem_inc(scaled, RING)
                dve.sem_inc(added, RING)
                for part in both:
                    with part.only(dve):
                        for s in range(RING):
                            build(part.first, 0, s)
                        steps(dve, part, step, finish)


def fuse_phase(nc, n, l, w_rel, table, er_table, out):
    gating, last, fusing = l == 0, l == LAYERS - 1, l >= 0
    order = []
    if last:
        order = [("sums", 0), ("ratio", 0)]
        for q in range(NCH):
            order += [("sums", q + 1), ("ratio", q + 1)] * (q + 1 < NCH) + [("fused", q)] + [("out", q - 1)] * (q >= 1)
        order += [("out", NCH - 1)]
    else:
        ahead = [["sums", "ratio"], ["fused"], ["gate"]] if gating else [["sums"], ["ratio"], ["fused"]]
        if not fusing:
            ahead = []
        order += [(k, 0) for kinds in ahead for k in kinds]
        for q, c in enumerate(CH):
            for j in range(min(c[1], NTABLE - c[0])):
                order += [("tile", c[0] + j)]
                if q + 1 < NCH and j < len(ahead):
                    order += [(k, q + 1) for k in ahead[j]]
    depth = 2 if last else 1
    with Phase(nc, f"fuse{l + 1}") as ph:
        link_sem, gat_ready, rel_made, rel_ready = ph.sem("link"), ph.sem("gat"), ph.sem("rel_made"), ph.sem("rel")
        fused, hc_ready, gated, sig, h_ready = ph.sem("fused"), ph.sem("hc"), ph.sem("gated"), ph.sem("sig"), ph.sem("h_ready")
        turned, x_ready, stored, bias_ready = ph.sem("turned"), ph.sem("x_ready"), ph.sem("stored"), ph.sem("bias")
        den_made, den_read, cleared = ph.sem("den_made"), ph.sem("den_read"), ph.sem("cleared")
        chunk_done = h_ready if gating else hc_ready
        gbias = ph.sb("gbias", [P, 1])
        rel = ph.sb("rel", [P, depth, 4 * P])
        hc = ph.sb("hc_v", [P, 4 * P])
        gate = ph.sb("gate", [P, 4 * P])
        ps_den, ps_rel = ph.ps("ps_den", [P, depth, 4 * P]), ph.ps("ps_rel", [P, depth, 4 * P])
        ps_fused = ph.ps("ps_fused", [P, depth, 4 * P])
        a0, a1, a2 = (n.acc[:, k, :] for k in range(3))
        if last:
            ps_out = ph.ps("ps_out", [P, 2, 4 * P])
        else:
            loaded = ph.sem("loaded")
            made = ph.sem("made")
            took_a, took_b, took_z = ph.sem("took_a"), ph.sem("took_b"), ph.sem("took_z")
            stored_h = [ph.sem(f"stored_h{k}") for k in range(2)]
            stored_z = [ph.sem(f"stored_z{k}") for k in range(2)]
            scores, stored_e = ph.sem("scores"), ph.sem("stored_e")
            wrel = ph.sb("wrel", [P, R16, D])
            st = ph.sb("st", [P, 2, R16 * D])
            zst = ph.sb("zst", [P, 2, D + H])
            prod = ph.sb("prod", [P, 2, D])
            elr = ph.sb("elr", [P, NT, 2 * H])
            rest = ph.sb("rest", [P, NT, H])
            er_parts = ph.sb("er_parts", [P, NT, H, PARTS], BF16)
            ps = ph.ps("ps", [P, 2, 1024])
            psz = ph.ps("psz", [P, 512])

        def rows_of(t):
            full = min(P, N - t * P)
            return table[t * P * R16:(t * P + full) * R16].rearrange("(p r) c -> p r c", r=R16), full

        def count(k, upto):
            return (upto - k + 1) // 2

        with nc.Block() as block:
            @block.tensor
            def _(pe):
                if not last:
                    pe.wait_ge(loaded, 16)
                for kind, q in order:
                    if kind == "ratio":
                        continue
                    c = CH[q] if kind != "tile" else CH[q // 4]
                    w, k = c[1] * P, q % depth
                    if kind == "sums":
                        if q >= depth:
                            pe.wait_ge(rel_ready, q - depth + 1)
                            pe.wait_ge(den_read, q - depth + 1)
                            if gating:
                                pe.wait_ge(sig, q - depth + 1)
                        nc.tensor.matmul(ps_den[:, k, 0:w], n.same_head[:, :], chunk(a2, c), start=True, stop=True).then_inc(den_made, 1)
                        nc.tensor.matmul(ps_rel[:, k, 0:w], n.wloop[:, l, :], chunk(n.ht, c), start=True, stop=True).then_inc(rel_made, 1)
                    elif kind == "fused":
                        pe.wait_ge(rel_ready, q + 1)
                        pe.wait_ge(gat_ready, q + 1)
                        if q >= depth:
                            pe.wait_ge(hc_ready, q - depth + 1)
                        nc.tensor.matmul(ps_fused[:, k, 0:w], n.wfuse[:, 0, :], rel[:, k, 0:w], start=True, stop=False)
                        nc.tensor.matmul(ps_fused[:, k, 0:w], n.wfuse[:, 1, :], chunk(a1, c), start=False, stop=True).then_inc(fused, 1)
                    elif kind == "gate":
                        pe.wait_ge(hc_ready, q + 1)
                        pe.wait_ge(den_read, q + 1)
                        nc.tensor.matmul(ps_den[:, k, 0:w], n.wgate[:, :], hc[:, 0:w], start=True, stop=True).then_inc(gated, 1)
                    elif kind == "out":
                        pe.wait_ge(hc_ready, q + 1)
                        if q >= 2:
                            pe.wait_ge(x_ready, q - 1)
                        for j in range(c[1]):
                            t = nc.tensor.transpose(ps_out[:, q % 2, j * P:(j + 1) * P], chunk(n.ht, (c[0] + j, 1)), n.ident[:, :])
                        t.then_inc(turned, 1)
                    else:
                        t = q
                        if fusing:
                            pe.wait_ge(chunk_done, t // 4 + 1)
                        for half in range(2):
                            if t:
                                pe.wait_ge(took_b if half else took_a, t)
                            for b in range(2):
                                r0 = half * 8 + b * 4
                                mm = nc.tensor.matmul(ps[:, half, b * 512:(b + 1) * 512], chunk(n.ht, (t, 1)),
                                                      wrel[:, r0:r0 + 4, :].rearrange("p r o -> p (r o)"), start=True, stop=True)
                            mm.then_inc(made, 1)
                        if t:
                            pe.wait_ge(scores, t)
                        nc.tensor.matmul(psz[:, 0:D], chunk(n.ht, (t, 1)), n.wgat[:, l + 1, :], start=True, stop=True).then_inc(made, 1)

            @block.scalar
            def _(act):
                if gating:
                    act.wait_ge(bias_ready, 1)
                for kind, q in order:
                    c = CH[q] if kind != "tile" else CH[q // 4]
                    w, k = c[1] * P, q % depth
                    if kind == "fused":
                        act.wait_ge(fused, q + 1)
                        if gating:
                            if q:
                                act.wait_ge(h_ready, q)
                            nc.scalar.activation(hc[:, 0:w], ps_fused[:, k, 0:w], ACT.Identity, bias=n.cols[:, 6:7]).then_inc(hc_ready, 1)
                        else:
                            nc.scalar.activation(chunk(n.ht, c), ps_fused[:, k, 0:w], ACT.Relu, bias=n.cols[:, 6:7]).then_inc(hc_ready, 1)
                    elif kind == "gate":
                        act.wait_ge(gated, q + 1)
                        nc.scalar.activation(gate[:, 0:w], ps_den[:, k, 0:w], ACT.Sigmoid, bias=gbias[:, 0:1]).then_inc(sig, 1)
                    elif kind == "tile":
                        t, (tab, full) = q, rows_of(q)
                        act.wait_ge(made, 3 * t + 1)
                        if t >= 2:
                            act.wait_ge(stored_h[t % 2], 16 * (t // 2))
                        nc.scalar.copy(st[:, t % 2, 0:1024], ps[:, 0, :]).then_inc(took_a, 1)
                        act.wait_ge(took_z, 2 * t + 2)
                        act.dma_start(tab[:, :, D:ROW], zst[0:full, t % 2, :].unsqueeze(1).to_broadcast([full, R16, ROW - D])).then_inc(stored_z[t % 2], 16)
                if not last:
                    for k in range(2):
                        act.wait_ge(stored_z[k], 16 * count(k, NTABLE))

            @block.vector
            def _(dve):
                v = nc.vector
                link = Link(dve, link_sem)
                if gating:
                    link(v.tensor_tensor(gbias[:, :], n.cols[:, 8:9], n.tw[:, :], ALU.mult))
                    v.tensor_tensor(gbias[:, :], gbias[:, :], n.cols[:, 7:8], ALU.add).then_inc(bias_ready, 1)
                if not last:
                    link(v.memset(elr[:, NTABLE:NT, :], 0.0))
                for kind, q in order:
                    c = CH[q] if kind != "tile" else CH[q // 4]
                    w, k = c[1] * P, q % depth
                    if kind == "sums":
                        dve.wait_ge(den_made, q + 1)
                        v.tensor_scalar(chunk(a2, c), ps_den[:, k, 0:w], 1e-30, None, ALU.max).then_inc(den_read, 1)
                        dve.wait_ge(den_read, q + 1)
                        link(v.reciprocal(chunk(a2, c), chunk(a2, c)))
                    elif kind == "ratio":
                        link(v.tensor_tensor(chunk(a1, c), chunk(a1, c), chunk(a2, c), ALU.mult))
                        v.tensor_scalar(chunk(a1, c), chunk(a1, c), n.cols[:, 3 + l:4 + l], None, ALU.add).then_inc(gat_ready, 1)
                        dve.wait_ge(rel_made, q + 1)
                        if q >= depth:
                            dve.wait_ge(fused, q - depth + 1)
                        v.scalar_tensor_tensor(out=rel[:, k, 0:w], in0=ps_rel[:, k, 0:w], scalar=n.cols[:, l:l + 1],
                                               in1=chunk(a0, c), op0=ALU.add, op1=ALU.add).then_inc(rel_ready, 1)
                    elif kind == "gate":
                        dve.wait_ge(sig, q + 1)
                        link(v.tensor_tensor(gate[:, 0:w], gate[:, 0:w], hc[:, 0:w], ALU.mult))
                        v.tensor_scalar(chunk(n.ht, c), gate[:, 0:w], 0.0, None, ALU.max).then_inc(h_ready, 1)
                    elif kind == "out":
                        dve.wait_ge(turned, q + 1)
                        v.tensor_tensor(chunk3(n.x, c), chunk3(n.x, c), ps_out[:, q % 2, 0:w].rearrange("p (t d) -> p t d", d=D),
                                        ALU.add).then_inc(x_ready, 1)
                    elif kind == "tile":
                        t = q
                        dve.wait_ge(made, 3 * t + 2)
                        if t >= 2:
                            dve.wait_ge(stored_h[t % 2], 16 * (t // 2))
                        v.tensor_copy(st[:, t % 2, 1024:2048], ps[:, 1, :]).then_inc(took_b, 1)
                        dve.wait_ge(made, 3 * t + 3)
                        if t >= 2:
                            dve.wait_ge(stored_z[t % 2], 16 * (t // 2))
                        v.tensor_copy(zst[:, t % 2, 0:D], psz[:, 0:D]).then_inc(took_z, 1)
                        link(v.tensor_tensor(prod[:, :, :], psz[:, 0:D].unsqueeze(1).to_broadcast([P, 2, D]), n.attn[:, l + 1, :, :], ALU.mult))
                        v.reduce_sum(elr[:, t, :], prod[:, :, :].rearrange("p s (h d) -> p (s h) d", d=DH), AX_X).then_inc(scores, 1)
                        dve.wait_ge(scores, t + 1)
                        v.tensor_copy(zst[:, t % 2, D:D + H], elr[:, t, 0:H]).then_inc(took_z, 1)
                if not last:
                    link(v.tensor_copy(er_parts[:, :, :, 0], elr[:, :, H:2 * H]))
                    link(v.tensor_tensor(rest[:, :, :], elr[:, :, H:2 * H], er_parts[:, :, :, 0], ALU.subtract))
                    link(v.tensor_copy(er_parts[:, :, :, 1], rest[:, :, :]))
                    link(v.tensor_tensor(rest[:, :, :], rest[:, :, :], er_parts[:, :, :, 1], ALU.subtract))
                    v.tensor_copy(er_parts[:, :, :, 2], rest[:, :, :]).then_inc(scores, 1)

            @block.gpsimd
            def _(pool):
                if not last:
                    for q, c in enumerate(CH):
                        if fusing:
                            pool.wait_ge(fused, q + 1)
                        nc.gpsimd.memset(n.acc[:, :, c[0] * P:(c[0] + c[1]) * P], 0.0).then_inc(cleared, 1)
                    pool.wait_ge(cleared, NCH)

            @block.sync
            def _(sp):
                if last:
                    n_dma = 0
                    for q, c in enumerate(CH):
                        sp.wait_ge(x_ready, q + 1)
                        full = min(c[1], max(0, N // P - c[0]))
                        if full:
                            sp.dma_start(rows(out, (c[0], full)), chunk3(n.x, (c[0], full))).then_inc(stored, 16)
                            n_dma += 1
                        if c[0] <= N // P < c[0] + c[1]:
                            sp.dma_start(out[N // P * P:N, :], chunk(n.x, (N // P, 1))[0:N % P, :]).then_inc(stored, 16)
                            n_dma += 1
                    sp.wait_ge(stored, 16 * n_dma)
                    return
                sp.dma_start(wrel[:, :, :], w_rel[l + 1].rearrange("r c o -> c r o")).then_inc(loaded, 16)
                for t in range(NTABLE):
                    tab, full = rows_of(t)
                    sp.wait_ge(took_a, t + 1)
                    sp.wait_ge(took_b, t + 1)
                    sp.dma_start(tab[:, :, 0:D], st[0:full, t % 2, :].rearrange("p (r o) -> p r o", o=D)).then_inc(stored_h[t % 2], 16)
                sp.wait_ge(scores, NTABLE + 1)
                sp.dma_start(er_table.rearrange("(t p) c -> p t c", p=P), er_parts[:, :, :, :].rearrange("p t h k -> p t (h k)")).then_inc(stored_e, 16)
                sp.wait_ge(stored_e, 16)
                for k in range(2):
                    sp.wait_ge(stored_h[k], 16 * count(k, NTABLE))


def bass_gnn_kernel(nc, a, out):
    n = Net()
    h_table = nc.dram_tensor("h_table", (NP, D), F32).ap()
    m_table = nc.dram_tensor("m_table", (NP * R4, HID), F32).ap()
    g_table = nc.dram_tensor("g_table", (N * R16, ROW), F32).ap()
    er_table = nc.dram_tensor("er_table", (NP, H * PARTS), BF16).ap()
    dealt_table = nc.dram_tensor("dealt_table", (GR * GE + P, FIELDS), I32).ap()
    flag_table = nc.dram_tensor("flag_table", (GR * H, 2 * GE), F32).ap()
    n.got = [nc.alloc_semaphore(f"got{s}", num=FIRST_GATHER_SEM + s) for s in range(RING)]
    n.att_got = [nc.alloc_semaphore(f"att_got{k}", num=FIRST_GATHER_SEM + RING + k) for k in range(2 * RING)]
    n.extra_got = [nc.alloc_semaphore(f"extra_got{s}", num=FIRST_GATHER_SEM + 3 * RING + s) for s in range(RING)]
    n.extra_att_got = [nc.alloc_semaphore(f"extra_att_got{k}", num=FIRST_GATHER_SEM + 4 * RING + k) for k in range(2 * RING)]
    n.dealt = nc.alloc_semaphore("dealt", num=FIRST_GATHER_SEM + 6 * RING)
    n.got_counts, n.att_counts = [0, 0], [0, 0]
    with ExitStack() as whole, ExitStack() as early:
        def sb(name, shape, dt=F32, ctx=whole):
            return ctx.enter_context(nc.sbuf_tensor(name, shape, dt))

        n.wide = sb("wide", [1, 1], I32)
        n.ident, n.iota, n.ones = sb("ident", [P, P]), sb("iota", [P, P]), sb("ones", [P, P])
        n.identb, n.selh, n.gmask = sb("identb", [P, P], BF16), sb("selh", [RING * H, P]), sb("gmask", [RING * H, RING])
        n.same_head = sb("same_head", [P, P])
        n.x, n.ht = sb("x", [P, NP]), sb("ht", [P, NP])
        n.acc = sb("acc", [P, 3, NP])
        n.hn = n.acc[:, 2, :]
        n.c_i16, n.c_dstl = sb("c_i16", [P, TILES + AHEAD], I32), sb("c_dstl", [P, TILES])
        n.seg, n.base, n.tw = sb("seg", [P, 2, GR]), sb("base", [1, GR], I32), sb("tw", [P, 1])
        n.wloop, n.wgat, n.wfuse = sb("wloop", [P, LAYERS, D]), sb("wgat", [P, LAYERS, D]), sb("wfuse", [P, 2, D])
        n.wgate, n.cols, n.attn = sb("wgate", [P, D]), sb("cols", [P, 9]), sb("attn", [P, LAYERS, 2, D])

        def sb0(name, shape, dt=F32):
            return sb(name, shape, dt, early)

        n.rdeg, n.rowb, n.eps = sb0("rdeg", [P, NP]), sb0("rowb", [P, 6, D]), sb0("eps", [P, 1])
        n.c_src, n.c_i4, n.c_u = sb0("c_src", [P, TILES + AHEAD], I32), sb0("c_i4", [P, TILES + AHEAD], I32), sb0("c_u", [P, TILES])
        n.wagg_t, n.w1, n.w2 = sb0("wagg_t", [P, 2, D]), sb0("w1", [P, 3, D]), sb0("w2", [P, 3, D])
        n.wr1, n.wr2, n.wr3 = sb0("wr1", [P, R4, HID]), sb0("wr2", [P, R4 // 2, P]), sb0("wr3", [P, R4, D])
        n.wn1, n.wn2, n.wn3 = sb0("wn1", [P, 1 + R4, HID]), sb0("wn2", [HID, HID]), sb0("wn3", [HID, D])
        n.br1, n.br2, n.br3, n.bn12 = sb0("br1", [P, R4 // 2]), sb0("br2", [P, R4 // 2]), sb0("br3", [P, R4]), sb0("bn12", [HID, 2])
        with ExitStack() as rows_ctx:
            n.erow_i = rows_ctx.enter_context(nc.sbuf_tensor("erow_i", [P, 4, GE], I32))
            n.erow_w = rows_ctx.enter_context(nc.sbuf_tensor("erow_w", [P, 2, GE], F32))
            load_phase(nc, n, a)
            span_phase(nc, n)
            deal_phase(nc, n, dealt_table)
            edge_phase(nc, n, flag_table)
        norm_phase(nc, n, "norm0", h_table)
        edge_pass(nc, n, "pass0", h_table, n.c_src, D, "degree")
        mean_layer(nc, n)
        norm_phase(nc, n, "norm1", h_table)
        edge_pass(nc, n, "pass1", h_table, n.c_src, D, "spline")
        spline_layer(nc, n, "conv1", n.w1, 3, h_table)
        edge_pass(nc, n, "pass2", h_table, n.c_src, D, "spline")
        spline_layer(nc, n, "conv2", n.w2, 4, None)
        norm_phase(nc, n, "norm2", h_table)
        message_phase(nc, n, m_table)
        edge_pass(nc, n, "pass3", m_table, n.c_i4, HID, "plain")
        relation_layer(nc, n)
        norm_phase(nc, n, "norm3", h_table)
        early.close()
        fuse_phase(nc, n, -1, a["L3_gnn_W_rel"], g_table, er_table, out)
        for l in range(LAYERS):
            attend_pass(nc, n, l, g_table, er_table, flag_table)
            fuse_phase(nc, n, l, a["L3_gnn_W_rel"], g_table, er_table, out)


_INS = ['x', 'src', 'dst', 'edge_type_16', 'edge_type_4', 'edge_weight', 'edge_weight1',
        'L0_gnn_W_agg', 'L0_gnn_b_agg', 'L0_gnn_gamma', 'L0_gnn_beta',
        'L1_gnn_W1', 'L1_gnn_root1', 'L1_gnn_b1', 'L1_gnn_W2', 'L1_gnn_root2', 'L1_gnn_b2',
        'L2_gnn_Wr1', 'L2_gnn_br1', 'L2_gnn_Wr2', 'L2_gnn_br2', 'L2_gnn_Wr3', 'L2_gnn_br3',
        'L2_gnn_Wn1', 'L2_gnn_bn1', 'L2_gnn_Wn2', 'L2_gnn_bn2', 'L2_gnn_Wn3', 'L2_gnn_bn3',
        'L3_gnn_W_rel', 'L3_gnn_b_rel', 'L3_gnn_W_loop', 'L3_gnn_W_gat', 'L3_gnn_attn_l', 'L3_gnn_attn_r',
        'L3_gnn_b_gat', 'L3_gnn_W_fuse', 'L3_gnn_b_fuse', 'L3_gnn_W_gate', 'L3_gnn_b_gate']


def kernel(**inputs):
    import numpy as _np
    import concourse.bacc as _bacc
    from concourse import mybir as _mybir
    from concourse.bass_utils import run_bass_kernel_spmd as _run

    nc = _bacc.Bacc("TRN2", target_bir_lowering=False, num_devices=1)
    arrays, args = {}, {}
    for name in _INS:
        v = _np.ascontiguousarray(inputs[name])
        arrays[f"in_{name}_dram"] = v
        args[name] = nc.dram_tensor(f"in_{name}_dram", v.shape, _mybir.dt.from_np(v.dtype), kind="ExternalInput").ap()
    out = nc.dram_tensor("out_0_dram", (N, D), F32, kind="ExternalOutput").ap()
    bass_gnn_kernel(nc, args, out)
    r = _run(nc, [arrays], core_ids=[0])
    return r.results[0]["out_0_dram"]
```
